# Optimizing a Trainium2 kernel written in Bass

```python
import numpy as np
import jax
import jax.numpy as jnp

def _softmax(x, axis=-1):
    return jax.nn.softmax(x, axis=axis)

def _gelu(x):
    return jax.nn.gelu(x, approximate=True)

def _silu(x):
    return jax.nn.silu(x)

def _sigmoid(x):
    return jax.nn.sigmoid(x)

def _layernorm(x, axis=-1, eps=1e-05):
    m = jnp.mean(x, axis=axis, keepdims=True)
    v = jnp.var(x, axis=axis, keepdims=True)
    return (x - m) / jnp.sqrt(v + eps)

def _scatter_add(tgt, idx, src, axis=0):
    return tgt.at[idx].add(src)

def _segment_sum(src, seg, n):
    return jax.ops.segment_sum(src, seg, n)
kernel_name = 'mk_flamingo_gated_d2_seqx_r8_d94a90'

def setup_inputs(seed: int=0):
    np.random.seed(seed)
    _w = jnp.asarray

    def _rec_inputs():
        import jax
        import jax.numpy as jnp
        _rk = jax.random.key(seed)
        x = -0.0002928 + 1 * jax.random.normal(jax.random.fold_in(_rk, 1), (4, 512, 128), jnp.float32)
        _lenS = 512 - jax.random.randint(jax.random.fold_in(_rk, 7), (4,), 0, max(1, 512 // 4) + 1, jnp.int32)
        _lenS2 = 77 - jax.random.randint(jax.random.fold_in(_rk, 8), (4,), 0, max(1, 77 // 4) + 1, jnp.int32)
        _ctx_1024P = jax.random.normal(jax.random.fold_in(_rk, 11), (4, 16, 128), jnp.float32)
        _ctx_1024c = jax.random.dirichlet(jax.random.fold_in(_rk, 511), 0.3 * jnp.ones((16,), jnp.float32), (4, 77))
        _ctx_1024t = jnp.einsum('bsk,bkd->bsd', _ctx_1024c, _ctx_1024P)
        _ctx_1024t = _ctx_1024t * jax.lax.rsqrt(jnp.mean(jnp.square(_ctx_1024t)) + 1e-12) * 0.953939
        ctx_1024 = 4.13588e-05 + 0.999923 * (_ctx_1024t + 0.3 * jax.random.normal(jax.random.fold_in(_rk, 611), (4, 77, 128), jnp.float32))
        fside_BxSxS2_0 = -1.47943e-05 + 1.00017 * jax.random.normal(jax.random.fold_in(_rk, 13), (4, 512, 77), jnp.float32)
        _validS = jnp.arange(512)[None, :] < _lenS[:, None]
        _validS2 = jnp.arange(77)[None, :] < _lenS2[:, None]
        _causal = jnp.tril(jnp.ones((512, 512), dtype=bool))
        mask_BxS2_bf0 = jnp.logical_not(jnp.ones((4, 77), dtype=bool))
        _g = jax.random.normal(jax.random.fold_in(_rk, 9001), (2, 2), jnp.float32)
        _g = jnp.sign(_g) * jnp.maximum(jnp.abs(_g), 1.0) + (_g == 0) * 1.0
        g_xattn = _g[0]
        g_ffn = _g[1]
        return (x, ctx_1024, fside_BxSxS2_0, mask_BxS2_bf0, g_xattn, g_ffn)
    x, ctx_1024, fside_BxSxS2_0, mask_BxS2_bf0, g_xattn, g_ffn = _rec_inputs()

    def _L0_xattn_setup():
        import jax, jax.numpy as jnp
        import numpy as np
        D = 128
        H = 16
        HD = D // H
        DFF = 4 * D
        EPS = 1e-05

        def _layernorm(x, g, b):
            mu = jnp.mean(x, axis=-1, keepdims=True)
            var = jnp.var(x, axis=-1, keepdims=True)
            return (x - mu) * jax.lax.rsqrt(var + EPS) * g + b
        key = jax.random.key(seed)
        ks = jax.random.split(key, 16)
        B, SQ, SK = (4, 128, 256)
        s = 1.0 / np.sqrt(D)
        inp = {'query': jax.random.normal(ks[0], (B, SQ, D), jnp.float32), 'key_value': jax.random.normal(ks[1], (B, SK, D), jnp.float32), 'key_padding_mask': jnp.zeros((B, SK), jnp.bool_), 'Wq': jax.random.normal(ks[2], (D, D), jnp.float32) * s, 'bq': jnp.zeros((D,), jnp.float32), 'Wk': jax.random.normal(ks[3], (D, D), jnp.float32) * s, 'bk': jnp.zeros((D,), jnp.float32), 'Wv': jax.random.normal(ks[4], (D, D), jnp.float32) * s, 'bv': jnp.zeros((D,), jnp.float32), 'Wo': jax.random.normal(ks[5], (D, D), jnp.float32) * s, 'bo': jnp.zeros((D,), jnp.float32), 'ln1_g': jnp.ones((D,), jnp.float32), 'ln1_b': jnp.zeros((D,), jnp.float32), 'W1': jax.random.normal(ks[6], (D, DFF), jnp.float32) * s, 'b1': jnp.zeros((DFF,), jnp.float32), 'W2': jax.random.normal(ks[7], (DFF, D), jnp.float32) * (1.0 / np.sqrt(DFF)), 'b2': jnp.zeros((D,), jnp.float32), 'ln2_g': jnp.ones((D,), jnp.float32), 'ln2_b': jnp.zeros((D,), jnp.float32)}
        return inp
    _L0_xattn_all = _L0_xattn_setup()
    _L0_xattn_in = {k: v for k, v in _L0_xattn_all.items() if k in ('Wq', 'bq', 'Wk', 'bk', 'Wv', 'bv', 'Wo', 'bo', 'ln1_g', 'ln1_b', 'W1', 'b1', 'W2', 'b2', 'ln2_g', 'ln2_b')}
    del _L0_xattn_all

    def _L0_ffn_setup():
        import jax, jax.numpy as jnp
        import numpy as np
        DIM = 128
        DEPTH = 2
        HEADS = 8
        DIM_HEAD = 64
        WINDOW = 64
        INNER = HEADS * DIM_HEAD
        HID = int(DIM * 4 * 2 / 3)
        B, N = (2, 1024)
        QK_SCALE = 8.0

        def shift_token(t):
            t1, t2 = jnp.split(t, 2, axis=-1)
            t2 = jnp.pad(t2, ((0, 0), (1, 0), (0, 0)))[:, :-1]
            return jnp.concatenate([t1, t2], axis=-1)

        def l2norm(t):
            return t / jnp.clip(jnp.linalg.norm(t, axis=-1, keepdims=True), 1e-12)

        def rotate_half(x):
            x1, x2 = jnp.split(x, 2, axis=-1)
            return jnp.concatenate([-x2, x1], axis=-1)

        def rotary_xpos(q, k):
            n = q.shape[-2]
            half_idx = jnp.arange(0, DIM_HEAD, 2, dtype=jnp.float32)
            inv_freq = 1.0 / 10000.0 ** (half_idx / DIM_HEAD)
            t = jnp.arange(n, dtype=jnp.float32)
            freqs = t[:, None] * inv_freq[None, :]
            freqs = jnp.concatenate([freqs, freqs], axis=-1)
            base = (half_idx + 0.4 * DIM_HEAD) / (1.4 * DIM_HEAD)
            power = (t - n // 2) / float(WINDOW // 2)
            scale = base[None, :] ** power[:, None]
            scale = jnp.concatenate([scale, scale], axis=-1)
            cos, sin = (jnp.cos(freqs), jnp.sin(freqs))
            q = q * cos * scale + rotate_half(q) * sin * scale
            k = k * cos / scale + rotate_half(k) * sin / scale
            return (q, k)

        def local_attention(q, k, v):
            b, h, n, d = q.shape
            w = n // WINDOW
            bq = q.reshape(b, h, w, WINDOW, d) * QK_SCALE
            bk = k.reshape(b, h, w, WINDOW, d)
            bv = v.reshape(b, h, w, WINDOW, d)

            def look_around(t):
                p = jnp.pad(t, ((0, 0), (0, 0), (1, 0), (0, 0), (0, 0)))
                return jnp.concatenate([p[:, :, :w], p[:, :, 1:]], axis=3)
            bk, bv = (look_around(bk), look_around(bv))
            bt = jnp.arange(n).reshape(w, WINDOW)
            btp = jnp.pad(bt, ((1, 0), (0, 0)), constant_values=-1)
            btk = jnp.concatenate([btp[:w], btp[1:]], axis=1)
            sim = jnp.einsum('bhwid,bhwjd->bhwij', bq, bk)
            i = bt[:, :, None]
            j = btk[:, None, :]
            mask = (i < j) | (i > j + WINDOW) | (j == -1)
            sim = jnp.where(mask, -jnp.finfo(sim.dtype).max, sim)
            attn = jax.nn.softmax(sim, axis=-1)
            out = jnp.einsum('bhwij,bhwjd->bhwid', attn, bv)
            return out.reshape(b, h, n, d)

        def _layer(x, wqkv, qs, ksc, wo, lg, lb, w1, b1, w2, b2):
            b, n, _ = x.shape
            h = shift_token(x)
            qkv = h @ wqkv
            q, k, v = jnp.split(qkv, 3, axis=-1)
            to_heads = lambda t: t.reshape(b, n, HEADS, DIM_HEAD).transpose(0, 2, 1, 3)
            q, k, v = (to_heads(q), to_heads(k), to_heads(v))
            q = l2norm(q) * qs
            k = l2norm(k) * ksc
            q, k = rotary_xpos(q, k)
            o = local_attention(q, k, v)
            o = o.transpose(0, 2, 1, 3).reshape(b, n, INNER)
            x = x + o @ wo
            h = shift_token(x)
            mu = h.mean(-1, keepdims=True)
            var = h.var(-1, keepdims=True)
            h = (h - mu) / jnp.sqrt(var + 1e-05) * lg + lb
            h = h @ w1 + b1
            a, g = jnp.split(h, 2, axis=-1)
            h = a * jax.nn.gelu(g, approximate=False)
            x = x + h @ w2 + b2
            return x
        key = jax.random.key(seed)
        ks = jax.random.split(key, 6)
        return {'x': jax.random.normal(ks[0], (B, N, DIM), jnp.float32), 'wqkv': jax.random.normal(ks[1], (DEPTH, DIM, 3 * INNER), jnp.float32) * 0.02, 'q_scale': jnp.ones((DEPTH, DIM_HEAD), jnp.float32), 'k_scale': jnp.ones((DEPTH, DIM_HEAD), jnp.float32), 'wo': jax.random.normal(ks[2], (DEPTH, INNER, DIM), jnp.float32) * 0.02, 'ln_g': jnp.ones((DEPTH, DIM), jnp.float32), 'ln_b': jnp.zeros((DEPTH, DIM), jnp.float32), 'w1': jax.random.normal(ks[3], (DEPTH, DIM, 2 * HID), jnp.float32) * 0.02, 'b1': jnp.zeros((DEPTH, 2 * HID), jnp.float32), 'w2': jax.random.normal(ks[4], (DEPTH, HID, DIM), jnp.float32) * 0.02, 'b2': jnp.zeros((DEPTH, DIM), jnp.float32)}
    _L0_ffn_all = _L0_ffn_setup()
    _L0_ffn_in = {k: v for k, v in _L0_ffn_all.items() if k in ('wqkv', 'q_scale', 'k_scale', 'wo', 'ln_g', 'ln_b', 'w1', 'b1', 'w2', 'b2')}
    del _L0_ffn_all

    def _L1_xattn_setup():
        import jax, jax.numpy as jnp
        import numpy as np
        B, N, DIM, H = (4, 256, 128, 8)
        HD = DIM // H
        SCALE = HD ** (-0.5)
        key = jax.random.key(seed)
        ks = jax.random.split(key, 9)
        inp = {'q': jax.random.normal(ks[0], (B, N, DIM), dtype=jnp.float32), 'k': jax.random.normal(ks[1], (B, N, DIM), dtype=jnp.float32), 'v': jax.random.normal(ks[2], (B, N, DIM), dtype=jnp.float32), 'trans_mat': jax.random.normal(ks[3], (B, N, N), dtype=jnp.float32), 'Wq': jax.random.normal(ks[4], (DIM, DIM), dtype=jnp.float32) * DIM ** (-0.5), 'Wk': jax.random.normal(ks[5], (DIM, DIM), dtype=jnp.float32) * DIM ** (-0.5), 'Wv': jax.random.normal(ks[6], (DIM, DIM), dtype=jnp.float32) * DIM ** (-0.5), 'Wp': jax.random.normal(ks[7], (DIM, DIM), dtype=jnp.float32) * DIM ** (-0.5), 'bp': jax.random.normal(ks[8], (DIM,), dtype=jnp.float32) * 0.01}
        return inp
    _L1_xattn_all = _L1_xattn_setup()
    _L1_xattn_in = {k: v for k, v in _L1_xattn_all.items() if k in ('Wq', 'Wk', 'Wv', 'Wp', 'bp')}
    del _L1_xattn_all

    def _L1_ffn_setup():
        import jax, jax.numpy as jnp
        import numpy as np
        FEATURES = 128
        D_IN = 128

        def fp8_gemm_optimized(x, input_scale, kernel, kernel_scale):
            s_in = input_scale[0]
            s_k = kernel_scale[0]
            x_q = (x.astype(jnp.float32) / s_in).astype(jnp.float8_e4m3fn)
            k_q = (kernel.astype(jnp.float32) / s_k).astype(jnp.float8_e4m3fn)
            y = jnp.dot(x_q.astype(jnp.float32), k_q.astype(jnp.float32), preferred_element_type=jnp.float32)
            return y * (s_in * s_k)
        key = jax.random.key(seed)
        kx, kk, kb = jax.random.split(key, 3)
        x = jax.random.normal(kx, (4, 1024, D_IN), dtype=jnp.float32)
        limit = np.sqrt(6.0 / (D_IN + FEATURES)).astype(np.float32)
        kernel = jax.random.uniform(kk, (D_IN, FEATURES), dtype=jnp.float32, minval=-limit, maxval=limit).astype(jnp.bfloat16)
        input_scale = jnp.ones((1,), dtype=jnp.float32)
        kernel_scale = jnp.ones((1,), dtype=jnp.float32)
        bias = jnp.zeros((FEATURES,), dtype=jnp.bfloat16)
        return {'x': x, 'kernel': kernel, 'input_scale': input_scale, 'kernel_scale': kernel_scale, 'bias': bias}
    _L1_ffn_all = _L1_ffn_setup()
    _L1_ffn_in = {k: v for k, v in _L1_ffn_all.items() if k in ('kernel', 'input_scale', 'kernel_scale', 'bias')}
    del _L1_ffn_all
    return {'x': x, 'ctx_1024': ctx_1024, 'fside_BxSxS2_0': fside_BxSxS2_0, 'mask_BxS2_bf0': mask_BxS2_bf0, 'g_xattn': g_xattn, 'g_ffn': g_ffn, 'L0_xattn_Wq': _L0_xattn_in['Wq'], 'L0_xattn_bq': _L0_xattn_in['bq'], 'L0_xattn_Wk': _L0_xattn_in['Wk'], 'L0_xattn_bk': _L0_xattn_in['bk'], 'L0_xattn_Wv': _L0_xattn_in['Wv'], 'L0_xattn_bv': _L0_xattn_in['bv'], 'L0_xattn_Wo': _L0_xattn_in['Wo'], 'L0_xattn_bo': _L0_xattn_in['bo'], 'L0_xattn_ln1_g': _L0_xattn_in['ln1_g'], 'L0_xattn_ln1_b': _L0_xattn_in['ln1_b'], 'L0_xattn_W1': _L0_xattn_in['W1'], 'L0_xattn_b1': _L0_xattn_in['b1'], 'L0_xattn_W2': _L0_xattn_in['W2'], 'L0_xattn_b2': _L0_xattn_in['b2'], 'L0_xattn_ln2_g': _L0_xattn_in['ln2_g'], 'L0_xattn_ln2_b': _L0_xattn_in['ln2_b'], 'L0_ffn_wqkv': _L0_ffn_in['wqkv'], 'L0_ffn_q_scale': _L0_ffn_in['q_scale'], 'L0_ffn_k_scale': _L0_ffn_in['k_scale'], 'L0_ffn_wo': _L0_ffn_in['wo'], 'L0_ffn_ln_g': _L0_ffn_in['ln_g'], 'L0_ffn_ln_b': _L0_ffn_in['ln_b'], 'L0_ffn_w1': _L0_ffn_in['w1'], 'L0_ffn_b1': _L0_ffn_in['b1'], 'L0_ffn_w2': _L0_ffn_in['w2'], 'L0_ffn_b2': _L0_ffn_in['b2'], 'L1_xattn_Wq': _L1_xattn_in['Wq'], 'L1_xattn_Wk': _L1_xattn_in['Wk'], 'L1_xattn_Wv': _L1_xattn_in['Wv'], 'L1_xattn_Wp': _L1_xattn_in['Wp'], 'L1_xattn_bp': _L1_xattn_in['bp'], 'L1_ffn_kernel': _L1_ffn_in['kernel'], 'L1_ffn_input_scale': _L1_ffn_in['input_scale'], 'L1_ffn_kernel_scale': _L1_ffn_in['kernel_scale'], 'L1_ffn_bias': _L1_ffn_in['bias']}

def reference(x, ctx_1024, fside_BxSxS2_0, mask_BxS2_bf0, g_xattn, g_ffn, L0_xattn_Wq, L0_xattn_bq, L0_xattn_Wk, L0_xattn_bk, L0_xattn_Wv, L0_xattn_bv, L0_xattn_Wo, L0_xattn_bo, L0_xattn_ln1_g, L0_xattn_ln1_b, L0_xattn_W1, L0_xattn_b1, L0_xattn_W2, L0_xattn_b2, L0_xattn_ln2_g, L0_xattn_ln2_b, L0_ffn_wqkv, L0_ffn_q_scale, L0_ffn_k_scale, L0_ffn_wo, L0_ffn_ln_g, L0_ffn_ln_b, L0_ffn_w1, L0_ffn_b1, L0_ffn_w2, L0_ffn_b2, L1_xattn_Wq, L1_xattn_Wk, L1_xattn_Wv, L1_xattn_Wp, L1_xattn_bp, L1_ffn_kernel, L1_ffn_input_scale, L1_ffn_kernel_scale, L1_ffn_bias):
    import jax
    import jax.numpy as jnp

    def _L0_xattn_ref(query, key_value, key_padding_mask, Wq, bq, Wk, bk, Wv, bv, Wo, bo, ln1_g, ln1_b, W1, b1, W2, b2, ln2_g, ln2_b):
        import jax, jax.numpy as jnp
        import numpy as np
        D = 128
        H = 16
        HD = D // H
        DFF = 4 * D
        EPS = 1e-05

        def _layernorm(x, g, b):
            mu = jnp.mean(x, axis=-1, keepdims=True)
            var = jnp.var(x, axis=-1, keepdims=True)
            return (x - mu) * jax.lax.rsqrt(var + EPS) * g + b
        B, SQ, _ = query.shape
        SK = key_value.shape[1]
        scale = HD ** (-0.5)
        q = (query @ Wq + bq).reshape(B, SQ, H, HD).transpose(0, 2, 1, 3)
        k = (key_value @ Wk + bk).reshape(B, SK, H, HD).transpose(0, 2, 1, 3)
        v = (key_value @ Wv + bv).reshape(B, SK, H, HD).transpose(0, 2, 1, 3)
        scores = jnp.einsum('bhqd,bhkd->bhqk', q, k) * scale
        scores = jnp.where(key_padding_mask[:, None, None, :], -jnp.inf, scores)
        attn = jax.nn.softmax(scores, axis=-1)
        attn_out = jnp.einsum('bhqk,bhkd->bhqd', attn, v)
        attn_out = attn_out.transpose(0, 2, 1, 3).reshape(B, SQ, D)
        attn_out = attn_out @ Wo + bo
        x = _layernorm(query + attn_out, ln1_g, ln1_b)
        ffn = jax.nn.gelu(x @ W1 + b1, approximate=False) @ W2 + b2
        return _layernorm(x + ffn, ln2_g, ln2_b)

    def _L0_ffn_ref(x, wqkv, q_scale, k_scale, wo, ln_g, ln_b, w1, b1, w2, b2):
        import jax, jax.numpy as jnp
        import numpy as np
        DIM = 128
        DEPTH = 2
        HEADS = 8
        DIM_HEAD = 64
        WINDOW = 64
        INNER = HEADS * DIM_HEAD
        HID = int(DIM * 4 * 2 / 3)
        B, N = (2, 1024)
        QK_SCALE = 8.0

        def shift_token(t):
            t1, t2 = jnp.split(t, 2, axis=-1)
            t2 = jnp.pad(t2, ((0, 0), (1, 0), (0, 0)))[:, :-1]
            return jnp.concatenate([t1, t2], axis=-1)

        def l2norm(t):
            return t / jnp.clip(jnp.linalg.norm(t, axis=-1, keepdims=True), 1e-12)

        def rotate_half(x):
            x1, x2 = jnp.split(x, 2, axis=-1)
            return jnp.concatenate([-x2, x1], axis=-1)

        def rotary_xpos(q, k):
            n = q.shape[-2]
            half_idx = jnp.arange(0, DIM_HEAD, 2, dtype=jnp.float32)
            inv_freq = 1.0 / 10000.0 ** (half_idx / DIM_HEAD)
            t = jnp.arange(n, dtype=jnp.float32)
            freqs = t[:, None] * inv_freq[None, :]
            freqs = jnp.concatenate([freqs, freqs], axis=-1)
            base = (half_idx + 0.4 * DIM_HEAD) / (1.4 * DIM_HEAD)
            power = (t - n // 2) / float(WINDOW // 2)
            scale = base[None, :] ** power[:, None]
            scale = jnp.concatenate([scale, scale], axis=-1)
            cos, sin = (jnp.cos(freqs), jnp.sin(freqs))
            q = q * cos * scale + rotate_half(q) * sin * scale
            k = k * cos / scale + rotate_half(k) * sin / scale
            return (q, k)

        def local_attention(q, k, v):
            b, h, n, d = q.shape
            w = n // WINDOW
            bq = q.reshape(b, h, w, WINDOW, d) * QK_SCALE
            bk = k.reshape(b, h, w, WINDOW, d)
            bv = v.reshape(b, h, w, WINDOW, d)

            def look_around(t):
                p = jnp.pad(t, ((0, 0), (0, 0), (1, 0), (0, 0), (0, 0)))
                return jnp.concatenate([p[:, :, :w], p[:, :, 1:]], axis=3)
            bk, bv = (look_around(bk), look_around(bv))
            bt = jnp.arange(n).reshape(w, WINDOW)
            btp = jnp.pad(bt, ((1, 0), (0, 0)), constant_values=-1)
            btk = jnp.concatenate([btp[:w], btp[1:]], axis=1)
            sim = jnp.einsum('bhwid,bhwjd->bhwij', bq, bk)
            i = bt[:, :, None]
            j = btk[:, None, :]
            mask = (i < j) | (i > j + WINDOW) | (j == -1)
            sim = jnp.where(mask, -jnp.finfo(sim.dtype).max, sim)
            attn = jax.nn.softmax(sim, axis=-1)
            out = jnp.einsum('bhwij,bhwjd->bhwid', attn, bv)
            return out.reshape(b, h, n, d)

        def _layer(x, wqkv, qs, ksc, wo, lg, lb, w1, b1, w2, b2):
            b, n, _ = x.shape
            h = shift_token(x)
            qkv = h @ wqkv
            q, k, v = jnp.split(qkv, 3, axis=-1)
            to_heads = lambda t: t.reshape(b, n, HEADS, DIM_HEAD).transpose(0, 2, 1, 3)
            q, k, v = (to_heads(q), to_heads(k), to_heads(v))
            q = l2norm(q) * qs
            k = l2norm(k) * ksc
            q, k = rotary_xpos(q, k)
            o = local_attention(q, k, v)
            o = o.transpose(0, 2, 1, 3).reshape(b, n, INNER)
            x = x + o @ wo
            h = shift_token(x)
            mu = h.mean(-1, keepdims=True)
            var = h.var(-1, keepdims=True)
            h = (h - mu) / jnp.sqrt(var + 1e-05) * lg + lb
            h = h @ w1 + b1
            a, g = jnp.split(h, 2, axis=-1)
            h = a * jax.nn.gelu(g, approximate=False)
            x = x + h @ w2 + b2
            return x
        for l in range(DEPTH):
            x = _layer(x, wqkv[l], q_scale[l], k_scale[l], wo[l], ln_g[l], ln_b[l], w1[l], b1[l], w2[l], b2[l])
        return x

    def _L1_xattn_ref(q, k, v, trans_mat, Wq, Wk, Wv, Wp, bp):
        import jax, jax.numpy as jnp
        import numpy as np
        B, N, DIM, H = (4, 256, 128, 8)
        HD = DIM // H
        SCALE = HD ** (-0.5)
        Bq, Nq, C = q.shape
        qh = (q @ Wq.T).reshape(Bq, Nq, H, HD).transpose(0, 2, 1, 3)
        kh = (k @ Wk.T).reshape(Bq, -1, H, HD).transpose(0, 2, 1, 3)
        vh = (v @ Wv.T).reshape(Bq, -1, H, HD).transpose(0, 2, 1, 3)
        scores = jnp.einsum('bhqd,bhkd->bhqk', qh, kh) * SCALE
        gated = scores * trans_mat[:, None, :, :]
        sm = jax.nn.softmax(gated, axis=-1)
        attn = jnp.where(gated != 0, sm, jnp.zeros((), dtype=sm.dtype))
        x = jnp.einsum('bhqk,bhkd->bhqd', attn, vh)
        x = x.transpose(0, 2, 1, 3).reshape(Bq, Nq, C)
        return x @ Wp.T + bp

    def _L1_ffn_ref(x, kernel, input_scale, kernel_scale, bias):
        import jax, jax.numpy as jnp
        import numpy as np
        FEATURES = 128
        D_IN = 128

        def fp8_gemm_optimized(x, input_scale, kernel, kernel_scale):
            s_in = input_scale[0]
            s_k = kernel_scale[0]
            x_q = (x.astype(jnp.float32) / s_in).astype(jnp.float8_e4m3fn)
            k_q = (kernel.astype(jnp.float32) / s_k).astype(jnp.float8_e4m3fn)
            y = jnp.dot(x_q.astype(jnp.float32), k_q.astype(jnp.float32), preferred_element_type=jnp.float32)
            return y * (s_in * s_k)
        dtype = jnp.bfloat16
        x = x.astype(dtype)
        orig_shape = x.shape
        x2 = x.reshape(-1, x.shape[-1])
        y = fp8_gemm_optimized(x2, input_scale, kernel, kernel_scale)
        y = y.astype(dtype) + bias
        return y.reshape(orig_shape[:-1] + (FEATURES,))
    x = x + jnp.tanh(g_xattn[0]) * _L0_xattn_ref(_layernorm(x, axis=-1), ctx_1024, mask_BxS2_bf0, L0_xattn_Wq, L0_xattn_bq, L0_xattn_Wk, L0_xattn_bk, L0_xattn_Wv, L0_xattn_bv, L0_xattn_Wo, L0_xattn_bo, L0_xattn_ln1_g, L0_xattn_ln1_b, L0_xattn_W1, L0_xattn_b1, L0_xattn_W2, L0_xattn_b2, L0_xattn_ln2_g, L0_xattn_ln2_b)
    x = x + jnp.tanh(g_ffn[0]) * _L0_ffn_ref(_layernorm(x, axis=-1), L0_ffn_wqkv, L0_ffn_q_scale, L0_ffn_k_scale, L0_ffn_wo, L0_ffn_ln_g, L0_ffn_ln_b, L0_ffn_w1, L0_ffn_b1, L0_ffn_w2, L0_ffn_b2)
    x = x + jnp.tanh(g_xattn[1]) * _L1_xattn_ref(_layernorm(x, axis=-1), ctx_1024, ctx_1024, fside_BxSxS2_0, L1_xattn_Wq, L1_xattn_Wk, L1_xattn_Wv, L1_xattn_Wp, L1_xattn_bp)
    x = x + jnp.tanh(g_ffn[1]) * _L1_ffn_ref(_layernorm(x, axis=-1), L1_ffn_kernel, L1_ffn_input_scale, L1_ffn_kernel_scale, L1_ffn_bias)
    return x

_drawn_inputs = setup_inputs


def setup_inputs(seed=0):
    import zlib

    import numpy as np

    out = dict(_drawn_inputs(seed))
    spreads = {'g_ffn': (-1.0, 0.2),
     'L0_xattn_bq': (0.0, 0.436),
     'L0_xattn_bk': (0.0, 0.8),
     'L0_xattn_bv': (0.0, 0.1),
     'L0_xattn_bo': (0.0, 0.1),
     'L0_xattn_ln1_g': (1.0, 0.2),
     'L0_xattn_ln1_b': (0.0, 0.1),
     'L0_xattn_b1': (0.0, 0.279),
     'L0_xattn_b2': (0.0, 0.1),
     'L0_xattn_ln2_g': (1.0, 0.2),
     'L0_xattn_ln2_b': (0.0, 0.1),
     'L0_ffn_q_scale': (1.0, 0.6),
     'L0_ffn_k_scale': (1.0, 0.6),
     'L0_ffn_ln_g': (1.0, 0.6),
     'L0_ffn_ln_b': (0.0, 0.8),
     'L0_ffn_b1': (0.0, 0.561),
     'L0_ffn_b2': (0.0, 0.1),
     'L1_ffn_bias': (0.0, 0.1)}
    factors = {'L0_ffn_w1': 2.959, 'L0_ffn_w2': 2.95, 'L1_xattn_bp': 4.045}
    for name, (base, spread) in spreads.items():
        noise = np.random.default_rng([zlib.crc32(name.encode()), seed]).standard_normal(out[name].shape)
        drawn = base * np.exp(spread * noise) if base else spread * noise
        out[name] = jnp.asarray(drawn.astype(out[name].dtype))
    for name, factor in factors.items():
        out[name] = (out[name] * factor).astype(out[name].dtype)
    return out
```

```python
from contextlib import ExitStack, contextmanager

import numpy as np

import concourse.bass as bass
from concourse import mybir

F32 = mybir.dt.float32
BF16 = mybir.dt.bfloat16
U8 = mybir.dt.uint8
U32 = mybir.dt.uint32
ALU = mybir.AluOpType
ACT = mybir.ActivationFunctionType
AX = mybir.AxisListType

P = 128
D = 128
B, S, SK = 4, 512, 77
U = 2
TPB = S // P
NT = U * TPB
EPS = 1e-5
NEG = -1e30

HA, DA = 16, 8
HC, DC = 8, 16
CA = -(-HA * SK // P)
CC = -(-HC * SK // P)
WIN = 3
GA = [(0, 6), (6, 12), (12, 16)]
GC = [(0, 4), (4, 8)]
FF = 512

DEPTH, HB, DH, W = 2, 8, 64, 64
INNER = HB * DH
HID = 341
HCH = [(0, 128), (128, 128), (256, 85)]
PAD = W


def chunk_rows(c, heads):
    return min(P, heads * SK - P * c)


def chunk_head(c, heads):
    return min(P * c // SK, heads - WIN)


class Chain:

    def __init__(self, eng, sem):
        self.eng, self.sem, self.n = eng, sem, 0

    def do(self, ins):
        ins.then_inc(self.sem, 1)
        self.n += 1
        return self.n

    def sync(self):
        self.eng.wait_ge(self.sem, self.n)


def quantise(dve, v, q, dst, n, ready=None):
    t, m, r = (b[:, 0:n] for b in q)
    v.do(dve.tensor_scalar(m.bitcast(U32), t.bitcast(U32), 0x7F800000, None, ALU.bitwise_and))
    v.sync()
    v.do(dve.tensor_scalar(m, m, 2.0 ** -6, 1.5 * 2.0 ** 20, ALU.max, ALU.mult))
    v.sync()
    v.do(dve.tensor_tensor(r, t, m, ALU.add))
    v.sync()
    v.do(dve.tensor_tensor(r, r, m, ALU.subtract))
    v.sync()
    v.do(dve.tensor_scalar(t.bitcast(U32), r.bitcast(U32), 0x7FFFFFFF, None, ALU.bitwise_and))
    v.sync()
    v.do(dve.tensor_scalar(t, t, 448.0, 448.0, ALU.max, ALU.subtract))
    v.sync()
    v.do(dve.tensor_scalar(t, t, 3e38, 0.0, ALU.mult, ALU.mult))
    v.sync()
    ins = dve.tensor_tensor(dst, r, t, ALU.add)
    v.do(ins) if ready is None else ins.then_inc(ready, 1)


def flamingo_kernel(nc, a, out):
    with ExitStack() as ctx:
        def sb(name, shape, dt=F32, scope=ctx):
            return scope.enter_context(nc.sbuf_tensor(name, shape, dt))

        bank = [ctx.enter_context(nc.psum_tensor(f"bank{i}", [P, 512], F32)) for i in range(8)]

        ident = sb("ident", [P, P])
        ident_bf = sb("ident_bf", [P, P], BF16)
        headmask_a = sb("headmask_a", [P, HA])
        headmask_c = sb("headmask_c", [P, HC])
        vmask_a = sb("vmask_a", [P, CA, WIN])
        vmask_c = sb("vmask_c", [P, CC, WIN])
        rot = sb("rot", [P, 4, S])
        band = sb("band", [P, 2, P], BF16)
        headones = sb("headones", [P, 2])
        shift = sb("shift", [P, 2, P])
        minus_half = sb("minus_half", [P, 64])
        ones_bf = sb("ones_bf", [1, P], BF16)

        wa = {k: sb(f"wa_{k}", [P, D]) for k in ("q", "k", "v", "o")}
        wc = {k: sb(f"wc_{k}", [P, D]) for k in ("q", "k", "v", "p")}
        wa1 = sb("wa1", [P, FF])
        wa2 = sb("wa2", [P, FF // P, D])
        cols_a = sb("cols_a", [P, 5])
        b1_a = sb("b1_a", [P, FF // P])
        rows = sb("rows", [P, 7, D])
        gates = sb("gates", [P, 4])
        tg = sb("tg", [P, 4])
        gated_rows = sb("gated_rows", [P, 3, D])
        kern = sb("kern", [P, D], BF16)
        kern_q = sb("kern_q", [P, D], BF16)
        fscale = sb("fscale", [P, 2])
        rscale = sb("rscale", [P, 2])
        sprod = sb("sprod", [P, 1])
        fbias = sb("fbias", [P, D], BF16)

        x = sb("x", [P, NT, D])
        xn = sb("xn", [P, NT, D])
        y = sb("y", [P, NT, D])
        tmat = sb("tmat", [P, NT, SK])
        ctxt = sb("ctxt", [P, U, SK])
        mflat = sb("mflat", [P, U, CA], U8)
        mrow = sb("mrow", [1, U, SK], U8)
        keep = sb("keep", [P, U, CA])
        mrow_bf = sb("mrow_bf", [1, U, SK], BF16)
        kt_a = sb("kt_a", [P, U, SK])
        kt_c = sb("kt_c", [P, U, SK])
        kbd_c = sb("kbd_c", [P, U, HC, SK])
        kmask = sb("kmask", [P, U, CA, WIN])
        vbd_a = sb("vbd_a", [P, U, CA, WIN, DA + 1])
        vbd_c = sb("vbd_c", [P, U, CC, WIN, DC])

        st = sb("st", [P, NT, 2, 6])
        mv = sb("mv", [P, NT, 2])
        rstd = sb("rstd", [P, NT])

        xt = sb("xt", [P, U, S])
        qt = sb("qt", [P, U, S])
        mx = sb("mx", [P, 2, HA])
        den = sb("den", [P, 2, HA])
        rd = sb("rd", [P, 2, HA])
        att = sb("att", [P, 2, D])
        attt = sb("attt", [P, 2, D])
        base = sb("base", [P, NT, D])

        wqkv = sb("wqkv", [P, 3 * INNER])
        wswap = sb("wswap", [P, 2 * HB, 2, DH // 2])
        headsel = sb("headsel", [HB, 4, P])
        wo_b = sb("wo_b", [P, INNER // P, D])
        w1_b = sb("w1_b", [P, 2 * HID])
        w2_b = sb("w2_b", [P, 3, D])
        cols_b = sb("cols_b", [P, 12])
        row_b = sb("row_b", [P, D])
        ht = sb("ht", [P, U, PAD + S + 1])
        rnt = sb("rnt", [HB, U, S])
        n2 = sb("n2", [P, U, TPB * 16])
        rn = sb("rn", [P, U, TPB, 2, HB])
        nb = sb("nb", [P, 2, HB])
        qsc = sb("qsc", [P, NT, HB])


        @contextmanager
        def stage(*names):
            with ExitStack() as c:
                sems = [c.enter_context(nc.semaphore(n)) for n in names]
                with nc.Block() as block:
                    yield block, sems
                nums = [s.num for s in sems]
                nc.all_engine_barrier(sems_to_clear=range(min(nums), max(nums) + 1))

        def dve_stats(dve, v, u, src, var_ready, src2=None):
            for j in range(TPB):
                n = TPB * u + j
                if src2 is None:
                    v.do(dve.bn_stats(st[:, n, 0, :], src[:, n, :]))
                else:
                    v.do(dve.bn_stats(st[:, n, 0, :], src[:, n, 0:64]))
                    v.do(dve.bn_stats(st[:, n, 1, :], src2(j)))
            v.sync()
            for j in range(TPB):
                n = TPB * u + j
                v.do(dve.bn_aggr(mv[:, n, :], st[:, n, 0, :] if src2 is None
                                 else st[:, n, :, :].rearrange("p a b -> p (a b)")))
            v.sync()
            dve.tensor_scalar(rstd[:, TPB * u:TPB * u + TPB], mv[:, TPB * u:TPB * u + TPB, 1], EPS, None,
                              ALU.add).then_inc(var_ready, 1)

        def pool_rstd(pool, u, var_ready, rstd_ready):
            pool.wait_ge(var_ready, u + 1)
            r = rstd[:, TPB * u:TPB * u + TPB]
            pool.tensor_tensor(r, r, minus_half[:, 0:TPB], ALU.pow).then_inc(rstd_ready, 1)

        def dve_normalize(dve, u, src, dst, rstd_ready, done=None, halves=None):
            dve.wait_ge(rstd_ready, u + 1)
            for j in range(TPB):
                n = TPB * u + j
                m, r = mv[:, n, 0:1], rstd[:, n:n + 1]
                if halves is None:
                    ins = dve.tensor_scalar(dst[:, n, :], src[:, n, :], m, r, ALU.subtract, ALU.mult)
                else:
                    dve.tensor_scalar(dst[:, n, 0:64], src[:, n, 0:64], m, r, ALU.subtract, ALU.mult)
                    ins = dve.tensor_scalar(dst[:, n, 64:128], halves(j), m, r, ALU.subtract, ALU.mult)
                if done is not None:
                    ins.then_inc(done, 1)

        with ExitStack() as once:
            band_f = sb("band_f", [P, 2, P], scope=once)
            qf = [sb(f"qf{i}k", [P, D], scope=once) for i in range(3)]
            with stage("loaded", "v_chain", "tanh_done") as (block, sems):
                loaded, v_chain, tanh_done = sems
                loads = [(ident, a["c_ident"]), (headmask_a, a["c_headmask_a"]), (headmask_c, a["c_headmask_c"]),
                         (vmask_a, a["c_vmask_a"]), (vmask_c, a["c_vmask_c"]), (rot, a["c_rot"]),
                         (band_f, a["c_band"]), (headones, a["c_headones"]), (headsel, a["c_headsel"]), (shift, a["c_shift"]),
                         (wa["q"], a["wa_q"]), (wa["k"], a["wa_k"]), (wa["v"], a["wa_v"]), (wa["o"], a["wa_o"]),
                         (wc["q"], a["wc_q"]), (wc["k"], a["wc_k"]), (wc["v"], a["wc_v"]), (wc["p"], a["wc_p"]),
                         (wa1, a["wa1"]), (wa2, a["wa2"].rearrange("(c p) d -> p c d", p=P)),
                         (cols_a, a["cols_a"]), (b1_a, a["b1_a"]), (kern, a["kern"]),
                         (rows, a["rows"].partition_broadcast(P)), (gates, a["gates"].partition_broadcast(P)),
                         (fscale, a["fscale"].partition_broadcast(P)), (fbias, a["fbias"].partition_broadcast(P))]
                NL = 16 * len(loads)

                @block.sync
                def _(sp):
                    for dst, src in loads:
                        sp.dma_start(dst[:], src).then_inc(loaded, 16)

                @block.scalar
                def _(act):
                    act.wait_ge(loaded, NL)
                    act.activation(tg[:], gates[:], ACT.Tanh).then_inc(tanh_done, 1)
                    act.activation(ident_bf[:], ident[:], ACT.Copy)
                    act.activation(band[:], band_f[:], ACT.Copy)

                @block.gpsimd
                def _(pool):
                    pool.memset(minus_half[:], -0.5)
                    pool.memset(ones_bf[:], 1.0)
                    pool.memset(ht[:], 0.0)

                @block.vector
                def _(dve):
                    v = Chain(dve, v_chain)
                    dve.wait_ge(loaded, NL)
                    dve.wait_ge(tanh_done, 1)
                    for i, (r, g) in enumerate(((4, 0), (5, 0), (6, 1))):
                        v.do(dve.tensor_scalar(gated_rows[:, i, :], rows[:, r, :], tg[:, g:g + 1], None, ALU.mult))
                    v.do(dve.tensor_tensor(sprod[:], fscale[:, 0:1], fscale[:, 1:2], ALU.mult))
                    v.do(dve.reciprocal(rscale[:], fscale[:]))
                    v.sync()
                    v.do(dve.tensor_scalar(qf[0][:], kern[:], rscale[:, 1:2], None, ALU.mult))
                    v.sync()
                    quantise(dve, v, qf, kern_q[:], D)

        with nc.Fori(0, B // U) as pair:
            with ExitStack() as cross_a:
                kbd_a = sb("kbd_a", [P, U, HA, SK], scope=cross_a)
                rep = sb("rep", [P, U, CA * P], scope=cross_a)
                sh = sb("sh", [P, 2, HA * SK], scope=cross_a)
                pr = sb("pr", [P, 2, HA * SK], scope=cross_a)
                pt = sb("pt", [P, CA, P], scope=cross_a)
                with stage("loaded", "kt_raw", "kt_done", "rep_done", "v_raw", "v_chain") as (block, sems):
                    loaded, kt_raw, kt_done, rep_done, v_raw, v_chain = sems

                    @block.sync
                    def _(sp):
                        pr_ = bass.ds(pair, 1)
                        sp.dma_start(ctxt[:], a["ctxt"][pr_].rearrange("o p u k -> p (o u) k")).then_inc(loaded, 16)
                        sp.dma_start(mflat[:], a["mflat"][pr_].rearrange("o p u k -> p (o u) k")).then_inc(loaded, 16)
                        sp.dma_start(mrow[:], a["mrow"][pr_]).then_inc(loaded, 16)
                        sp.dma_start(x[:], a["x"][pr_].rearrange("o (n p) d -> p (o n) d", p=P)).then_inc(loaded, 16)
                        sp.dma_start(tmat[:], a["tmat"][pr_].rearrange("o (n p) d -> p (o n) d", p=P)).then_inc(loaded, 16)

                    @block.tensor
                    def _(pe):
                        pe.wait_ge(loaded, 80)
                        c = ctxt[:].rearrange("p u k -> p (u k)")
                        pe.matmul(bank[0][:, 0:U * SK], wa["k"][:], c, start=True, stop=True).then_inc(kt_raw, 1)
                        pe.matmul(bank[1][:, 0:U * SK], wc["k"][:], c, start=True, stop=True).then_inc(kt_raw, 1)
                        for u in range(U):
                            pe.wait_ge(rep_done, u + 1)
                            for k in range(CA):
                                h0 = chunk_head(k, HA)
                                w = WIN * DA
                                mm = pe.matmul(bank[2 + u][:, k * w:(k + 1) * w], rep[:, u, k * P:(k + 1) * P],
                                               wa["v"][:, h0 * DA:h0 * DA + w], start=True, stop=True)
                            for k in range(CC):
                                h0 = chunk_head(k, HC)
                                w = WIN * DC
                                mm = pe.matmul(bank[4 + u][:, k * w:(k + 1) * w], rep[:, u, k * P:(k + 1) * P],
                                               wc["v"][:, h0 * DC:h0 * DC + w], start=True, stop=True)
                            mm.then_inc(v_raw, 1)

                    @block.scalar
                    def _(act):
                        act.wait_ge(kt_raw, 2)
                        act.activation(kt_a[:].rearrange("p u k -> p (u k)"), bank[0][:, 0:U * SK], ACT.Identity,
                                       bias=cols_a[:, 1:2])
                        act.activation(kt_c[:].rearrange("p u k -> p (u k)"), bank[1][:, 0:U * SK],
                                       ACT.Copy).then_inc(kt_done, 1)

                    @block.vector
                    def _(dve):
                        v = Chain(dve, v_chain)
                        dve.wait_ge(loaded, 80)
                        for u in range(U):
                            full = CA * P // SK
                            dve.tensor_copy(rep[:, u, 0:full * SK].rearrange("p (r k) -> p r k", k=SK),
                                            ctxt[:, u, :].unsqueeze(1).broadcast_to([P, full, SK]))
                            dve.tensor_copy(rep[:, u, full * SK:CA * P],
                                            ctxt[:, u, 0:CA * P - full * SK]).then_inc(rep_done, 1)
                        v.do(dve.tensor_scalar(keep[:], mflat[:], -1.0, 1.0, ALU.mult, ALU.add))
                        v.do(dve.tensor_scalar(mrow_bf[:], mrow[:], NEG, None, ALU.mult))
                        v.sync()
                        for u in range(U):
                            v.do(dve.tensor_tensor(kmask[:, u], vmask_a[:],
                                                   keep[:, u, :].unsqueeze(2).broadcast_to([P, CA, WIN]), ALU.mult))
                        dve.wait_ge(kt_done, 1)
                        for u in range(U):
                            dve.tensor_tensor(kbd_a[:, u], kt_a[:, u, :].unsqueeze(1).broadcast_to([P, HA, SK]),
                                              headmask_a[:].unsqueeze(2).broadcast_to([P, HA, SK]), ALU.mult)
                            dve.tensor_tensor(kbd_c[:, u], kt_c[:, u, :].unsqueeze(1).broadcast_to([P, HC, SK]),
                                              headmask_c[:].unsqueeze(2).broadcast_to([P, HC, SK]), ALU.mult)
                        v.sync()
                        for u in range(U):
                            dve.wait_ge(v_raw, u + 1)
                            for k in range(CA):
                                dve.tensor_tensor(vbd_a[:, u, k, :, 0:DA],
                                                  bank[2 + u][:, k * WIN * DA:(k + 1) * WIN * DA].rearrange(
                                                      "p (w d) -> p w d", w=WIN),
                                                  kmask[:, u, k, :].unsqueeze(2).broadcast_to([P, WIN, DA]), ALU.mult)
                            dve.tensor_copy(vbd_a[:, u, :, :, DA], kmask[:, u])
                            dve.tensor_tensor(vbd_c[:, u].rearrange("p c w d -> p (c w) d"),
                                              bank[4 + u][:, 0:CC * WIN * DC].rearrange("p (w d) -> p w d", d=DC),
                                              vmask_c[:].rearrange("p c w -> p (c w)").unsqueeze(2).broadcast_to(
                                                  [P, CC * WIN, DC]), ALU.mult)


                with stage("v_chain", "var_ready", "rstd_ready", "xn_done", "xnt_raw", "xnt_done", "q_raw", "q_done",
                           "s_raw", "s_used", "sh_done", "exp_done", "pt_raw", "pt_done", "o_raw", "att_done",
                           "attt_raw", "attt_done", "r_raw", "r_done", "base_done") as (block, sems):
                    (v_chain, var_ready, rstd_ready, xn_done, xnt_raw, xnt_done, q_raw, q_done,
                     s_raw, s_used, sh_done, exp_done, pt_raw, pt_done, o_raw, att_done,
                     attt_raw, attt_done, r_raw, r_done, base_done) = sems
                    PTG = [(0, 4), (4, 8), (8, 10)]

                    @block.vector
                    def _(dve):
                        v = Chain(dve, v_chain)
                        for u in range(U):
                            dve_stats(dve, v, u, x, var_ready)
                        for u in range(U):
                            dve_normalize(dve, u, x, xn, rstd_ready, xn_done)
                        for n in range(NT + 2):
                            if n < NT:
                                k = n % 2
                                s3 = sh[:, k, :].rearrange("p (h k) -> p h k", k=SK)
                                for g, (h0, h1) in enumerate(GA):
                                    dve.wait_ge(s_raw, 3 * n + g + 1)
                                    src = bank[g][:, 0:(h1 - h0) * SK].rearrange("p (h k) -> p h k", k=SK)
                                    v.do(dve.tensor_reduce(mx[:, k, h0:h1], src, AX.X, ALU.max))
                                v.sync()
                                if n >= 2:
                                    dve.wait_ge(exp_done, n - 1)
                                for g, (h0, h1) in enumerate(GA):
                                    src = bank[g][:, 0:(h1 - h0) * SK].rearrange("p (h k) -> p h k", k=SK)
                                    dve.tensor_tensor(s3[:, h0:h1, :], src,
                                                      mx[:, k, h0:h1].unsqueeze(2).broadcast_to([P, h1 - h0, SK]),
                                                      ALU.subtract).then_inc(s_used, 1)
                            if 1 <= n <= NT:
                                m = n - 1
                                k = m % 2
                                o3 = bank[6][:, 0:HA * (DA + 1)].rearrange("p (h d) -> p h d", d=DA + 1)
                                dve.wait_ge(o_raw, m + 1)
                                v.do(dve.reciprocal(rd[:, k, :], o3[:, :, DA]))
                                v.sync()
                                if m >= 2:
                                    dve.wait_ge(attt_raw, m - 1)
                                dve.tensor_tensor(att[:, k, :].rearrange("p (h d) -> p h d", d=DA), o3[:, :, 0:DA],
                                                  rd[:, k, :].unsqueeze(2).broadcast_to([P, HA, DA]),
                                                  ALU.mult).then_inc(att_done, 1)
                            if n >= 2:
                                m = n - 2
                                dve.wait_ge(r_raw, m + 1)
                                dve.wait_ge(base_done, m // TPB + 1)
                                dve.tensor_tensor(base[:, m, :], bank[7][:, P:2 * P], base[:, m, :],
                                                  ALU.add).then_inc(r_done, 1)

                    @block.gpsimd
                    def _(pool):
                        for u in range(U):
                            pool_rstd(pool, u, var_ready, rstd_ready)
                        for u in range(U):
                            pool.wait_ge(xn_done, TPB * (u + 1))
                            pool.tensor_tensor(base[:, TPB * u:TPB * (u + 1), :], xn[:, TPB * u:TPB * (u + 1), :],
                                               rows[:, 0:1, :].broadcast_to([P, TPB, D]), ALU.add).then_inc(base_done, 1)

                    @block.tensor
                    def _(pe):
                        for u in range(U):
                            for j in range(TPB):
                                n = TPB * u + j
                                pe.wait_ge(xn_done, n + 1)
                                t = pe.transpose(bank[2 * u][:, j * P:(j + 1) * P], xn[:, n, :], ident[:])
                            t.then_inc(xnt_raw, 1)
                        for u in range(U):
                            pe.wait_ge(xnt_done, u + 1)
                            pe.matmul(bank[2 * u + 1][:], wa["q"][:], xt[:, u, :], start=True, stop=True).then_inc(q_raw, 1)
                        for n in range(NT + 2):
                            if n < NT:
                                u, j = divmod(n, TPB)
                                pe.wait_ge(q_done, U)
                                for g, (h0, h1) in enumerate(GA):
                                    if n:
                                        pe.wait_ge(s_used, 3 * (n - 1) + g + 1)
                                    w = (h1 - h0) * SK
                                    pe.matmul(bank[g][:, 0:w], ones_bf[:],
                                              mrow_bf[:, u:u + 1, :].broadcast_to([1, h1 - h0, SK]), start=True, stop=False)
                                    pe.matmul(bank[g][:, 0:w], qt[:, u, j * P:(j + 1) * P],
                                              kbd_a[:, u, h0:h1, :].rearrange("p h k -> p (h k)"),
                                              start=False, stop=True).then_inc(s_raw, 1)
                            if 1 <= n <= NT:
                                m = n - 1
                                u = m // TPB
                                pe.wait_ge(exp_done, m + 1)
                                for g, (c0, c1) in enumerate(PTG):
                                    if m:
                                        pe.wait_ge(pt_done, 3 * (m - 1) + g + 1)
                                    for c in range(c0, c1):
                                        r = chunk_rows(c, HA)
                                        t = pe.transpose(bank[3 + g][0:r, (c - c0) * P:(c - c0 + 1) * P],
                                                         pr[:, m % 2, c * P:c * P + r], ident[:])
                                    t.then_inc(pt_raw, 1)
                                if m:
                                    pe.wait_ge(att_done, m)
                                for c in range(CA):
                                    r, h0 = chunk_rows(c, HA), chunk_head(c, HA)
                                    pe.wait_ge(pt_done, 3 * m + min(c // 4, 2) + 1)
                                    mm = pe.matmul(bank[6][:, h0 * (DA + 1):(h0 + WIN) * (DA + 1)], pt[0:r, c, :],
                                                   vbd_a[0:r, u, c, :, :].rearrange("p w d -> p (w d)"),
                                                   start=(c == 0), stop=True, skip_group_check=True)
                                mm.then_inc(o_raw, 1)
                            if n >= 2:
                                m = n - 2
                                pe.wait_ge(att_done, m + 1)
                                if m:
                                    pe.wait_ge(attt_done, m)
                                    pe.wait_ge(r_done, m)
                                pe.transpose(bank[7][:, 0:P], att[:, m % 2, :], ident[:]).then_inc(attt_raw, 1)
                                pe.wait_ge(attt_done, m + 1)
                                pe.matmul(bank[7][:, P:2 * P], attt[:, m % 2, :], wa["o"][:], start=True,
                                          stop=True).then_inc(r_raw, 1)

                    @block.scalar
                    def _(act):
                        for u in range(U):
                            act.wait_ge(xnt_raw, u + 1)
                            act.activation(xt[:, u, :], bank[2 * u][:], ACT.Copy).then_inc(xnt_done, 1)
                        for u in range(U):
                            act.wait_ge(q_raw, u + 1)
                            act.activation(qt[:, u, :], bank[2 * u + 1][:], ACT.Identity,
                                           bias=cols_a[:, 0:1]).then_inc(q_done, 1)
                        for n in range(NT + 2):
                            if 1 <= n <= NT:
                                m = n - 1
                                if m:
                                    act.wait_ge(o_raw, m)
                                for g, (c0, c1) in enumerate(PTG):
                                    act.wait_ge(pt_raw, 3 * m + g + 1)
                                    if g < 2:
                                        act.activation(pt[:, c0:c1, :], bank[3 + g][:].rearrange("p (c q) -> p c q", q=P),
                                                       ACT.Copy).then_inc(pt_done, 1)
                                    else:
                                        r = chunk_rows(CA - 1, HA)
                                        act.activation(pt[:, 8, :], bank[5][:, 0:P], ACT.Copy)
                                        act.activation(pt[0:r, 9, :], bank[5][0:r, P:2 * P], ACT.Copy).then_inc(pt_done, 1)
                            if n >= 2:
                                m = n - 2
                                act.wait_ge(attt_raw, m + 1)
                                if m >= 2:
                                    act.wait_ge(r_raw, m - 1)
                                act.activation(attt[:, m % 2, :], bank[7][:, 0:P], ACT.Identity,
                                               bias=cols_a[:, 2:3]).then_inc(attt_done, 1)
                            if n < NT:
                                act.wait_ge(s_used, 3 * (n + 1))
                                if n >= 2:
                                    act.wait_ge(pt_raw, 3 * (n - 1))
                                act.activation(pr[:, n % 2, :], sh[:, n % 2, :], ACT.Exp,
                                               scale=DA ** -0.5).then_inc(exp_done, 1)


            with ExitStack() as ffn:
                hidt = sb("hidt", [P, U, FF // P, S], scope=ffn)
                with stage("v_chain", "p_chain", "var1", "rstd1", "var2", "rstd2", "var3", "rstd3", "xn_done", "xnt_raw",
                           "xnt_done", "h_raw", "h_done", "f_raw", "base_done", "ln2_done", "x_done") as (block, sems):
                    (v_chain, p_chain, var1, rstd1, var2, rstd2, var3, rstd3, xn_done, xnt_raw,
                     xnt_done, h_raw, h_done, f_raw, base_done, ln2_done, x_done) = sems
                    NC = FF // P

                    @block.vector
                    def _(dve):
                        v = Chain(dve, v_chain)
                        for u in range(U):
                            dve_stats(dve, v, u, base, var1)
                        for u in range(U):
                            dve_normalize(dve, u, base, xn, rstd1, xn_done)
                        for u in range(U):
                            sl = slice(TPB * u, TPB * (u + 1))
                            dve.wait_ge(f_raw, u + 1)
                            dve.wait_ge(base_done, u + 1)
                            v.do(dve.tensor_tensor(base[:, sl, :], bank[6 + u][:].rearrange("p (j d) -> p j d", d=D),
                                                   base[:, sl, :], ALU.add))
                            v.sync()
                            dve_stats(dve, v, u, base, var2)
                        for u in range(U):
                            dve_normalize(dve, u, base, base, rstd2, ln2_done)
                        for u in range(U):
                            dve.wait_ge(x_done, u + 1)
                            dve_stats(dve, v, u, x, var3)
                        for u in range(U):
                            dve_normalize(dve, u, x, y, rstd3)

                    @block.gpsimd
                    def _(pool):
                        p = Chain(pool, p_chain)

                        def rows_op(u, dst, src, t, r, op):
                            sl = slice(TPB * u, TPB * (u + 1))
                            return pool.tensor_tensor(dst[:, sl, :], src[:, sl, :],
                                                      t[:, r:r + 1, :].broadcast_to([P, TPB, D]), op)

                        for u in range(U):
                            pool_rstd(pool, u, var1, rstd1)
                        for u in range(U):
                            pool.wait_ge(xn_done, TPB * (u + 1))
                            p.do(rows_op(u, base, xn, rows, 1, ALU.mult))
                            p.sync()
                            p.do(rows_op(u, base, base, rows, 2, ALU.add))
                            p.sync()
                            rows_op(u, base, base, rows, 3, ALU.add).then_inc(base_done, 1)
                        for u in range(U):
                            pool_rstd(pool, u, var2, rstd2)
                        for u in range(U):
                            sl = slice(TPB * u, TPB * (u + 1))
                            pool.wait_ge(ln2_done, TPB * (u + 1))
                            p.do(rows_op(u, base, base, gated_rows, 0, ALU.mult))
                            p.do(rows_op(u, x, x, gated_rows, 1, ALU.add))
                            p.sync()
                            pool.tensor_tensor(x[:, sl, :], x[:, sl, :], base[:, sl, :], ALU.add).then_inc(x_done, 1)
                        for u in range(U):
                            pool_rstd(pool, u, var3, rstd3)

                    @block.tensor
                    def _(pe):
                        for u in range(U):
                            for j in range(TPB):
                                n = TPB * u + j
                                pe.wait_ge(xn_done, n + 1)
                                t = pe.transpose(bank[u][:, j * P:(j + 1) * P], xn[:, n, :], ident[:])
                            t.then_inc(xnt_raw, 1)
                        for u in range(U):
                            pe.wait_ge(xnt_done, u + 1)
                            for c in range(NC):
                                if u:
                                    pe.wait_ge(h_done, NC * (u - 1) + c + 1)
                                pe.matmul(bank[2 + c][:], wa1[:, c * P:(c + 1) * P], xt[:, u, :], start=True,
                                          stop=True).then_inc(h_raw, 1)
                        for u in range(U):
                            pe.wait_ge(h_done, NC * (u + 1))
                            for j in range(TPB):
                                for c in range(NC):
                                    mm = pe.matmul(bank[6 + u][:, j * P:(j + 1) * P], hidt[:, u, c, j * P:(j + 1) * P],
                                                   wa2[:, c, :], start=(c == 0), stop=(c == NC - 1))
                            mm.then_inc(f_raw, 1)

                    @block.scalar
                    def _(act):
                        for u in range(U):
                            act.wait_ge(xnt_raw, u + 1)
                            act.activation(xt[:, u, :], bank[u][:], ACT.Identity, bias=cols_a[:, 4:5],
                                           scale=cols_a[:, 3:4]).then_inc(xnt_done, 1)
                        for u in range(U):
                            for c in range(NC):
                                act.wait_ge(h_raw, NC * u + c + 1)
                                act.activation(hidt[:, u, c, :], bank[2 + c][:], ACT.Gelu,
                                               bias=b1_a[:, c:c + 1]).then_inc(h_done, 1)

            with nc.Fori(0, DEPTH) as layer:
                with ExitStack() as local:
                    rt = sb("rt", [P, 4, S], scope=local)
                    sq = sb("sq", [P, 2, S], scope=local)
                    t1 = sb("t1", [P, 2, S], scope=local)
                    t2 = sb("t2", [P, 2, S], scope=local)
                    qtb = sb("qtb", [P, U, 4, S], scope=local)
                    krb = sb("krb", [P, 4, S], scope=local)
                    ktb = sb("ktb", [P, U, 4, PAD + S], scope=local)
                    va = sb("va", [P, U, TPB, INNER], scope=local)
                    vm = sb("vm", [P, U, TPB + 1, INNER], scope=local)
                    pb = sb("pb", [P, 2, HB, P], scope=local)
                    ptb = sb("ptb", [P, HB, P], scope=local)
                    on = xt
                    ont = qt
                    with stage("loaded", "y_raw", "ht_done", "pads_done", "swap_done", "rt_done", "p_raw", "sq_done", "t_done", "sum_done", "n2_raw",
                               "n2_done", "rn_done", "rnt_raw", "rnt_done", "rk_raw", "kt_done", "v_raw", "v_done") as (block, sems):
                        (loaded, y_raw, ht_done, pads_done, swap_done, rt_done, p_raw, sq_done, t_done, sum_done, n2_raw,
                         n2_done, rn_done, rnt_raw, rnt_done, rk_raw, kt_done, v_raw, v_done) = sems
                        NS = 8
                        NL = 16 * 7

                        @block.sync
                        def _(sp):
                            l = bass.ds(layer, 1)
                            sp.dma_start(wqkv[:], a["wqkv"][l].rearrange("o p n -> (o p) n")).then_inc(loaded, 16)
                            sp.dma_start(cols_b[:], a["cols_b"][l].rearrange("o p n -> (o p) n")).then_inc(loaded, 16)
                            sp.dma_start(wo_b[:], a["wo_b"][l].rearrange("o (c p) d -> p (o c) d", p=P)).then_inc(loaded, 16)
                            sp.dma_start(w1_b[:], a["w1_b"][l].rearrange("o p n -> (o p) n")).then_inc(loaded, 16)
                            sp.dma_start(w2_b[:, 0:2, :], a["w2_b"][l, 0:2 * P, :].rearrange(
                                "o (c p) d -> p (o c) d", p=P)).then_inc(loaded, 16)
                            sp.dma_start(w2_b[0:HID - 2 * P, 2, :], a["w2_b"][l, 2 * P:HID, :].rearrange(
                                "o p d -> p (o d)")).then_inc(loaded, 16)
                            sp.dma_start(row_b[:], a["row_b"][l].partition_broadcast(P).rearrange(
                                "p o d -> p (o d)")).then_inc(loaded, 16)

                        @block.tensor
                        def _(pe):
                            for u in range(U):
                                for j in range(TPB):
                                    t = pe.transpose(bank[u][:, j * P:(j + 1) * P], y[:, TPB * u + j, :], ident[:])
                                t.then_inc(y_raw, 1)
                            pe.wait_ge(loaded, NL)
                            pe.wait_ge(swap_done, 1)
                            for u in range(U):
                                pe.wait_ge(ht_done, u + 1)
                                h = ht[:, u, PAD:PAD + S]
                                for s in range(NS + 1):
                                    if s < NS:
                                        c, kind = divmod(s, 2)
                                        w0 = kind * INNER + c * P
                                        w = wqkv[:, w0:w0 + P]
                                        g = NS * u + s
                                        if g >= 2:
                                            pe.wait_ge(sq_done, g - 1)
                                            pe.wait_ge(t_done, g - 1)
                                        b0 = 2 + 2 * (s % 2)
                                        pe.matmul(bank[b0][:], w, h, start=True, stop=True)
                                        halves = wswap[:, kind * HB + 2 * c:kind * HB + 2 * c + 2].rearrange(
                                            "p h a e -> p (h a e)")
                                        pe.matmul(bank[b0 + 1][:], halves, h, start=True, stop=True).then_inc(p_raw, 1)
                                    if s:
                                        c, kind = divmod(s - 1, 2)
                                        pe.wait_ge(sq_done, NS * u + s)
                                        if u:
                                            pe.wait_ge(n2_done, u)
                                        for j in range(TPB):
                                            col = 64 * u + (j * 2 + kind) * HB + 2 * c
                                            mm = pe.matmul(bank[7][:, col:col + 2], sq[:, (s - 1) % 2, j * P:(j + 1) * P],
                                                           headones[:], start=True, stop=True)
                                        mm.then_inc(n2_raw, 1)
                                for j in range(TPB):
                                    g = TPB * u + j
                                    if g >= 2:
                                        pe.wait_ge(v_done, g - 1)
                                    else:
                                        pe.wait_ge(ht_done, U)
                                    pe.matmul(bank[j % 2][:], ht[:, u, PAD + j * P:PAD + (j + 1) * P],
                                              wqkv[:, 2 * INNER:], start=True, stop=True).then_inc(v_raw, 1)
                                pe.wait_ge(rn_done, u + 1)
                                if u:
                                    pe.wait_ge(kt_done, 4 * u)
                                for j in range(TPB):
                                    t = pe.transpose(bank[6][0:HB, j * P:(j + 1) * P], rn[:, u, j, 1, :], ident[:])
                                t.then_inc(rnt_raw, 1)
                                pe.wait_ge(rnt_done, u + 1)
                                for c in range(4):
                                    g = 4 * u + c
                                    if c:
                                        pe.wait_ge(kt_done, g)
                                    pe.matmul(bank[6][:], headsel[:, c, :], rnt[:, u, :], start=True,
                                              stop=True).then_inc(rk_raw, 1)

                        @block.scalar
                        def _(act):
                            for u in range(U):
                                act.wait_ge(y_raw, u + 1)
                                act.activation(ht[0:64, u, PAD:PAD + S], bank[u][0:64, :], ACT.Copy)
                                act.activation(ht[64:128, u, PAD + 1:PAD + S + 1], bank[u][64:128, :],
                                               ACT.Copy).then_inc(ht_done, 1)
                            for u in range(U):
                                for s in range(NS):
                                    g = NS * u + s
                                    act.wait_ge(p_raw, g + 1)
                                    if g >= 2:
                                        act.wait_ge(n2_raw, g - 1)
                                    act.activation(sq[:, s % 2, :], bank[2 + 2 * (s % 2)][:], ACT.Square).then_inc(sq_done, 1)
                                for j in range(TPB):
                                    act.wait_ge(v_raw, TPB * u + j + 1)
                                    act.activation(va[:, u, j, :], bank[j % 2][:], ACT.Copy)
                                    act.activation(vm[0:64, u, j, :], bank[j % 2][0:64, :], ACT.Copy)
                                    act.activation(vm[64:128, u, j + 1, :], bank[j % 2][64:128, :],
                                                   ACT.Copy).then_inc(v_done, 1)
                                act.wait_ge(rnt_raw, u + 1)
                                act.activation(rnt[:, u, :], bank[6][0:HB, :], ACT.Copy).then_inc(rnt_done, 1)

                        @block.vector
                        def _(dve):
                            dve.wait_ge(loaded, NL)
                            w = wqkv[:, 0:2 * INNER].rearrange("p (h a e) -> p h a e", a=2, e=DH // 2)
                            for half in range(2):
                                r = dve.tensor_copy(wswap[:, :, half, :], w[:, :, 1 - half, :])
                            r.then_inc(swap_done, 1)
                            for i in range(4):
                                r = dve.tensor_scalar(rt[:, i, :], rot[:, i, :], cols_b[:, i:i + 1], None, ALU.mult)
                            r.then_inc(rt_done, 1)
                            dve.wait_ge(rt_done, 1)
                            for u in range(U):
                                for s in range(NS):
                                    g = NS * u + s
                                    kind = s % 2
                                    b0 = 2 + 2 * kind
                                    dve.wait_ge(p_raw, g + 1)
                                    if g >= 2:
                                        dve.wait_ge(sum_done, g - 1)
                                    dve.tensor_tensor(t2[:, s % 2, :], bank[b0 + 1][:], rt[:, 2 * kind + 1, :], ALU.mult)
                                    dve.wait_ge(sq_done, g + 1)
                                    dve.tensor_tensor(t1[:, s % 2, :], bank[b0][:], rt[:, 2 * kind, :],
                                                      ALU.mult).then_inc(t_done, 1)
                                dve.wait_ge(n2_raw, NS * (u + 1))
                                dve.tensor_scalar(n2[:, u, :], bank[7][:, 64 * u:64 * u + 64], 1e-24, None,
                                                  ALU.max).then_inc(n2_done, 1)
                                dve.wait_ge(sum_done, NS * (u + 1))
                                for c in range(4):
                                    dve.wait_ge(rk_raw, 4 * u + c + 1)
                                    dve.tensor_tensor(ktb[:, u, c, PAD:PAD + S], bank[6][:], krb[:, c, :],
                                                      ALU.mult).then_inc(kt_done, 1)

                        @block.gpsimd
                        def _(pool):
                            pool.memset(ktb[:, :, :, 0:PAD], 0.0).then_inc(pads_done, 1)
                            pool.wait_ge(pads_done, 1)
                            pool.memset(vm[64:128, :, 0, :], 0.0).then_inc(pads_done, 1)
                            pool.wait_ge(pads_done, 2)
                            for u in range(U):
                                for s in range(NS):
                                    c, kind = divmod(s, 2)
                                    g = NS * u + s
                                    pool.wait_ge(t_done, g + 1)
                                    if kind and u:
                                        pool.wait_ge(kt_done, 4 * (u - 1) + c + 1)
                                    dst = krb[:, c, :] if kind else qtb[:, u, c, :]
                                    pool.tensor_tensor(dst, t1[:, s % 2, :], t2[:, s % 2, :], ALU.add).then_inc(sum_done, 1)
                                pool.wait_ge(n2_done, u + 1)
                                pool.tensor_tensor(rn[:, u].rearrange("p j k h -> p (j k h)"), n2[:, u, :],
                                                   minus_half[:], ALU.pow).then_inc(rn_done, 1)

                    with stage("v_chain", "qsc_done", "s_raw", "s_used", "nb_done", "exp_done", "pt_raw", "pt_done", "o_raw",
                               "on_done", "ont_raw", "ont_done", "r_raw", "r_done") as (block, sems):
                        (v_chain, qsc_done, s_raw, s_used, nb_done, exp_done, pt_raw, pt_done, o_raw,
                         on_done, ont_raw, ont_done, r_raw, r_done) = sems

                        @block.tensor
                        def _(pe):
                            for n in range(NT + 2):
                                if n < NT:
                                    u, j = divmod(n, TPB)
                                    if n >= 2:
                                        pe.wait_ge(exp_done, HB * (n - 1))
                                    for g in range(2):
                                        pe.matmul(bank[2 * (n % 2) + g][:], ident_bf[:], band[:, 0 if j else 1, :].unsqueeze(1).broadcast_to(
                                            [P, 4, P]), start=True, stop=True, skip_group_check=True)
                                    q0 = j * P
                                    for c in range(4):
                                        for g in range(2):
                                            bk, r, col = bank[2 * (n % 2) + g], slice(64 * g, 64 * g + 64), slice(c * P, (c + 1) * P)
                                            keys = ktb[r, u, c, q0:q0 + P].rearrange("p (a e) -> p a e", a=2)[:, ::-1, :]
                                            pe.matmul(bk[0:64, col], qtb[r, u, c, q0:q0 + 64], keys, start=False, stop=True,
                                                      skip_group_check=True)
                                            mm = pe.matmul(bk[64:128, col], qtb[r, u, c, q0 + 64:q0 + P],
                                                           ktb[r, u, c, PAD + q0:PAD + q0 + P], start=False, stop=True,
                                                           skip_group_check=True)
                                            if c == 3:
                                                mm.then_inc(s_raw, 1)
                                if 1 <= n <= NT:
                                    m = n - 1
                                    u, j = divmod(m, TPB)
                                    for g in range(2):
                                        pe.wait_ge(exp_done, HB * m + 4 * g + 4)
                                        if m:
                                            pe.wait_ge(pt_done, 2 * (m - 1) + g + 1)
                                        for c in range(4):
                                            t = pe.transpose(bank[4 + g][:, c * P:(c + 1) * P], pb[:, m % 2, 2 * c + g, :],
                                                             ident[:])
                                        t.then_inc(pt_raw, 1)
                                    if m:
                                        pe.wait_ge(on_done, m)
                                    for i in range(HB):
                                        h = 2 * (i % 4) + i // 4
                                        pe.wait_ge(pt_done, 2 * m + i // 4 + 1)
                                        hs = slice(h * DH, (h + 1) * DH)
                                        pe.matmul(bank[6][0:64, hs], ptb[:, i, 0:64], vm[:, u, j, hs], start=True, stop=True)
                                        mm = pe.matmul(bank[6][64:128, hs], ptb[:, i, 64:128], va[:, u, j, hs], start=True,
                                                       stop=True)
                                    mm.then_inc(o_raw, 1)
                                if n >= 2:
                                    m = n - 2
                                    pe.wait_ge(on_done, m + 1)
                                    if m:
                                        pe.wait_ge(ont_done, m)
                                        pe.wait_ge(r_done, m)
                                    for c in range(4):
                                        t = pe.transpose(bank[7][:, c * P:(c + 1) * P], on[:, m % 2, c * P:(c + 1) * P], ident[:])
                                    t.then_inc(ont_raw, 1)
                                    pe.wait_ge(ont_done, m + 1)
                                    for c in range(4):
                                        mm = pe.matmul(bank[7][:, 0:P], ont[:, m % 2, c * P:(c + 1) * P], wo_b[:, c, :],
                                                       start=(c == 0), stop=(c == 3))
                                    mm.then_inc(r_raw, 1)

                        @block.scalar
                        def _(act):
                            for n in range(NT + 2):
                                if 1 <= n <= NT:
                                    m = n - 1
                                    if m:
                                        act.wait_ge(o_raw, m)
                                    for g in range(2):
                                        act.wait_ge(pt_raw, 2 * m + g + 1)
                                        act.activation(ptb[:, 4 * g:4 * g + 4, :], bank[4 + g][:].rearrange(
                                            "p (h q) -> p h q", q=P), ACT.Copy).then_inc(pt_done, 1)
                                if n >= 2:
                                    m = n - 2
                                    act.wait_ge(ont_raw, m + 1)
                                    if m >= 2:
                                        act.wait_ge(r_raw, m - 1)
                                    act.activation(ont[:, m % 2, :], bank[7][:], ACT.Copy).then_inc(ont_done, 1)
                                if n < NT:
                                    k = n % 2
                                    act.wait_ge(qsc_done, 1)
                                    if n >= 2:
                                        act.wait_ge(pt_raw, 2 * (n - 1))
                                        act.wait_ge(on_done, n - 1)
                                    for i in range(HB):
                                        h = 2 * (i % 4) + i // 4
                                        if i % 4 == 0:
                                            act.wait_ge(nb_done, 2 * n + i // 4 + 1)
                                        act.activation(pb[:, k, h, :], bank[2 * k + i // 4][:, (i % 4) * P:(i % 4 + 1) * P],
                                                       ACT.Exp, bias=nb[:, k, h:h + 1], scale=qsc[:, n, h:h + 1],
                                                       accum_out=den[:, k, h:h + 1]).then_inc(exp_done, 1)

                        @block.vector
                        def _(dve):
                            v = Chain(dve, v_chain)
                            dve.tensor_scalar(qsc[:].rearrange("p (u j) h -> p u j h", u=U), rn[:, :, :, 0, :], 8.0, None,
                                              ALU.mult).then_inc(qsc_done, 1)
                            dve.wait_ge(qsc_done, 1)
                            for n in range(NT + 2):
                                if n < NT:
                                    k = n % 2
                                    for g in range(2):
                                        hs = slice(g, HB, 2)
                                        dve.wait_ge(s_raw, 2 * n + g + 1)
                                        v.do(dve.tensor_reduce(mx[:, k, hs], bank[2 * k + g][:].rearrange(
                                            "p (h q) -> p h q", q=P), AX.X, ALU.max))
                                        v.sync()
                                        if n >= 2:
                                            dve.wait_ge(exp_done, HB * (n - 1))
                                        dve.scalar_tensor_tensor(out=nb[:, k, hs], in0=mx[:, k, hs], scalar=-1.0,
                                                                 in1=qsc[:, n, hs], op0=ALU.mult,
                                                                 op1=ALU.mult).then_inc(nb_done, 1)
                                if 1 <= n <= NT:
                                    m = n - 1
                                    k = m % 2
                                    dve.wait_ge(o_raw, m + 1)
                                    dve.wait_ge(exp_done, HB * (m + 1))
                                    v.do(dve.reciprocal(rd[:, k, 0:HB], den[:, k, 0:HB]))
                                    v.sync()
                                    if m >= 2:
                                        dve.wait_ge(ont_raw, m - 1)
                                    dve.tensor_tensor(on[:, k, :].rearrange("p (h d) -> p h d", d=DH),
                                                      bank[6][:].rearrange("p (h d) -> p h d", d=DH),
                                                      rd[:, k, 0:HB].unsqueeze(2).broadcast_to([P, HB, DH]),
                                                      ALU.mult).then_inc(on_done, 1)
                                if n >= 2:
                                    m = n - 2
                                    dve.wait_ge(r_raw, m + 1)
                                    dve.tensor_tensor(y[:, m, :], bank[7][:, 0:P], y[:, m, :], ALU.add).then_inc(r_done, 1)

                with ExitStack() as ffn:
                    hidt = sb("hidt_b", [P, U, len(HCH), S], scope=ffn)
                    gel = sb("gel", [P, 2, S], scope=ffn)
                    with stage("v_chain", "sh_raw", "var_ready", "rstd_ready", "xn_done", "xnt_raw", "xnt_done", "g_raw",
                               "gel_done", "hid_done", "f_raw", "base_done") as (block, sems):
                        (v_chain, sh_raw, var_ready, rstd_ready, xn_done, xnt_raw, xnt_done, g_raw,
                         gel_done, hid_done, f_raw, base_done) = sems
                        NH = len(HCH)

                        @block.tensor
                        def _(pe):
                            for u in range(U):
                                t0 = TPB * u
                                pe.matmul(bank[u][:, 0:TPB * 64], shift[:, 0, :], y[:, t0:t0 + TPB, 64:128], start=True,
                                          stop=True, skip_group_check=True)
                                pe.matmul(bank[u][:, 64:TPB * 64], shift[:, 1, :], y[:, t0:t0 + TPB - 1, 64:128],
                                          start=False, stop=True, skip_group_check=True).then_inc(sh_raw, 1)
                            for u in range(U):
                                pe.wait_ge(xn_done, TPB * (u + 1))
                                for j in range(TPB):
                                    t = pe.transpose(bank[u][:, j * P:(j + 1) * P], xn[:, TPB * u + j, :], ident[:])
                                t.then_inc(xnt_raw, 1)
                            for u in range(U):
                                pe.wait_ge(xnt_done, u + 1)
                                for c, (h0, w) in enumerate(HCH):
                                    g = NH * u + c
                                    if g >= 2:
                                        pe.wait_ge(hid_done, g - 1)
                                    b0 = 2 + 2 * (g % 2)
                                    pe.matmul(bank[b0][0:w, :], w1_b[:, h0:h0 + w], xt[:, u, :], start=True, stop=True)
                                    pe.matmul(bank[b0 + 1][0:w, :], w1_b[:, HID + h0:HID + h0 + w], xt[:, u, :], start=True,
                                              stop=True).then_inc(g_raw, 1)
                            for u in range(U):
                                pe.wait_ge(hid_done, NH * (u + 1))
                                for j in range(TPB):
                                    for c, (h0, w) in enumerate(HCH):
                                        mm = pe.matmul(bank[6 + u][:, j * P:(j + 1) * P], hidt[0:w, u, c, j * P:(j + 1) * P],
                                                       w2_b[0:w, c, :], start=(c == 0), stop=(c == NH - 1))
                                mm.then_inc(f_raw, 1)

                        @block.scalar
                        def _(act):
                            for u in range(U):
                                act.wait_ge(xnt_raw, u + 1)
                                act.activation(xt[:, u, :], bank[u][:], ACT.Identity, bias=cols_b[:, 5:6],
                                               scale=cols_b[:, 4:5]).then_inc(xnt_done, 1)
                            for u in range(U):
                                for c, (h0, w) in enumerate(HCH):
                                    g = NH * u + c
                                    act.wait_ge(g_raw, g + 1)
                                    if g >= 2:
                                        act.wait_ge(hid_done, g - 1)
                                    act.activation(gel[0:w, g % 2, :], bank[3 + 2 * (g % 2)][0:w, :], ACT.Gelu,
                                                   bias=cols_b[0:w, 9 + c:10 + c]).then_inc(gel_done, 1)

                        @block.gpsimd
                        def _(pool):
                            for u in range(U):
                                pool_rstd(pool, u, var_ready, rstd_ready)
                            for u in range(U):
                                sl = slice(TPB * u, TPB * (u + 1))
                                pool.tensor_tensor(base[:, sl, :], y[:, sl, :], row_b[:].unsqueeze(1).broadcast_to([P, TPB, D]),
                                                   ALU.add).then_inc(base_done, 1)

                        @block.vector
                        def _(dve):
                            v = Chain(dve, v_chain)
                            for u in range(U):
                                dve.wait_ge(sh_raw, u + 1)
                                dve_stats(dve, v, u, y, var_ready, lambda j: bank[u][:, 64 * j:64 * j + 64])
                            for u in range(U):
                                dve_normalize(dve, u, y, xn, rstd_ready, xn_done, lambda j: bank[u][:, 64 * j:64 * j + 64])
                            for u in range(U):
                                for c, (h0, w) in enumerate(HCH):
                                    g = NH * u + c
                                    dve.wait_ge(gel_done, g + 1)
                                    dve.scalar_tensor_tensor(out=hidt[0:w, u, c, :], in0=bank[2 + 2 * (g % 2)][0:w, :],
                                                             scalar=cols_b[0:w, 6 + c:7 + c], in1=gel[0:w, g % 2, :],
                                                             op0=ALU.add, op1=ALU.mult).then_inc(hid_done, 1)
                            for u in range(U):
                                sl = slice(TPB * u, TPB * (u + 1))
                                dve.wait_ge(f_raw, u + 1)
                                dve.wait_ge(base_done, u + 1)
                                dve.tensor_tensor(y[:, sl, :], bank[6 + u][:].rearrange("p (j d) -> p j d", d=D),
                                                  base[:, sl, :], ALU.add)

            with ExitStack() as cross_c:
                sh = sb("sh_c", [P, 2, HA * SK], scope=cross_c)
                gt = sb("gt_c", [P, 2, HC * SK], scope=cross_c)
                pr = sb("pr_c", [P, 2, HA * SK], scope=cross_c)
                pt = sb("pt_c", [P, CA, P], scope=cross_c)
                with stage("v_chain", "var_ready", "rstd_ready", "xn_done", "xnt_raw", "xnt_done", "q_raw", "q_done",
                           "s_raw", "g_done", "sh_done", "exp_done", "pm_done", "pt_raw", "pt_done", "o_raw", "att_done",
                           "attt_raw", "attt_done", "r_raw", "r_done", "x_stats", "base_done") as (block, sems):
                    (v_chain, var_ready, rstd_ready, xn_done, xnt_raw, xnt_done, q_raw, q_done,
                     s_raw, g_done, sh_done, exp_done, pm_done, pt_raw, pt_done, o_raw, att_done,
                     attt_raw, attt_done, r_raw, r_done, x_stats, base_done) = sems
                    WC_ = HC * SK

                    @block.vector
                    def _(dve):
                        v = Chain(dve, v_chain)
                        v.do(dve.scalar_tensor_tensor(out=x[:], in0=y[:], scalar=tg[:, 2:3], in1=x[:], op0=ALU.mult,
                                                      op1=ALU.add))
                        v.sync()
                        for u in range(U):
                            dve_stats(dve, v, u, x, var_ready)
                        for u in range(U):
                            dve_normalize(dve, u, x, xn, rstd_ready, xn_done)
                        for n in range(NT + 2):
                            if n < NT:
                                k = n % 2
                                g3 = gt[:, k, :].rearrange("p (h k) -> p h k", k=SK)
                                if n >= 2:
                                    dve.wait_ge(pm_done, n - 1)
                                for g, (h0, h1) in enumerate(GC):
                                    dve.wait_ge(s_raw, 2 * n + g + 1)
                                    src = bank[2 * k + g][:, 0:(h1 - h0) * SK].rearrange("p (h k) -> p h k", k=SK)
                                    dve.tensor_tensor(g3[:, h0:h1, :], src, tmat[:, n:n + 1, :].broadcast_to(
                                        [P, h1 - h0, SK]), ALU.mult).then_inc(g_done, 1)
                                dve.wait_ge(g_done, 2 * (n + 1))
                                v.do(dve.tensor_reduce(mx[:, k, 0:HC], g3, AX.X, ALU.max))
                                v.sync()
                                if n >= 2:
                                    dve.wait_ge(exp_done, n - 1)
                                dve.tensor_tensor(sh[:, k, 0:WC_].rearrange("p (h k) -> p h k", k=SK), g3,
                                                  mx[:, k, 0:HC].unsqueeze(2).broadcast_to([P, HC, SK]),
                                                  ALU.subtract).then_inc(sh_done, 1)
                            if 1 <= n <= NT:
                                m = n - 1
                                k = m % 2
                                dve.wait_ge(exp_done, m + 1)
                                v.do(dve.tensor_reduce(den[:, k, 0:HC], sh[:, k, 0:WC_].rearrange("p (h k) -> p h k", k=SK),
                                                       AX.X, ALU.add))
                                if m >= 2:
                                    dve.wait_ge(pt_raw, 2 * (m - 1))
                                dve.scalar_tensor_tensor(out=pr[:, k, 0:WC_], in0=gt[:, k, :], scalar=0.0,
                                                         in1=sh[:, k, 0:WC_], op0=ALU.not_equal,
                                                         op1=ALU.mult).then_inc(pm_done, 1)
                                v.sync()
                                v.do(dve.reciprocal(rd[:, k, 0:HC], den[:, k, 0:HC]))
                            if n >= 2:
                                m = n - 2
                                k = m % 2
                                dve.wait_ge(o_raw, m + 1)
                                v.sync()
                                if m >= 2:
                                    dve.wait_ge(attt_raw, m - 1)
                                dve.tensor_tensor(att[:, k, :].rearrange("p (h d) -> p h d", d=DC),
                                                  bank[6][:, 0:P].rearrange("p (h d) -> p h d", d=DC),
                                                  rd[:, k, 0:HC].unsqueeze(2).broadcast_to([P, HC, DC]),
                                                  ALU.mult).then_inc(att_done, 1)
                                dve.wait_ge(r_raw, m + 1)
                                dve.wait_ge(base_done, 2)
                                dve.scalar_tensor_tensor(out=x[:, m, :], in0=bank[7][:, P:2 * P], scalar=tg[:, 1:2],
                                                         in1=base[:, m, :], op0=ALU.mult, op1=ALU.add).then_inc(r_done, 1)

                    @block.gpsimd
                    def _(pool):
                        for u in range(U):
                            pool_rstd(pool, u, var_ready, rstd_ready)
                        for u in range(U):
                            sl = slice(TPB * u, TPB * (u + 1))
                            pool.tensor_tensor(base[:, sl, :], x[:, sl, :], gated_rows[:, 2:3, :].broadcast_to([P, TPB, D]),
                                               ALU.add).then_inc(base_done, 1)

                    @block.tensor
                    def _(pe):
                        for u in range(U):
                            for j in range(TPB):
                                n = TPB * u + j
                                pe.wait_ge(xn_done, n + 1)
                                t = pe.transpose(bank[2 * u][:, j * P:(j + 1) * P], xn[:, n, :], ident[:])
                            t.then_inc(xnt_raw, 1)
                        for u in range(U):
                            pe.wait_ge(xnt_done, u + 1)
                            pe.matmul(bank[2 * u + 1][:], wc["q"][:], xt[:, u, :], start=True, stop=True).then_inc(q_raw, 1)
                        for n in range(NT + 2):
                            if n < NT:
                                u, j = divmod(n, TPB)
                                pe.wait_ge(q_done, U)
                                for g, (h0, h1) in enumerate(GC):
                                    if n >= 2:
                                        pe.wait_ge(g_done, 2 * (n - 2) + g + 1)
                                    pe.matmul(bank[2 * (n % 2) + g][:, 0:(h1 - h0) * SK], qt[:, u, j * P:(j + 1) * P],
                                              kbd_c[:, u, h0:h1, :].rearrange("p h k -> p (h k)"),
                                              start=True, stop=True).then_inc(s_raw, 1)
                            if 1 <= n <= NT:
                                m = n - 1
                                u = m // TPB
                                pe.wait_ge(pm_done, m + 1)
                                for g in range(2):
                                    if m:
                                        pe.wait_ge(pt_done, 2 * (m - 1) + g + 1)
                                    for c in range(4 * g, min(4 * g + 4, CC)):
                                        r = chunk_rows(c, HC)
                                        t = pe.transpose(bank[4 + g][0:r, (c % 4) * P:(c % 4 + 1) * P],
                                                         pr[:, m % 2, c * P:c * P + r], ident[:])
                                    t.then_inc(pt_raw, 1)
                                if m:
                                    pe.wait_ge(att_done, m)
                                for c in range(CC):
                                    r, h0 = chunk_rows(c, HC), chunk_head(c, HC)
                                    pe.wait_ge(pt_done, 2 * m + c // 4 + 1)
                                    mm = pe.matmul(bank[6][:, h0 * DC:(h0 + WIN) * DC], pt[0:r, c, :],
                                                   vbd_c[0:r, u, c, :, :].rearrange("p w d -> p (w d)"),
                                                   start=(c == 0), stop=True, skip_group_check=True)
                                mm.then_inc(o_raw, 1)
                            if n >= 2:
                                m = n - 2
                                pe.wait_ge(att_done, m + 1)
                                if m:
                                    pe.wait_ge(attt_done, m)
                                    pe.wait_ge(r_done, m)
                                pe.transpose(bank[7][:, 0:P], att[:, m % 2, :], ident[:]).then_inc(attt_raw, 1)
                                pe.wait_ge(attt_done, m + 1)
                                pe.matmul(bank[7][:, P:2 * P], attt[:, m % 2, :], wc["p"][:], start=True,
                                          stop=True).then_inc(r_raw, 1)

                    @block.scalar
                    def _(act):
                        for u in range(U):
                            act.wait_ge(xnt_raw, u + 1)
                            act.activation(xt[:, u, :], bank[2 * u][:], ACT.Copy).then_inc(xnt_done, 1)
                        for u in range(U):
                            act.wait_ge(q_raw, u + 1)
                            act.activation(qt[:, u, :], bank[2 * u + 1][:], ACT.Copy).then_inc(q_done, 1)
                        for n in range(NT + 2):
                            if 1 <= n <= NT:
                                m = n - 1
                                if m:
                                    act.wait_ge(o_raw, m)
                                act.wait_ge(pt_raw, 2 * m + 1)
                                act.activation(pt[:, 0:4, :], bank[4][:].rearrange("p (c q) -> p c q", q=P),
                                               ACT.Copy).then_inc(pt_done, 1)
                                act.wait_ge(pt_raw, 2 * m + 2)
                                r = chunk_rows(CC - 1, HC)
                                act.activation(pt[0:r, 4, :], bank[5][0:r, 0:P], ACT.Copy).then_inc(pt_done, 1)
                            if n >= 2:
                                m = n - 2
                                act.wait_ge(attt_raw, m + 1)
                                if m >= 2:
                                    act.wait_ge(r_raw, m - 1)
                                act.activation(attt[:, m % 2, :], bank[7][:, 0:P], ACT.Copy).then_inc(attt_done, 1)
                            if n < NT:
                                act.wait_ge(sh_done, n + 1)
                                act.activation(sh[:, n % 2, 0:WC_], sh[:, n % 2, 0:WC_], ACT.Exp,
                                               scale=DC ** -0.5).then_inc(exp_done, 1)

            with ExitStack() as quant:
                xbf = sb("xbf", [P, NT, D], BF16, scope=quant)
                xq = sb("xq", [P, NT, D], BF16, scope=quant)
                xqt = sb("xqt", [P, U, S], BF16, scope=quant)
                fo = sb("fo", [P, NT, D], BF16, scope=quant)
                qf = [sb(f"qf{i}", [P, NT * D], scope=quant) for i in range(3)]
                with stage("v_chain", "var_ready", "rstd_ready", "xbf_done", "xq_done", "xqt_raw", "xqt_done", "f_raw",
                           "x_done", "stored") as (block, sems):
                    (v_chain, var_ready, rstd_ready, xbf_done, xq_done, xqt_raw, xqt_done, f_raw, x_done, stored) = sems

                    @block.vector
                    def _(dve):
                        v = Chain(dve, v_chain)
                        for u in range(U):
                            dve_stats(dve, v, u, x, var_ready)
                        for u in range(U):
                            dve_normalize(dve, u, x, xbf, rstd_ready, xbf_done)
                        dve.wait_ge(xbf_done, NT)
                        v.do(dve.tensor_scalar(qf[0][:], xbf[:].rearrange("p n d -> p (n d)"), rscale[:, 0:1], None,
                                               ALU.mult))
                        v.sync()
                        quantise(dve, v, qf, xq[:].rearrange("p n d -> p (n d)"), NT * D, xq_done)
                        for u in range(U):
                            sl = slice(TPB * u, TPB * (u + 1))
                            dve.wait_ge(f_raw, u + 1)
                            v.do(dve.tensor_scalar(fo[:, sl, :], bank[2 + u][:].rearrange("p (j d) -> p j d", d=D),
                                                   sprod[:, 0:1], None, ALU.mult))
                            v.sync()
                            v.do(dve.tensor_tensor(fo[:, sl, :], fo[:, sl, :], fbias[:].unsqueeze(1).broadcast_to(
                                [P, TPB, D]), ALU.add))
                            v.sync()
                            dve.scalar_tensor_tensor(out=x[:, sl, :], in0=fo[:, sl, :], scalar=tg[:, 3:4],
                                                     in1=x[:, sl, :], op0=ALU.mult, op1=ALU.add).then_inc(x_done, 1)

                    @block.gpsimd
                    def _(pool):
                        for u in range(U):
                            pool_rstd(pool, u, var_ready, rstd_ready)

                    @block.tensor
                    def _(pe):
                        pe.wait_ge(xq_done, 1)
                        for u in range(U):
                            for j in range(TPB):
                                t = pe.transpose(bank[u][:].bitcast(BF16)[:, j * P:(j + 1) * P], xq[:, TPB * u + j, :],
                                                 ident_bf[:])
                            t.then_inc(xqt_raw, 1)
                        for u in range(U):
                            pe.wait_ge(xqt_done, u + 1)
                            for j in range(TPB):
                                mm = pe.matmul(bank[2 + u][:, j * P:(j + 1) * P], xqt[:, u, j * P:(j + 1) * P], kern_q[:],
                                               start=True, stop=True)
                            mm.then_inc(f_raw, 1)

                    @block.scalar
                    def _(act):
                        for u in range(U):
                            act.wait_ge(xqt_raw, u + 1)
                            act.activation(xqt[:, u, :], bank[u][:].bitcast(BF16)[:, 0:S], ACT.Copy).then_inc(xqt_done, 1)

                    @block.sync
                    def _(sp):
                        dst = out[bass.ds(pair, 1)].rearrange("o (u j p) d -> o u p j d", p=P, u=U)
                        for u in range(U):
                            sp.wait_ge(x_done, u + 1)
                            sp.dma_start(dst[:, u].rearrange("o p j d -> p (o j) d"),
                                         x[:, TPB * u:TPB * (u + 1), :]).then_inc(stored, 16)
                        sp.wait_ge(stored, 16 * U)


def constants():
    f = np.float32
    c = {"c_ident": np.eye(P, dtype=f)}
    p = np.arange(P)
    c["c_headmask_a"] = (p[:, None] // DA == np.arange(HA)).astype(f)
    c["c_headmask_c"] = (p[:, None] // DC == np.arange(HC)).astype(f)
    for name, heads, chunks in (("c_vmask_a", HA, CA), ("c_vmask_c", HC, CC)):
        m = np.zeros((P, chunks, WIN), f)
        for k in range(chunks):
            r = np.arange(chunk_rows(k, heads))
            m[r, k, (P * k + r) // SK - chunk_head(k, heads)] = 1
        c[name] = m
    half = np.arange(0, DH, 2, dtype=f)
    inv = (f(1.0) / np.power(f(10000.0), half / f(DH))).astype(f)
    t = np.arange(S, dtype=f)
    ang = (t[None, :] * inv[:, None]).astype(f)
    power = ((t - S // 2) / f(W // 2)).astype(f)
    basis = ((half + f(0.4 * DH)) / f(1.4 * DH)).astype(f)
    scale = np.power(basis[:, None], power[None, :]).astype(f)
    tile = lambda m: np.concatenate([m, m, m, m])
    sign = np.where(p % DH < DH // 2, -1, 1).astype(f)[:, None]
    cos, sin, scale = tile(np.cos(ang)), tile(np.sin(ang)) * sign, tile(scale)
    c["c_rot"] = np.stack([cos * scale, sin * scale, cos / scale, sin / scale], 1).astype(f)
    i = p[:, None] % W
    slot = p[None, :]
    even = p[:, None] < W
    key = np.where(even, np.where(slot < W, slot, slot - 2 * W), np.where(slot < W, slot - W, slot - W))
    ok = (key <= i) & (key >= i - W)
    first = ok & ~(even & (slot >= W))
    c["c_band"] = np.stack([np.where(ok, 0, NEG), np.where(first, 0, NEG)], 1).astype(f)
    c["c_headones"] = (p[:, None] // DH == np.arange(2)).astype(f)
    c["c_headsel"] = np.repeat(np.eye(HB, dtype=f), DH, 1).reshape(HB, 4, P)
    sh = np.zeros((P, 2, P), f)
    sh[p[:-1], 0, p[1:]] = 1
    sh[P - 1, 1, 0] = 1
    c["c_shift"] = sh
    return c


def layout(i):
    a = constants()
    n = B // U
    a["x"] = i["x"].reshape(n, U * S, D)
    a["tmat"] = i["fside_BxSxS2_0"].reshape(n, U * S, SK)
    a["ctxt"] = i["ctx_1024"].reshape(n, U, SK, D).transpose(0, 3, 1, 2)
    m = i["mask_BxS2_bf0"].reshape(n, U, SK)
    a["mrow"] = m.reshape(n, U, SK)
    flat = m[:, :, np.arange(CA * P) % SK].reshape(n, U, CA, P)
    a["mflat"] = flat.transpose(0, 3, 1, 2)
    for k, w in (("q", "Wq"), ("k", "Wk"), ("v", "Wv"), ("o", "Wo")):
        a["wa_" + k] = i["L0_xattn_" + w]
    for k, w in (("q", "Wq"), ("k", "Wk"), ("v", "Wv"), ("p", "Wp")):
        a["wc_" + k] = i["L1_xattn_" + w].T
    a["wa1"], a["wa2"] = i["L0_xattn_W1"], i["L0_xattn_W2"]
    x0 = lambda k: i["L0_xattn_" + k]
    a["cols_a"] = np.stack([x0("bq"), x0("bk"), x0("bv"), x0("ln1_g"), x0("ln1_b")], 1)
    a["b1_a"] = x0("b1").reshape(FF // P, P).T
    a["rows"] = np.stack([x0("bo"), x0("ln1_g"), x0("ln1_b"), x0("b2"), x0("ln2_g"), x0("ln2_b"), i["L1_xattn_bp"]])
    a["gates"] = np.concatenate([i["g_xattn"], i["g_ffn"]])
    a["kern"] = i["L1_ffn_kernel"]
    a["fscale"] = np.concatenate([i["L1_ffn_input_scale"], i["L1_ffn_kernel_scale"]])
    a["fbias"] = i["L1_ffn_bias"]
    f = lambda k: i["L0_ffn_" + k]
    a["wqkv"], a["wo_b"], a["w1_b"], a["w2_b"], a["row_b"] = f("wqkv"), f("wo"), f("w1"), f("w2"), f("b2")
    d = np.arange(P) % DH
    swap = (d + DH // 2) % DH
    pad = np.zeros((DEPTH, 3 * P - HID), f("b1").dtype)
    b1 = [np.concatenate([f("b1")[:, k * HID:(k + 1) * HID], pad], 1).reshape(DEPTH, 3, P).transpose(0, 2, 1)
          for k in range(2)]
    a["cols_b"] = np.concatenate([np.stack([f("q_scale")[:, d], f("q_scale")[:, swap], f("k_scale")[:, d],
                                            f("k_scale")[:, swap], f("ln_g"), f("ln_b")], 2), *b1], 2)
    return {k: np.ascontiguousarray(v) for k, v in a.items()}


def kernel(**inputs):
    import concourse.bacc as bacc
    from concourse.bass_utils import run_bass_kernel_spmd

    nc = bacc.Bacc("TRN2", target_bir_lowering=False, num_devices=1)
    arrays = layout({k: np.asarray(v) for k, v in inputs.items()})
    aps = {k: nc.dram_tensor(f"in_{k}", v.shape, mybir.dt.from_np(v.dtype), kind="ExternalInput").ap()
           for k, v in arrays.items()}
    out = nc.dram_tensor("out_0", (B // U, U * S, D), F32, kind="ExternalOutput").ap()
    flamingo_kernel(nc, aps, out)
    r = run_bass_kernel_spmd(nc, [{f"in_{k}": v for k, v in arrays.items()}], core_ids=[0])
    return r.results[0]["out_0"].reshape(B, S, D)
```

```python
from contextlib import ExitStack, contextmanager

import numpy as np

import concourse.bass as bass
from concourse import mybir

F32 = mybir.dt.float32
BF16 = mybir.dt.bfloat16
U8 = mybir.dt.uint8
U32 = mybir.dt.uint32
I32 = mybir.dt.int32
ALU = mybir.AluOpType
ACT = mybir.ActivationFunctionType
AX = mybir.AxisListType

P = 128
D = 128
B, S, SK = 4, 512, 77
U = 2
LP, LT, LO = 2, 3, 4
TPB = S // P
NT = U * TPB
EPS = 1e-5
NEG = -1e30

HA, DA = 16, 8
HC, DC = 8, 16
CA = -(-HA * SK // P)
CC = -(-HC * SK // P)
WIN = 3
GA = [(0, 6), (6, 12), (12, 16)]
GC = [(0, 4), (4, 8)]
FF = 512

DEPTH, HB, DH, W = 2, 8, 64, 64
INNER = HB * DH
HID = 341
HCH = [(0, 128), (128, 128), (256, 85)]
PAD = W


def chunk_rows(c, heads):
    return min(P, heads * SK - P * c)


def chunk_head(c, heads):
    return min(P * c // SK, heads - WIN)


class Chain:

    def __init__(self, eng, sem):
        self.eng, self.sem, self.n = eng, sem, 0

    def do(self, ins):
        ins.then_inc(self.sem, 1)
        self.n += 1
        return self.n

    def sync(self):
        self.eng.wait_ge(self.sem, self.n)


def quantise(dve, v, q, dst, n, ready=None):
    t, m, r = (b[:, 0:n] for b in q)
    v.do(dve.tensor_scalar(m.bitcast(U32), t.bitcast(U32), 0x7F800000, None, ALU.bitwise_and))
    v.sync()
    v.do(dve.tensor_scalar(m, m, 2.0 ** -6, 1.5 * 2.0 ** 20, ALU.max, ALU.mult))
    v.sync()
    v.do(dve.tensor_tensor(r, t, m, ALU.add))
    v.sync()
    v.do(dve.tensor_tensor(r, r, m, ALU.subtract))
    v.sync()
    v.do(dve.tensor_scalar(t.bitcast(U32), r.bitcast(U32), 0x7FFFFFFF, None, ALU.bitwise_and))
    v.sync()
    v.do(dve.tensor_scalar(t, t, 448.0, 448.0, ALU.max, ALU.subtract))
    v.sync()
    v.do(dve.tensor_scalar(t, t, 3e38, 0.0, ALU.mult, ALU.mult))
    v.sync()
    ins = dve.tensor_tensor(dst, r, t, ALU.add)
    v.do(ins) if ready is None else ins.then_inc(ready, 1)


def flamingo_kernel(nc, a, out):
    with ExitStack() as ctx:
        def sb(name, shape, dt=F32, scope=ctx):
            return scope.enter_context(nc.sbuf_tensor(name, shape, dt))

        bank = [ctx.enter_context(nc.psum_tensor(f"bank{i}", [P, 512], F32)) for i in range(8)]

        ident = sb("ident", [P, P])
        ident_bf = sb("ident_bf", [P, P], BF16)
        headmask_a = sb("headmask_a", [P, HA])
        headmask_c = sb("headmask_c", [P, HC])
        vmask_a = sb("vmask_a", [P, CA, WIN])
        vmask_c = sb("vmask_c", [P, CC, WIN])
        rot = sb("rot", [P, TPB, 4, DH])
        band = sb("band", [P, 2, P], BF16)
        shift = sb("shift", [P, 2, P])
        minus_half = sb("minus_half", [P, TPB])
        ones_bf = sb("ones_bf", [1, P], BF16)

        wa = {k: sb(f"wa_{k}", [P, D]) for k in ("q", "k", "v", "o")}
        wc = {k: sb(f"wc_{k}", [P, D]) for k in ("q", "k", "v", "p")}
        wa1 = sb("wa1", [P, FF])
        wa2 = sb("wa2", [P, FF // P, D])
        cols_a = sb("cols_a", [P, 5])
        b1_a = sb("b1_a", [P, FF // P])
        rows = sb("rows", [P, 7, D])
        gates = sb("gates", [P, 4])
        tg = sb("tg", [P, 4])
        gated_rows = sb("gated_rows", [P, 3, D])
        kern = sb("kern", [P, D], BF16)
        kern_q = sb("kern_q", [P, D], BF16)
        fscale = sb("fscale", [P, 2])
        rscale = sb("rscale", [P, 2])
        sprod = sb("sprod", [P, 1])
        fbias = sb("fbias", [P, D], BF16)

        x = sb("x", [P, NT, D])
        xn = sb("xn", [P, NT, D])
        y = sb("y", [P, NT, D])
        tmat = sb("tmat", [P, NT, SK])
        ctxt = sb("ctxt", [P, U, SK])
        mflat = sb("mflat", [P, U, CA], U8)
        mrow = sb("mrow", [1, U, SK], U8)
        keep = sb("keep", [P, U, CA])
        mrow_bf = sb("mrow_bf", [1, U, SK], BF16)
        kt_a = sb("kt_a", [P, U, SK])
        kt_c = sb("kt_c", [P, U, SK])
        kbd_c = sb("kbd_c", [P, U, HC, SK])
        kmask = sb("kmask", [P, U, CA, WIN])
        vbd_a = sb("vbd_a", [P, U, CA, WIN, DA + 1])
        vbd_c = sb("vbd_c", [P, U, CC, WIN, DC])

        st = sb("st", [P, NT, 2, 6])
        mv = sb("mv", [P, NT, 2])
        rstd = sb("rstd", [P, NT])

        xt = sb("xt", [P, U, S])
        qt = sb("qt", [P, U, S])
        mx = sb("mx", [P, 2, HA])
        den = sb("den", [P, 2, HA])
        rd = sb("rd", [P, 2, HA])
        att = sb("att", [P, 2, D])
        attt = sb("attt", [P, 2, D])
        base = sb("base", [P, NT, D])

        wqkv = sb("wqkv", [P, 3 * INNER])
        wo_b = sb("wo_b", [P, INNER // P, D])
        w1_b = sb("w1_b", [P, 2 * HID])
        w2_b = sb("w2_b", [P, 3, D])
        srow = sb("srow", [P, 4, DH])
        cols_b = sb("cols_b", [P, 8])
        row_b = sb("row_b", [P, D])
        ht = sb("ht", [P, U, PAD + S + 1])
        rn = sb("rn", [P, NT, 2, HB])
        nb = sb("nb", [P, 2, HB])
        qsc = sb("qsc", [P, NT, HB])


        @contextmanager
        def stage(*names):
            with ExitStack() as c:
                sems = [c.enter_context(nc.semaphore(n)) for n in names]
                with nc.Block() as block:
                    yield block, sems
                nums = [s.num for s in sems]
                nc.all_engine_barrier(sems_to_clear=range(min(nums), max(nums) + 1))

        def dve_stats(dve, v, u, src, var_ready, src2=None):
            for j in range(TPB):
                n = TPB * u + j
                if src2 is None:
                    v.do(dve.bn_stats(st[:, n, 0, :], src[:, n, :]))
                else:
                    v.do(dve.bn_stats(st[:, n, 0, :], src[:, n, 0:64]))
                    v.do(dve.bn_stats(st[:, n, 1, :], src2(j)))
            v.sync()
            for j in range(TPB):
                n = TPB * u + j
                v.do(dve.bn_aggr(mv[:, n, :], st[:, n, 0, :] if src2 is None
                                 else st[:, n, :, :].rearrange("p a b -> p (a b)")))
            v.sync()
            dve.tensor_scalar(rstd[:, TPB * u:TPB * u + TPB], mv[:, TPB * u:TPB * u + TPB, 1], EPS, None,
                              ALU.add).then_inc(var_ready, 1)

        def pool_rstd(pool, u, var_ready, rstd_ready):
            pool.wait_ge(var_ready, u + 1)
            r = rstd[:, TPB * u:TPB * u + TPB]
            pool.tensor_tensor(r, r, minus_half[:, 0:TPB], ALU.pow).then_inc(rstd_ready, 1)

        def dve_normalize(dve, u, src, dst, rstd_ready, done=None, halves=None):
            dve.wait_ge(rstd_ready, u + 1)
            for j in range(TPB):
                n = TPB * u + j
                m, r = mv[:, n, 0:1], rstd[:, n:n + 1]
                if halves is None:
                    ins = dve.tensor_scalar(dst[:, n, :], src[:, n, :], m, r, ALU.subtract, ALU.mult)
                else:
                    dve.tensor_scalar(dst[:, n, 0:64], src[:, n, 0:64], m, r, ALU.subtract, ALU.mult)
                    ins = dve.tensor_scalar(dst[:, n, 64:128], halves(j), m, r, ALU.subtract, ALU.mult)
                if done is not None:
                    ins.then_inc(done, 1)

        with ExitStack() as once:
            band_f = sb("band_f", [P, 2, P], scope=once)
            qf = [sb(f"qf{i}k", [P, D], scope=once) for i in range(3)]
            with stage("loaded", "v_chain", "tanh_done") as (block, sems):
                loaded, v_chain, tanh_done = sems
                loads = [(ident, a["c_ident"]), (headmask_a, a["c_headmask_a"]), (headmask_c, a["c_headmask_c"]),
                         (vmask_a, a["c_vmask_a"]), (vmask_c, a["c_vmask_c"]), (rot, a["c_rot"]),
                         (band_f, a["c_band"]), (wqkv, a["wqkv"][0]), (shift, a["c_shift"]),
                         (wa["q"], a["wa_q"]), (wa["k"], a["wa_k"]), (wa["v"], a["wa_v"]), (wa["o"], a["wa_o"]),
                         (wc["q"], a["wc_q"]), (wc["k"], a["wc_k"]), (wc["v"], a["wc_v"]), (wc["p"], a["wc_p"]),
                         (wa1, a["wa1"]), (wa2, a["wa2"].rearrange("(c p) d -> p c d", p=P)),
                         (cols_a, a["cols_a"]), (b1_a, a["b1_a"]), (kern, a["kern"]),
                         (rows, a["rows"].partition_broadcast(P)), (gates, a["gates"].partition_broadcast(P)),
                         (srow, a["srow_b"][0].partition_broadcast(P)),
                         (fscale, a["fscale"].partition_broadcast(P)), (fbias, a["fbias"].partition_broadcast(P))]
                NL = 16 * len(loads)

                @block.sync
                def _(sp):
                    for dst, src in loads:
                        sp.dma_start(dst[:], src).then_inc(loaded, 16)

                @block.scalar
                def _(act):
                    act.wait_ge(loaded, NL)
                    act.activation(tg[:], gates[:], ACT.Tanh).then_inc(tanh_done, 1)
                    act.activation(ident_bf[:], ident[:], ACT.Copy)
                    act.activation(band[:], band_f[:], ACT.Copy)

                @block.gpsimd
                def _(pool):
                    pool.memset(minus_half[:], -0.5)
                    pool.memset(ones_bf[:], 1.0)
                    pool.memset(ht[:], 0.0)

                @block.vector
                def _(dve):
                    v = Chain(dve, v_chain)
                    dve.wait_ge(loaded, NL)
                    dve.wait_ge(tanh_done, 1)
                    for i, (r, g) in enumerate(((4, 0), (5, 0), (6, 1))):
                        v.do(dve.tensor_scalar(gated_rows[:, i, :], rows[:, r, :], tg[:, g:g + 1], None, ALU.mult))
                    v.do(dve.tensor_tensor(sprod[:], fscale[:, 0:1], fscale[:, 1:2], ALU.mult))
                    v.do(dve.reciprocal(rscale[:], fscale[:]))
                    v.sync()
                    v.do(dve.tensor_scalar(qf[0][:], kern[:], rscale[:, 1:2], None, ALU.mult))
                    v.sync()
                    quantise(dve, v, qf, kern_q[:], D)

        with nc.Fori(0, B // U) as pair:
            with ExitStack() as cross_a:
                kbd_a = sb("kbd_a", [P, U, HA, SK], scope=cross_a)
                rep = sb("rep", [P, U, CA * P], scope=cross_a)
                sh = sb("sh", [P, 2, HA * SK], scope=cross_a)
                pr = sb("pr", [P, 3, HA * SK], scope=cross_a)
                pt = sb("pt", [P, CA, P], scope=cross_a)
                with stage("loaded", "kt_raw", "kt_done", "rep_done", "v_raw", "v_chain", "var_ready", "rstd_ready", "xn_done",
                           "xnt_raw", "xnt_done", "q_raw") as (block, sems):
                    (loaded, kt_raw, kt_done, rep_done, v_raw, v_chain, var_ready, rstd_ready, xn_done,
                     xnt_raw, xnt_done, q_raw) = sems

                    @block.sync
                    def _(sp):
                        pr_ = bass.ds(pair, 1)
                        sp.dma_start(x[:], a["x"][pr_].rearrange("o (n p) d -> p (o n) d", p=P)).then_inc(loaded, 16)
                        sp.dma_start(ctxt[:], a["ctxt"][pr_].rearrange("o p u k -> p (o u) k")).then_inc(loaded, 16)
                        sp.dma_start(mflat[:], a["mflat"][pr_].rearrange("o p u k -> p (o u) k")).then_inc(loaded, 16)
                        sp.dma_start(mrow[:], a["mrow"][pr_]).then_inc(loaded, 16)
                        sp.dma_start(tmat[:], a["tmat"][pr_].rearrange("o (n p) d -> p (o n) d", p=P)).then_inc(loaded, 16)

                    @block.tensor
                    def _(pe):
                        pe.wait_ge(loaded, 80)
                        c = ctxt[:].rearrange("p u k -> p (u k)")
                        pe.matmul(bank[0][:, 0:U * SK], wa["k"][:], c, start=True, stop=True).then_inc(kt_raw, 1)
                        pe.matmul(bank[1][:, 0:U * SK], wc["k"][:], c, start=True, stop=True).then_inc(kt_raw, 1)
                        for u in range(U):
                            pe.wait_ge(rep_done, u + 1)
                            for k in range(CA):
                                h0 = chunk_head(k, HA)
                                w = WIN * DA
                                mm = pe.matmul(bank[2 + u][:, k * w:(k + 1) * w], rep[:, u, k * P:(k + 1) * P],
                                               wa["v"][:, h0 * DA:h0 * DA + w], start=True, stop=True)
                            for k in range(CC):
                                h0 = chunk_head(k, HC)
                                w = WIN * DC
                                mm = pe.matmul(bank[4 + u][:, k * w:(k + 1) * w], rep[:, u, k * P:(k + 1) * P],
                                               wc["v"][:, h0 * DC:h0 * DC + w], start=True, stop=True)
                            mm.then_inc(v_raw, 1)
                        for u in range(U):
                            pe.wait_ge(xn_done, TPB * (u + 1))
                            for j in range(TPB):
                                t = pe.transpose(bank[6 + u][:, j * P:(j + 1) * P], xn[:, TPB * u + j, :], ident[:])
                            t.then_inc(xnt_raw, 1)
                        pe.wait_ge(kt_done, 1)
                        for u in range(U):
                            pe.wait_ge(xnt_done, u + 1)
                            pe.matmul(bank[u][:], wa["q"][:], xt[:, u, :], start=True, stop=True).then_inc(q_raw, 1)

                    @block.scalar
                    def _(act):
                        act.wait_ge(kt_raw, 2)
                        act.activation(kt_a[:].rearrange("p u k -> p (u k)"), bank[0][:, 0:U * SK], ACT.Identity,
                                       bias=cols_a[:, 1:2])
                        act.activation(kt_c[:].rearrange("p u k -> p (u k)"), bank[1][:, 0:U * SK],
                                       ACT.Copy).then_inc(kt_done, 1)
                        for u in range(U):
                            act.wait_ge(xnt_raw, u + 1)
                            act.activation(xt[:, u, :], bank[6 + u][:], ACT.Copy).then_inc(xnt_done, 1)
                        for u in range(U):
                            act.wait_ge(q_raw, u + 1)
                            act.activation(qt[:, u, :], bank[u][:], ACT.Identity, bias=cols_a[:, 0:1])

                    @block.gpsimd
                    def _(pool):
                        for u in range(U):
                            pool_rstd(pool, u, var_ready, rstd_ready)
                        for u in range(U):
                            pool.wait_ge(xn_done, TPB * (u + 1))
                            pool.tensor_tensor(base[:, TPB * u:TPB * (u + 1), :], xn[:, TPB * u:TPB * (u + 1), :],
                                               rows[:, 0:1, :].broadcast_to([P, TPB, D]), ALU.add)

                    @block.vector
                    def _(dve):
                        v = Chain(dve, v_chain)
                        dve.wait_ge(loaded, 80)
                        for u in range(U):
                            dve_stats(dve, v, u, x, var_ready)
                            full = CA * P // SK
                            dve.tensor_copy(rep[:, u, 0:full * SK].rearrange("p (r k) -> p r k", k=SK),
                                            ctxt[:, u, :].unsqueeze(1).broadcast_to([P, full, SK]))
                            dve.tensor_copy(rep[:, u, full * SK:CA * P],
                                            ctxt[:, u, 0:CA * P - full * SK]).then_inc(rep_done, 1)
                        for u in range(U):
                            dve_normalize(dve, u, x, xn, rstd_ready, xn_done)
                        v.do(dve.tensor_scalar(keep[:], mflat[:], -1.0, 1.0, ALU.mult, ALU.add))
                        v.do(dve.tensor_scalar(mrow_bf[:], mrow[:], NEG, None, ALU.mult))
                        v.sync()
                        for u in range(U):
                            v.do(dve.tensor_tensor(kmask[:, u], vmask_a[:],
                                                   keep[:, u, :].unsqueeze(2).broadcast_to([P, CA, WIN]), ALU.mult))
                        dve.wait_ge(kt_done, 1)
                        for u in range(U):
                            dve.tensor_tensor(kbd_a[:, u], kt_a[:, u, :].unsqueeze(1).broadcast_to([P, HA, SK]),
                                              headmask_a[:].unsqueeze(2).broadcast_to([P, HA, SK]), ALU.mult)
                            dve.tensor_tensor(kbd_c[:, u], kt_c[:, u, :].unsqueeze(1).broadcast_to([P, HC, SK]),
                                              headmask_c[:].unsqueeze(2).broadcast_to([P, HC, SK]), ALU.mult)
                        v.sync()
                        for u in range(U):
                            dve.wait_ge(v_raw, u + 1)
                            dve.tensor_tensor(vbd_a[:, u, :, :, 0:DA].rearrange("p c w d -> p (c w) d"),
                                              bank[2 + u][:, 0:CA * WIN * DA].rearrange("p (w d) -> p w d", d=DA),
                                              kmask[:, u].rearrange("p c w -> p (c w)").unsqueeze(2).broadcast_to(
                                                  [P, CA * WIN, DA]), ALU.mult)
                            dve.tensor_copy(vbd_a[:, u, :, :, DA], kmask[:, u])
                            dve.tensor_tensor(vbd_c[:, u].rearrange("p c w d -> p (c w) d"),
                                              bank[4 + u][:, 0:CC * WIN * DC].rearrange("p (w d) -> p w d", d=DC),
                                              vmask_c[:].rearrange("p c w -> p (c w)").unsqueeze(2).broadcast_to(
                                                  [P, CC * WIN, DC]), ALU.mult)

                with stage("v_chain", "s_raw", "s_used", "exp_done", "pt_raw", "pt_done", "o_raw", "att_done",
                           "attt_raw", "attt_done", "r_raw", "r_done") as (block, sems):
                    (v_chain, s_raw, s_used, exp_done, pt_raw, pt_done, o_raw, att_done,
                     attt_raw, attt_done, r_raw, r_done) = sems
                    PTG = [(0, 4), (4, 8), (8, 10)]

                    @block.vector
                    def _(dve):
                        v = Chain(dve, v_chain)
                        for n in range(NT + LO):
                            if n >= LO:
                                m = n - LO
                                dve.wait_ge(r_raw, m + 1)
                                dve.tensor_tensor(base[:, m, :], bank[6][:, 2 * P:3 * P], base[:, m, :],
                                                  ALU.add).then_inc(r_done, 1)
                            if n < NT:
                                k = n % 2
                                s3 = sh[:, k, :].rearrange("p (h k) -> p h k", k=SK)
                                for g, (h0, h1) in enumerate(GA):
                                    dve.wait_ge(s_raw, 3 * n + g + 1)
                                    src = bank[g][:, 0:(h1 - h0) * SK].rearrange("p (h k) -> p h k", k=SK)
                                    v.do(dve.tensor_reduce(mx[:, k, h0:h1], src, AX.X, ALU.max))
                                v.sync()
                                if n >= 2:
                                    dve.wait_ge(exp_done, n - 1)
                                for g, (h0, h1) in enumerate(GA):
                                    src = bank[g][:, 0:(h1 - h0) * SK].rearrange("p (h k) -> p h k", k=SK)
                                    dve.tensor_tensor(s3[:, h0:h1, :], src,
                                                      mx[:, k, h0:h1].unsqueeze(2).broadcast_to([P, h1 - h0, SK]),
                                                      ALU.subtract).then_inc(s_used, 1)
                            if LP <= n < NT + LP:
                                m = n - LP
                                k = m % 2
                                o3 = bank[6][:, 0:HA * (DA + 1)].rearrange("p (h d) -> p h d", d=DA + 1)
                                dve.wait_ge(o_raw, m + 1)
                                v.do(dve.reciprocal(rd[:, k, :], o3[:, :, DA]))
                                v.sync()
                                if m >= 2:
                                    dve.wait_ge(attt_raw, m - 1)
                                dve.tensor_tensor(att[:, k, :].rearrange("p (h d) -> p h d", d=DA), o3[:, :, 0:DA],
                                                  rd[:, k, :].unsqueeze(2).broadcast_to([P, HA, DA]),
                                                  ALU.mult).then_inc(att_done, 1)

                    @block.tensor
                    def _(pe):
                        for n in range(NT + LO):
                            if n >= LO:
                                m = n - LO
                                pe.wait_ge(attt_done, m + 1)
                                pe.wait_ge(att_done, min(m + 2, NT))
                                if m:
                                    pe.wait_ge(r_done, m)
                                pe.matmul(bank[6][:, 2 * P:3 * P], attt[:, m % 2, :], wa["o"][:], start=True,
                                          stop=True).then_inc(r_raw, 1)
                            if n < NT:
                                u, j = divmod(n, TPB)
                                for g, (h0, h1) in enumerate(GA):
                                    if n:
                                        pe.wait_ge(s_used, 3 * (n - 1) + g + 1)
                                    w = (h1 - h0) * SK
                                    pe.matmul(bank[g][:, 0:w], ones_bf[:],
                                              mrow_bf[:, u:u + 1, :].broadcast_to([1, h1 - h0, SK]), start=True, stop=False)
                                    pe.matmul(bank[g][:, 0:w], qt[:, u, j * P:(j + 1) * P],
                                              kbd_a[:, u, h0:h1, :].rearrange("p h k -> p (h k)"),
                                              start=False, stop=True).then_inc(s_raw, 1)
                            if LT <= n < NT + LT:
                                m = n - LT
                                pe.wait_ge(att_done, m + 1)
                                if m:
                                    pe.wait_ge(attt_done, m)
                                pe.transpose(bank[7][:, 0:P], att[:, m % 2, :], ident[:]).then_inc(attt_raw, 1)
                            if LP <= n < NT + LP:
                                m = n - LP
                                u = m // TPB
                                pe.wait_ge(exp_done, m + 1)
                                for g, (c0, c1) in enumerate(PTG):
                                    if m:
                                        pe.wait_ge(pt_done, 3 * (m - 1) + g + 1)
                                    for c in range(c0, c1):
                                        r = chunk_rows(c, HA)
                                        t = pe.transpose(bank[3 + g][0:r, (c - c0) * P:(c - c0 + 1) * P],
                                                         pr[:, m % 3, c * P:c * P + r], ident[:])
                                    t.then_inc(pt_raw, 1)
                                if m:
                                    pe.wait_ge(att_done, m)
                                if n >= LO:
                                    pe.wait_ge(r_done, n - LO + 1)
                                for c in range(CA):
                                    r, h0 = chunk_rows(c, HA), chunk_head(c, HA)
                                    pe.wait_ge(pt_done, 3 * m + min(c // 4, 2) + 1)
                                    mm = pe.matmul(bank[6][:, h0 * (DA + 1):(h0 + WIN) * (DA + 1)], pt[0:r, c, :],
                                                   vbd_a[0:r, u, c, :, :].rearrange("p w d -> p (w d)"),
                                                   start=(c == 0), stop=True, skip_group_check=True)
                                mm.then_inc(o_raw, 1)

                    @block.scalar
                    def _(act):
                        for n in range(NT + LT):
                            if n >= LT:
                                m = n - LT
                                act.wait_ge(attt_raw, m + 1)
                                if m >= 2:
                                    act.wait_ge(r_raw, m - 1)
                                act.activation(attt[:, m % 2, :], bank[7][:, 0:P], ACT.Identity,
                                               bias=cols_a[:, 2:3]).then_inc(attt_done, 1)
                            if LP <= n < NT + LP:
                                m = n - LP
                                if m:
                                    act.wait_ge(o_raw, m)
                                for g, (c0, c1) in enumerate(PTG):
                                    act.wait_ge(pt_raw, 3 * m + g + 1)
                                    if g < 2:
                                        act.activation(pt[:, c0:c1, :], bank[3 + g][:].rearrange("p (c q) -> p c q", q=P),
                                                       ACT.Copy).then_inc(pt_done, 1)
                                    else:
                                        r = chunk_rows(CA - 1, HA)
                                        act.activation(pt[:, 8, :], bank[5][:, 0:P], ACT.Copy)
                                        act.activation(pt[0:r, 9, :], bank[5][0:r, P:2 * P], ACT.Copy).then_inc(pt_done, 1)
                            if n < NT:
                                act.wait_ge(s_used, 3 * (n + 1))
                                if n >= 3:
                                    act.wait_ge(pt_raw, 3 * (n - 2))
                                act.activation(pr[:, n % 3, :], sh[:, n % 2, :], ACT.Exp,
                                               scale=DA ** -0.5).then_inc(exp_done, 1)

            with ExitStack() as ffn:
                hidt = sb("hidt", [P, U, FF // P, S], scope=ffn)
                with stage("v_chain", "p_chain", "var1", "rstd1", "var2", "rstd2", "var3", "rstd3", "xn_done", "xnt_raw",
                           "xnt_done", "h_raw", "h_done", "f_raw", "base_done", "ln2_done", "x_done") as (block, sems):
                    (v_chain, p_chain, var1, rstd1, var2, rstd2, var3, rstd3, xn_done, xnt_raw,
                     xnt_done, h_raw, h_done, f_raw, base_done, ln2_done, x_done) = sems
                    NC = FF // P

                    @block.vector
                    def _(dve):
                        v = Chain(dve, v_chain)
                        for u in range(U):
                            dve_stats(dve, v, u, base, var1)
                        for u in range(U):
                            dve_normalize(dve, u, base, xn, rstd1, xn_done)
                        for u in range(U):
                            sl = slice(TPB * u, TPB * (u + 1))
                            dve.wait_ge(f_raw, u + 1)
                            dve.wait_ge(base_done, u + 1)
                            v.do(dve.tensor_tensor(base[:, sl, :], bank[6 + u][:].rearrange("p (j d) -> p j d", d=D),
                                                   base[:, sl, :], ALU.add))
                            v.sync()
                            dve_stats(dve, v, u, base, var2)
                        for u in range(U):
                            dve_normalize(dve, u, base, base, rstd2, ln2_done)
                        for u in range(U):
                            dve.wait_ge(x_done, u + 1)
                            dve_stats(dve, v, u, x, var3)
                        for u in range(U):
                            dve_normalize(dve, u, x, y, rstd3)

                    @block.gpsimd
                    def _(pool):
                        p = Chain(pool, p_chain)

                        def rows_op(u, dst, src, t, r, op):
                            sl = slice(TPB * u, TPB * (u + 1))
                            return pool.tensor_tensor(dst[:, sl, :], src[:, sl, :],
                                                      t[:, r:r + 1, :].broadcast_to([P, TPB, D]), op)

                        for u in range(U):
                            pool_rstd(pool, u, var1, rstd1)
                        for u in range(U):
                            pool.wait_ge(xn_done, TPB * (u + 1))
                            p.do(rows_op(u, base, xn, rows, 1, ALU.mult))
                            p.sync()
                            p.do(rows_op(u, base, base, rows, 2, ALU.add))
                            p.sync()
                            rows_op(u, base, base, rows, 3, ALU.add).then_inc(base_done, 1)
                        for u in range(U):
                            pool_rstd(pool, u, var2, rstd2)
                        for u in range(U):
                            sl = slice(TPB * u, TPB * (u + 1))
                            pool.wait_ge(ln2_done, TPB * (u + 1))
                            p.do(rows_op(u, base, base, gated_rows, 0, ALU.mult))
                            p.do(rows_op(u, x, x, gated_rows, 1, ALU.add))
                            p.sync()
                            pool.tensor_tensor(x[:, sl, :], x[:, sl, :], base[:, sl, :], ALU.add).then_inc(x_done, 1)
                        for u in range(U):
                            pool_rstd(pool, u, var3, rstd3)

                    @block.tensor
                    def _(pe):
                        for u in range(U):
                            for j in range(TPB):
                                n = TPB * u + j
                                pe.wait_ge(xn_done, n + 1)
                                t = pe.transpose(bank[u][:, j * P:(j + 1) * P], xn[:, n, :], ident[:])
                            t.then_inc(xnt_raw, 1)
                        for u in range(U):
                            pe.wait_ge(xnt_done, u + 1)
                            for c in range(NC):
                                if u:
                                    pe.wait_ge(h_done, NC * (u - 1) + c + 1)
                                pe.matmul(bank[2 + c][:], wa1[:, c * P:(c + 1) * P], xt[:, u, :], start=True,
                                          stop=True).then_inc(h_raw, 1)
                        for u in range(U):
                            pe.wait_ge(h_done, NC * (u + 1))
                            for j in range(TPB):
                                for c in range(NC):
                                    mm = pe.matmul(bank[6 + u][:, j * P:(j + 1) * P], hidt[:, u, c, j * P:(j + 1) * P],
                                                   wa2[:, c, :], start=(c == 0), stop=(c == NC - 1))
                            mm.then_inc(f_raw, 1)

                    @block.scalar
                    def _(act):
                        for u in range(U):
                            act.wait_ge(xnt_raw, u + 1)
                            act.activation(xt[:, u, :], bank[u][:], ACT.Identity, bias=cols_a[:, 4:5],
                                           scale=cols_a[:, 3:4]).then_inc(xnt_done, 1)
                        for u in range(U):
                            for c in range(NC):
                                act.wait_ge(h_raw, NC * u + c + 1)
                                act.activation(hidt[:, u, c, :], bank[2 + c][:], ACT.Gelu,
                                               bias=b1_a[:, c:c + 1]).then_inc(h_done, 1)

            with nc.Fori(0, DEPTH) as layer:
                with ExitStack() as local:
                    qtb = sb("qtb", [P, U, 4, S], scope=local)
                    ktb = sb("ktb", [P, U, 4, PAD + S], scope=local)
                    va = sb("va", [P, U, TPB, INNER], scope=local)
                    vm = sb("vm", [P, U, TPB + 1, INNER], scope=local)
                    with ExitStack() as proj:
                        rt = sb("rt", [P, TPB, 4, DH], scope=proj)
                        sq = sb("sq", [P, 2, 2, INNER], scope=proj)
                        t2 = sb("t2", [P, 2, 2, INNER], scope=proj)
                        qrot = sb("qrot", [P, 3, INNER], scope=proj)
                        krot = sb("krot", [P, 4, INNER], scope=proj)
                        n2 = sb("n2", [P, NT, 2 * HB], scope=proj)
                        nh = sb("nh", [P, 2, 2 * HB], scope=proj)
                        with stage("loaded", "v_chain", "y_raw", "ht_done", "pads_done", "rt_done", "q_raw", "k_raw", "v_raw", "sq_done",
                                   "k_prod", "q_prod", "k_sum", "q_sum", "n2_done", "rn_done", "k_normed", "qt_raw", "kt_raw",
                                   "qt_done", "kt_done", "v_done") as (block, sems):
                            (loaded, v_chain, y_raw, ht_done, pads_done, rt_done, q_raw, k_raw, v_raw, sq_done,
                             k_prod, q_prod, k_sum, q_sum, n2_done, rn_done, k_normed, qt_raw, kt_raw,
                             qt_done, kt_done, v_done) = sems
                            LQ, LK = 1, 4
                            vbank = (4, 7)

                            @block.sync
                            def _(sp):
                                l = bass.ds(layer, 1)
                                sp.dma_start(cols_b[:], a["cols_b"][l].rearrange("o p n -> (o p) n")).then_inc(loaded, 16)
                                sp.dma_start(wo_b[:], a["wo_b"][l].rearrange("o (c p) d -> p (o c) d", p=P)).then_inc(loaded, 16)
                                sp.dma_start(w1_b[:], a["w1_b"][l].rearrange("o p n -> (o p) n")).then_inc(loaded, 16)
                                sp.dma_start(w2_b[:, 0:2, :], a["w2_b"][l, 0:2 * P, :].rearrange(
                                    "o (c p) d -> p (o c) d", p=P)).then_inc(loaded, 16)
                                sp.dma_start(w2_b[0:HID - 2 * P, 2, :], a["w2_b"][l, 2 * P:HID, :].rearrange(
                                    "o p d -> p (o d)")).then_inc(loaded, 16)
                                sp.dma_start(row_b[:], a["row_b"][l].partition_broadcast(P).rearrange(
                                    "p o d -> p (o d)")).then_inc(loaded, 16)
                                sp.wait_ge(loaded, 96)

                            @block.tensor
                            def _(pe):
                                for u in range(U):
                                    for j in range(TPB):
                                        t = pe.transpose(bank[vbank[u]][:, j * P:(j + 1) * P], y[:, TPB * u + j, :], ident[:])
                                    t.then_inc(y_raw, 1)
                                for n in range(NT + LK):
                                    if n < NT:
                                        u, j = divmod(n, TPB)
                                        b = n % 2
                                        h = ht[:, u, PAD + j * P:PAD + (j + 1) * P]
                                        pe.wait_ge(ht_done, u + 1)
                                        if n >= 2:
                                            pe.wait_ge(q_prod, n - 1)
                                            pe.wait_ge(sq_done, 2 * (n - 1))
                                        pe.matmul(bank[b][:], h, wqkv[:, 0:INNER], start=True, stop=True).then_inc(q_raw, 1)
                                        if n >= 2:
                                            pe.wait_ge(k_prod, n - 1)
                                        pe.matmul(bank[2 + b][:], h, wqkv[:, INNER:2 * INNER], start=True, stop=True).then_inc(k_raw, 1)
                                        if n >= 2:
                                            pe.wait_ge(v_done, n - 1)
                                        else:
                                            pe.wait_ge(ht_done, U)
                                        pe.matmul(bank[vbank[b]][:], h, wqkv[:, 2 * INNER:], start=True, stop=True).then_inc(v_raw, 1)
                                    if LQ <= n < NT + LQ:
                                        m = n - LQ
                                        pe.wait_ge(q_sum, m + 1)
                                        if m:
                                            pe.wait_ge(qt_done, m)
                                        for c in range(4):
                                            t = pe.transpose(bank[5][:, c * P:(c + 1) * P], qrot[:, m % 3, c * P:(c + 1) * P], ident[:])
                                        t.then_inc(qt_raw, 1)
                                    if n >= LK:
                                        m = n - LK
                                        pe.wait_ge(k_normed, m + 1)
                                        if m:
                                            pe.wait_ge(kt_done, m)
                                        for c in range(4):
                                            t = pe.transpose(bank[6][:, c * P:(c + 1) * P], krot[:, m % 4, c * P:(c + 1) * P], ident[:])
                                        t.then_inc(kt_raw, 1)

                            @block.scalar
                            def _(act):
                                for u in range(U):
                                    act.wait_ge(y_raw, u + 1)
                                    b = bank[vbank[u]]
                                    act.activation(ht[0:64, u, PAD:PAD + S], b[0:64, :], ACT.Copy)
                                    act.activation(ht[64:128, u, PAD + 1:PAD + S + 1], b[64:128, :], ACT.Copy).then_inc(ht_done, 1)
                                for n in range(NT + LK):
                                    if n < NT:
                                        u, j = divmod(n, TPB)
                                        b = n % 2
                                        if n >= 2:
                                            act.wait_ge(n2_done, n - 1)
                                        act.wait_ge(q_raw, n + 1)
                                        act.activation(sq[:, b, 0, :], bank[b][:], ACT.Square).then_inc(sq_done, 1)
                                        act.wait_ge(k_prod, n + 1)
                                        act.activation(sq[:, b, 1, :], bank[2 + b][:], ACT.Square).then_inc(sq_done, 1)
                                        act.wait_ge(v_raw, n + 1)
                                        bv = bank[vbank[b]]
                                        act.activation(va[:, u, j, :], bv[:], ACT.Copy)
                                        act.activation(vm[0:64, u, j, :], bv[0:64, :], ACT.Copy)
                                        act.activation(vm[64:128, u, j + 1, :], bv[64:128, :], ACT.Copy).then_inc(v_done, 1)
                                    if LQ <= n < NT + LQ:
                                        u, j = divmod(n - LQ, TPB)
                                        act.wait_ge(qt_raw, n - LQ + 1)
                                        act.activation(qtb[:, u, :, j * P:(j + 1) * P], bank[5][:].rearrange("p (c q) -> p c q", q=P),
                                                       ACT.Copy).then_inc(qt_done, 1)
                                    if n >= LK:
                                        u, j = divmod(n - LK, TPB)
                                        act.wait_ge(kt_raw, n - LK + 1)
                                        act.activation(ktb[:, u, :, PAD + j * P:PAD + (j + 1) * P],
                                                       bank[6][:].rearrange("p (c q) -> p c q", q=P), ACT.Copy).then_inc(kt_done, 1)

                            @block.vector
                            def _(dve):
                                v = Chain(dve, v_chain)
                                dve.tensor_tensor(rt[:], rot[:], srow[:].unsqueeze(1).broadcast_to([P, TPB, 4, DH]),
                                                  ALU.mult).then_inc(rt_done, 1)
                                dve.wait_ge(rt_done, 1)

                                def products(src, dst, tmp, j, i):
                                    dve.tensor_tensor(dst.rearrange("p (h d) -> p h d", d=DH), src.rearrange("p (h d) -> p h d", d=DH),
                                                      rt[:, j, i:i + 1, :].broadcast_to([P, HB, DH]), ALU.mult)
                                    return dve.tensor_tensor(
                                        tmp.rearrange("p (h a e) -> p h a e", a=2, e=DH // 2),
                                        src.rearrange("p (h a e) -> p h a e", a=2, e=DH // 2)[:, :, ::-1, :],
                                        rt[:, j, i + 1:i + 2, :].rearrange("p i (a e) -> p i a e", a=2).broadcast_to(
                                            [P, HB, 2, DH // 2]), ALU.mult)

                                for n in range(NT):
                                    j = n % TPB
                                    b = n % 2
                                    dve.wait_ge(k_raw, n + 1)
                                    if n >= 2:
                                        dve.wait_ge(k_sum, n - 1)
                                    if n >= 4:
                                        dve.wait_ge(kt_raw, n - 3)
                                    products(bank[2 + b][:], krot[:, n % 4, :], t2[:, b, 1, :], j, 2).then_inc(k_prod, 1)
                                    dve.wait_ge(sq_done, 2 * n + 1)
                                    if n >= 2:
                                        dve.wait_ge(q_sum, n - 1)
                                    if n >= 3:
                                        dve.wait_ge(qt_raw, n - 2)
                                    products(bank[b][:], qrot[:, n % 3, :], t2[:, b, 0, :], j, 0).then_inc(q_prod, 1)
                                    dve.wait_ge(sq_done, 2 * n + 2)
                                    dve.tensor_reduce(n2[:, n, :], sq[:, b].rearrange("p k (h d) -> p (k h) d", d=DH), AX.X,
                                                      ALU.add).then_inc(n2_done, 1)
                                    if b == 0:
                                        continue
                                    dve.wait_ge(n2_done, n + 1)
                                    e = n2[:, n - 1:n + 1, :]
                                    w = rn[:, n - 1:n + 1].rearrange("p n k h -> p n (k h)")
                                    v.do(dve.tensor_scalar(e, e, 1e-24, None, ALU.max))
                                    v.sync()
                                    v.do(dve.tensor_scalar(w.bitcast(I32), e.bitcast(I32), -0.5, 1597463007.0, ALU.mult, ALU.add))
                                    v.sync()
                                    for i in range(3):
                                        v.do(dve.scalar_tensor_tensor(out=nh[:], in0=w, scalar=-0.5, in1=w, op0=ALU.mult, op1=ALU.mult))
                                        v.sync()
                                        v.do(dve.tensor_tensor(nh[:], nh[:], e, ALU.mult))
                                        v.sync()
                                        ins = dve.scalar_tensor_tensor(out=w, in0=nh[:], scalar=1.5, in1=w, op0=ALU.add, op1=ALU.mult)
                                        if i < 2:
                                            v.do(ins)
                                            v.sync()
                                    ins.then_inc(rn_done, 1)

                            @block.gpsimd
                            def _(pool):
                                pool.memset(ktb[:, :, :, 0:PAD], 0.0).then_inc(pads_done, 1)
                                pool.wait_ge(pads_done, 1)
                                pool.memset(vm[64:128, :, 0, :], 0.0).then_inc(pads_done, 1)
                                pool.wait_ge(pads_done, 2)
                                for n in range(NT + 2):
                                    if n < NT:
                                        pool.wait_ge(k_prod, n + 1)
                                        pool.tensor_tensor(krot[:, n % 4, :], krot[:, n % 4, :], t2[:, n % 2, 1, :],
                                                           ALU.add).then_inc(k_sum, 1)
                                        pool.wait_ge(q_prod, n + 1)
                                        pool.tensor_tensor(qrot[:, n % 3, :], qrot[:, n % 3, :], t2[:, n % 2, 0, :],
                                                           ALU.add).then_inc(q_sum, 1)
                                    if n >= 2:
                                        m = n - 2
                                        pool.wait_ge(rn_done, m // 2 + 1)
                                        pool.wait_ge(k_sum, m + 1)
                                        k3 = krot[:, m % 4, :].rearrange("p (h d) -> p h d", d=DH)
                                        pool.tensor_tensor(k3, k3, rn[:, m, 1, :].unsqueeze(2).broadcast_to([P, HB, DH]),
                                                           ALU.mult).then_inc(k_normed, 1)
                    pb = sb("pb", [P, 3, HB, P], scope=local)
                    ptb = sb("ptb", [P, HB, P], scope=local)
                    on = xt
                    ont = qt
                    with stage("loaded", "v_chain", "qsc_done", "s_raw", "s_used", "nb_done", "exp_done", "pt_raw", "pt_done", "o_raw",
                               "on_done", "ont_raw", "ont_done", "r_raw", "r_done") as (block, sems):
                        (loaded, v_chain, qsc_done, s_raw, s_used, nb_done, exp_done, pt_raw, pt_done, o_raw,
                         on_done, ont_raw, ont_done, r_raw, r_done) = sems

                        @block.sync
                        def _(sp):
                            sp.dma_start(wqkv[:], a["wqkv"][bass.ds(layer + 1, 1)].rearrange(
                                "o p n -> (o p) n")).then_inc(loaded, 16)
                            sp.dma_start(srow[:], a["srow_b"][bass.ds(layer + 1, 1)].partition_broadcast(P).rearrange(
                                "p o i d -> p (o i) d")).then_inc(loaded, 16)
                            sp.wait_ge(loaded, 32)

                        @block.tensor
                        def _(pe):
                            for n in range(NT + 2):
                                if n < NT:
                                    u, j = divmod(n, TPB)
                                    if n >= 2:
                                        pe.wait_ge(exp_done, HB * (n - 1))
                                    for g in range(2):
                                        pe.matmul(bank[2 * (n % 2) + g][:], ident_bf[:], band[:, 0 if j else 1, :].unsqueeze(1).broadcast_to(
                                            [P, 4, P]), start=True, stop=True, skip_group_check=True)
                                    q0 = j * P
                                    for c in range(4):
                                        for g in range(2):
                                            bk, r, col = bank[2 * (n % 2) + g], slice(64 * g, 64 * g + 64), slice(c * P, (c + 1) * P)
                                            keys = ktb[r, u, c, q0:q0 + P].rearrange("p (a e) -> p a e", a=2)[:, ::-1, :]
                                            pe.matmul(bk[0:64, col], qtb[r, u, c, q0:q0 + 64], keys, start=False, stop=True,
                                                      skip_group_check=True)
                                            mm = pe.matmul(bk[64:128, col], qtb[r, u, c, q0 + 64:q0 + P],
                                                           ktb[r, u, c, PAD + q0:PAD + q0 + P], start=False, stop=True,
                                                           skip_group_check=True)
                                            if c == 3:
                                                mm.then_inc(s_raw, 1)
                                if 1 <= n <= NT:
                                    m = n - 1
                                    u, j = divmod(m, TPB)
                                    for g in range(2):
                                        pe.wait_ge(exp_done, HB * m + 4 * g + 4)
                                        if m:
                                            pe.wait_ge(pt_done, 2 * (m - 1) + g + 1)
                                        for c in range(4):
                                            t = pe.transpose(bank[4 + g][:, c * P:(c + 1) * P], pb[:, m % 2, 2 * c + g, :],
                                                             ident[:])
                                        t.then_inc(pt_raw, 1)
                                    if m:
                                        pe.wait_ge(on_done, m)
                                    for i in range(HB):
                                        h = 2 * (i % 4) + i // 4
                                        pe.wait_ge(pt_done, 2 * m + i // 4 + 1)
                                        hs = slice(h * DH, (h + 1) * DH)
                                        pe.matmul(bank[6][0:64, hs], ptb[:, i, 0:64], vm[:, u, j, hs], start=True, stop=True)
                                        mm = pe.matmul(bank[6][64:128, hs], ptb[:, i, 64:128], va[:, u, j, hs], start=True,
                                                       stop=True)
                                    mm.then_inc(o_raw, 1)
                                if n >= 2:
                                    m = n - 2
                                    pe.wait_ge(on_done, m + 1)
                                    if m:
                                        pe.wait_ge(ont_done, m)
                                        pe.wait_ge(r_done, m)
                                    for c in range(4):
                                        t = pe.transpose(bank[7][:, c * P:(c + 1) * P], on[:, m % 2, c * P:(c + 1) * P], ident[:])
                                    t.then_inc(ont_raw, 1)
                                    pe.wait_ge(ont_done, m + 1)
                                    for c in range(4):
                                        mm = pe.matmul(bank[7][:, 0:P], ont[:, m % 2, c * P:(c + 1) * P], wo_b[:, c, :],
                                                       start=(c == 0), stop=(c == 3))
                                    mm.then_inc(r_raw, 1)

                        @block.scalar
                        def _(act):
                            for n in range(NT + 2):
                                if 1 <= n <= NT:
                                    m = n - 1
                                    if m:
                                        act.wait_ge(o_raw, m)
                                    for g in range(2):
                                        act.wait_ge(pt_raw, 2 * m + g + 1)
                                        act.activation(ptb[:, 4 * g:4 * g + 4, :], bank[4 + g][:].rearrange(
                                            "p (h q) -> p h q", q=P), ACT.Copy).then_inc(pt_done, 1)
                                if n >= 2:
                                    m = n - 2
                                    act.wait_ge(ont_raw, m + 1)
                                    if m >= 2:
                                        act.wait_ge(r_raw, m - 1)
                                    act.activation(ont[:, m % 2, :], bank[7][:], ACT.Copy).then_inc(ont_done, 1)
                                if n < NT:
                                    k = n % 2
                                    act.wait_ge(qsc_done, 1)
                                    if n >= 2:
                                        act.wait_ge(pt_raw, 2 * (n - 1))
                                        act.wait_ge(on_done, n - 1)
                                    for i in range(HB):
                                        h = 2 * (i % 4) + i // 4
                                        if i % 4 == 0:
                                            act.wait_ge(nb_done, 2 * n + i // 4 + 1)
                                        act.activation(pb[:, k, h, :], bank[2 * k + i // 4][:, (i % 4) * P:(i % 4 + 1) * P],
                                                       ACT.Exp, bias=nb[:, k, h:h + 1], scale=qsc[:, n, h:h + 1],
                                                       accum_out=den[:, k, h:h + 1]).then_inc(exp_done, 1)

                        @block.vector
                        def _(dve):
                            v = Chain(dve, v_chain)
                            dve.tensor_scalar(qsc[:], rn[:, :, 0, :], 8.0, None,
                                              ALU.mult).then_inc(qsc_done, 1)
                            dve.wait_ge(qsc_done, 1)
                            for n in range(NT + 2):
                                if n < NT:
                                    k = n % 2
                                    for g in range(2):
                                        hs = slice(g, HB, 2)
                                        dve.wait_ge(s_raw, 2 * n + g + 1)
                                        v.do(dve.tensor_reduce(mx[:, k, hs], bank[2 * k + g][:].rearrange(
                                            "p (h q) -> p h q", q=P), AX.X, ALU.max))
                                        v.sync()
                                        if n >= 2:
                                            dve.wait_ge(exp_done, HB * (n - 1))
                                        dve.scalar_tensor_tensor(out=nb[:, k, hs], in0=mx[:, k, hs], scalar=-1.0,
                                                                 in1=qsc[:, n, hs], op0=ALU.mult,
                                                                 op1=ALU.mult).then_inc(nb_done, 1)
                                if 1 <= n <= NT:
                                    m = n - 1
                                    k = m % 2
                                    dve.wait_ge(o_raw, m + 1)
                                    dve.wait_ge(exp_done, HB * (m + 1))
                                    v.do(dve.reciprocal(rd[:, k, 0:HB], den[:, k, 0:HB]))
                                    v.sync()
                                    if m >= 2:
                                        dve.wait_ge(ont_raw, m - 1)
                                    dve.tensor_tensor(on[:, k, :].rearrange("p (h d) -> p h d", d=DH),
                                                      bank[6][:].rearrange("p (h d) -> p h d", d=DH),
                                                      rd[:, k, 0:HB].unsqueeze(2).broadcast_to([P, HB, DH]),
                                                      ALU.mult).then_inc(on_done, 1)
                                if n >= 2:
                                    m = n - 2
                                    dve.wait_ge(r_raw, m + 1)
                                    dve.tensor_tensor(y[:, m, :], bank[7][:, 0:P], y[:, m, :], ALU.add).then_inc(r_done, 1)

                with ExitStack() as ffn:
                    hidt = sb("hidt_b", [P, U, len(HCH), S], scope=ffn)
                    gel = sb("gel", [P, 2, S], scope=ffn)
                    with stage("v_chain", "sh_raw", "var_ready", "rstd_ready", "xn_done", "xnt_raw", "xnt_done", "g_raw",
                               "gel_done", "hid_done", "f_raw", "base_done") as (block, sems):
                        (v_chain, sh_raw, var_ready, rstd_ready, xn_done, xnt_raw, xnt_done, g_raw,
                         gel_done, hid_done, f_raw, base_done) = sems
                        NH = len(HCH)

                        @block.tensor
                        def _(pe):
                            for u in range(U):
                                t0 = TPB * u
                                pe.matmul(bank[u][:, 0:TPB * 64], shift[:, 0, :], y[:, t0:t0 + TPB, 64:128], start=True,
                                          stop=True, skip_group_check=True)
                                pe.matmul(bank[u][:, 64:TPB * 64], shift[:, 1, :], y[:, t0:t0 + TPB - 1, 64:128],
                                          start=False, stop=True, skip_group_check=True).then_inc(sh_raw, 1)
                            for u in range(U):
                                pe.wait_ge(xn_done, TPB * (u + 1))
                                for j in range(TPB):
                                    t = pe.transpose(bank[u][:, j * P:(j + 1) * P], xn[:, TPB * u + j, :], ident[:])
                                t.then_inc(xnt_raw, 1)
                            for u in range(U):
                                pe.wait_ge(xnt_done, u + 1)
                                for c, (h0, w) in enumerate(HCH):
                                    g = NH * u + c
                                    if g >= 2:
                                        pe.wait_ge(hid_done, g - 1)
                                    b0 = 2 + 2 * (g % 2)
                                    pe.matmul(bank[b0][0:w, :], w1_b[:, h0:h0 + w], xt[:, u, :], start=True, stop=True)
                                    pe.matmul(bank[b0 + 1][0:w, :], w1_b[:, HID + h0:HID + h0 + w], xt[:, u, :], start=True,
                                              stop=True).then_inc(g_raw, 1)
                            for u in range(U):
                                pe.wait_ge(hid_done, NH * (u + 1))
                                for j in range(TPB):
                                    for c, (h0, w) in enumerate(HCH):
                                        mm = pe.matmul(bank[6 + u][:, j * P:(j + 1) * P], hidt[0:w, u, c, j * P:(j + 1) * P],
                                                       w2_b[0:w, c, :], start=(c == 0), stop=(c == NH - 1))
                                mm.then_inc(f_raw, 1)

                        @block.scalar
                        def _(act):
                            for u in range(U):
                                act.wait_ge(xnt_raw, u + 1)
                                act.activation(xt[:, u, :], bank[u][:], ACT.Identity, bias=cols_b[:, 1:2],
                                               scale=cols_b[:, 0:1]).then_inc(xnt_done, 1)
                            for u in range(U):
                                for c, (h0, w) in enumerate(HCH):
                                    g = NH * u + c
                                    act.wait_ge(g_raw, g + 1)
                                    if g >= 2:
                                        act.wait_ge(hid_done, g - 1)
                                    act.activation(gel[0:w, g % 2, :], bank[3 + 2 * (g % 2)][0:w, :], ACT.Gelu,
                                                   bias=cols_b[0:w, 5 + c:6 + c]).then_inc(gel_done, 1)

                        @block.gpsimd
                        def _(pool):
                            for u in range(U):
                                pool_rstd(pool, u, var_ready, rstd_ready)
                            for u in range(U):
                                sl = slice(TPB * u, TPB * (u + 1))
                                pool.tensor_tensor(base[:, sl, :], y[:, sl, :], row_b[:].unsqueeze(1).broadcast_to([P, TPB, D]),
                                                   ALU.add).then_inc(base_done, 1)

                        @block.vector
                        def _(dve):
                            v = Chain(dve, v_chain)
                            for u in range(U):
                                dve.wait_ge(sh_raw, u + 1)
                                dve_stats(dve, v, u, y, var_ready, lambda j: bank[u][:, 64 * j:64 * j + 64])
                            for u in range(U):
                                dve_normalize(dve, u, y, xn, rstd_ready, xn_done, lambda j: bank[u][:, 64 * j:64 * j + 64])
                            for u in range(U):
                                for c, (h0, w) in enumerate(HCH):
                                    g = NH * u + c
                                    dve.wait_ge(gel_done, g + 1)
                                    dve.scalar_tensor_tensor(out=hidt[0:w, u, c, :], in0=bank[2 + 2 * (g % 2)][0:w, :],
                                                             scalar=cols_b[0:w, 2 + c:3 + c], in1=gel[0:w, g % 2, :],
                                                             op0=ALU.add, op1=ALU.mult).then_inc(hid_done, 1)
                            for u in range(U):
                                sl = slice(TPB * u, TPB * (u + 1))
                                dve.wait_ge(f_raw, u + 1)
                                dve.wait_ge(base_done, u + 1)
                                dve.tensor_tensor(y[:, sl, :], bank[6 + u][:].rearrange("p (j d) -> p j d", d=D),
                                                  base[:, sl, :], ALU.add)

            with ExitStack() as cross_c:
                sh = sb("sh_c", [P, 2, HA * SK], scope=cross_c)
                gt = sb("gt_c", [P, 2, HC * SK], scope=cross_c)
                pr = sb("pr_c", [P, 2, HA * SK], scope=cross_c)
                pt = sb("pt_c", [P, CA, P], scope=cross_c)
                with stage("v_chain", "var_ready", "rstd_ready", "xn_done", "xnt_raw", "xnt_done", "q_raw", "q_done",
                           "s_raw", "g_done", "sh_done", "exp_done", "pm_done", "pt_raw", "pt_done", "o_raw", "att_done",
                           "attt_raw", "attt_done", "r_raw", "r_done", "x_stats", "base_done") as (block, sems):
                    (v_chain, var_ready, rstd_ready, xn_done, xnt_raw, xnt_done, q_raw, q_done,
                     s_raw, g_done, sh_done, exp_done, pm_done, pt_raw, pt_done, o_raw, att_done,
                     attt_raw, attt_done, r_raw, r_done, x_stats, base_done) = sems
                    WC_ = HC * SK

                    @block.vector
                    def _(dve):
                        v = Chain(dve, v_chain)
                        v.do(dve.scalar_tensor_tensor(out=x[:], in0=y[:], scalar=tg[:, 2:3], in1=x[:], op0=ALU.mult,
                                                      op1=ALU.add))
                        v.sync()
                        for u in range(U):
                            dve_stats(dve, v, u, x, var_ready)
                        for u in range(U):
                            dve_normalize(dve, u, x, xn, rstd_ready, xn_done)
                        for n in range(NT + LO):
                            if n >= LO:
                                m = n - LO
                                dve.wait_ge(r_raw, m + 1)
                                dve.wait_ge(base_done, U)
                                dve.scalar_tensor_tensor(out=x[:, m, :], in0=bank[6][:, 2 * P:3 * P], scalar=tg[:, 1:2],
                                                         in1=base[:, m, :], op0=ALU.mult, op1=ALU.add).then_inc(r_done, 1)
                            if n < NT:
                                k = n % 2
                                g3 = gt[:, k, :].rearrange("p (h k) -> p h k", k=SK)
                                if n >= 2:
                                    dve.wait_ge(pm_done, n - 1)
                                for g, (h0, h1) in enumerate(GC):
                                    dve.wait_ge(s_raw, 2 * n + g + 1)
                                    src = bank[2 * k + g][:, 0:(h1 - h0) * SK].rearrange("p (h k) -> p h k", k=SK)
                                    dve.tensor_tensor(g3[:, h0:h1, :], src, tmat[:, n:n + 1, :].broadcast_to(
                                        [P, h1 - h0, SK]), ALU.mult).then_inc(g_done, 1)
                                dve.wait_ge(g_done, 2 * (n + 1))
                                v.do(dve.tensor_reduce(mx[:, k, 0:HC], g3, AX.X, ALU.max))
                                v.sync()
                                if n >= 2:
                                    dve.wait_ge(exp_done, n - 1)
                                dve.tensor_tensor(sh[:, k, 0:WC_].rearrange("p (h k) -> p h k", k=SK), g3,
                                                  mx[:, k, 0:HC].unsqueeze(2).broadcast_to([P, HC, SK]),
                                                  ALU.subtract).then_inc(sh_done, 1)
                            if 1 <= n <= NT:
                                m = n - 1
                                k = m % 2
                                dve.wait_ge(exp_done, m + 1)
                                v.do(dve.tensor_reduce(den[:, k, 0:HC], sh[:, k, 0:WC_].rearrange("p (h k) -> p h k", k=SK),
                                                       AX.X, ALU.add))
                                if m >= 2:
                                    dve.wait_ge(pt_raw, 2 * (m - 1))
                                dve.scalar_tensor_tensor(out=pr[:, k, 0:WC_], in0=gt[:, k, :], scalar=0.0,
                                                         in1=sh[:, k, 0:WC_], op0=ALU.not_equal,
                                                         op1=ALU.mult).then_inc(pm_done, 1)
                                v.sync()
                                v.do(dve.reciprocal(rd[:, k, 0:HC], den[:, k, 0:HC]))
                            if LP <= n < NT + LP:
                                m = n - LP
                                k = m % 2
                                dve.wait_ge(o_raw, m + 1)
                                v.sync()
                                if m >= 2:
                                    dve.wait_ge(attt_raw, m - 1)
                                dve.tensor_tensor(att[:, k, :].rearrange("p (h d) -> p h d", d=DC),
                                                  bank[6][:, 0:P].rearrange("p (h d) -> p h d", d=DC),
                                                  rd[:, k, 0:HC].unsqueeze(2).broadcast_to([P, HC, DC]),
                                                  ALU.mult).then_inc(att_done, 1)

                    @block.gpsimd
                    def _(pool):
                        for u in range(U):
                            pool_rstd(pool, u, var_ready, rstd_ready)
                        for u in range(U):
                            sl = slice(TPB * u, TPB * (u + 1))
                            pool.tensor_tensor(base[:, sl, :], x[:, sl, :], gated_rows[:, 2:3, :].broadcast_to([P, TPB, D]),
                                               ALU.add).then_inc(base_done, 1)

                    @block.tensor
                    def _(pe):
                        for u in range(U):
                            for j in range(TPB):
                                n = TPB * u + j
                                pe.wait_ge(xn_done, n + 1)
                                t = pe.transpose(bank[2 * u][:, j * P:(j + 1) * P], xn[:, n, :], ident[:])
                            t.then_inc(xnt_raw, 1)
                        for u in range(U):
                            pe.wait_ge(xnt_done, u + 1)
                            pe.matmul(bank[2 * u + 1][:], wc["q"][:], xt[:, u, :], start=True, stop=True).then_inc(q_raw, 1)
                        for n in range(NT + LO):
                            if n >= LO:
                                m = n - LO
                                pe.wait_ge(attt_done, m + 1)
                                pe.wait_ge(att_done, min(m + 2, NT))
                                if m:
                                    pe.wait_ge(r_done, m)
                                pe.matmul(bank[6][:, 2 * P:3 * P], attt[:, m % 2, :], wc["p"][:], start=True,
                                          stop=True).then_inc(r_raw, 1)
                            if n < NT:
                                u, j = divmod(n, TPB)
                                pe.wait_ge(q_done, U)
                                for g, (h0, h1) in enumerate(GC):
                                    if n >= 2:
                                        pe.wait_ge(g_done, 2 * (n - 2) + g + 1)
                                    pe.matmul(bank[2 * (n % 2) + g][:, 0:(h1 - h0) * SK], qt[:, u, j * P:(j + 1) * P],
                                              kbd_c[:, u, h0:h1, :].rearrange("p h k -> p (h k)"),
                                              start=True, stop=True).then_inc(s_raw, 1)
                            if LT <= n < NT + LT:
                                m = n - LT
                                pe.wait_ge(att_done, m + 1)
                                if m:
                                    pe.wait_ge(attt_done, m)
                                pe.transpose(bank[7][:, 0:P], att[:, m % 2, :], ident[:]).then_inc(attt_raw, 1)
                            if LP <= n < NT + LP:
                                m = n - LP
                                u = m // TPB
                                pe.wait_ge(pm_done, m + 1)
                                for g in range(2):
                                    if m:
                                        pe.wait_ge(pt_done, 2 * (m - 1) + g + 1)
                                    for c in range(4 * g, min(4 * g + 4, CC)):
                                        r = chunk_rows(c, HC)
                                        t = pe.transpose(bank[4 + g][0:r, (c % 4) * P:(c % 4 + 1) * P],
                                                         pr[:, m % 2, c * P:c * P + r], ident[:])
                                    t.then_inc(pt_raw, 1)
                                if m:
                                    pe.wait_ge(att_done, m)
                                if n >= LO:
                                    pe.wait_ge(r_done, n - LO + 1)
                                for c in range(CC):
                                    r, h0 = chunk_rows(c, HC), chunk_head(c, HC)
                                    pe.wait_ge(pt_done, 2 * m + c // 4 + 1)
                                    mm = pe.matmul(bank[6][:, h0 * DC:(h0 + WIN) * DC], pt[0:r, c, :],
                                                   vbd_c[0:r, u, c, :, :].rearrange("p w d -> p (w d)"),
                                                   start=(c == 0), stop=True, skip_group_check=True)
                                mm.then_inc(o_raw, 1)

                    @block.scalar
                    def _(act):
                        for u in range(U):
                            act.wait_ge(xnt_raw, u + 1)
                            act.activation(xt[:, u, :], bank[2 * u][:], ACT.Copy).then_inc(xnt_done, 1)
                        for u in range(U):
                            act.wait_ge(q_raw, u + 1)
                            act.activation(qt[:, u, :], bank[2 * u + 1][:], ACT.Copy).then_inc(q_done, 1)
                        for n in range(NT + LT):
                            if n >= LT:
                                m = n - LT
                                act.wait_ge(attt_raw, m + 1)
                                if m >= 2:
                                    act.wait_ge(r_raw, m - 1)
                                act.activation(attt[:, m % 2, :], bank[7][:, 0:P], ACT.Copy).then_inc(attt_done, 1)
                            if LP <= n < NT + LP:
                                m = n - LP
                                if m:
                                    act.wait_ge(o_raw, m)
                                act.wait_ge(pt_raw, 2 * m + 1)
                                act.activation(pt[:, 0:4, :], bank[4][:].rearrange("p (c q) -> p c q", q=P),
                                               ACT.Copy).then_inc(pt_done, 1)
                                act.wait_ge(pt_raw, 2 * m + 2)
                                r = chunk_rows(CC - 1, HC)
                                act.activation(pt[0:r, 4, :], bank[5][0:r, 0:P], ACT.Copy).then_inc(pt_done, 1)
                            if n < NT:
                                act.wait_ge(sh_done, n + 1)
                                act.activation(sh[:, n % 2, 0:WC_], sh[:, n % 2, 0:WC_], ACT.Exp,
                                               scale=DC ** -0.5).then_inc(exp_done, 1)

            with ExitStack() as quant:
                xbf = sb("xbf", [P, NT, D], BF16, scope=quant)
                xq = sb("xq", [P, NT, D], BF16, scope=quant)
                xqt = sb("xqt", [P, U, S], BF16, scope=quant)
                fo = sb("fo", [P, NT, D], BF16, scope=quant)
                qf = [sb(f"qf{i}", [P, NT * D], scope=quant) for i in range(3)]
                with stage("v_chain", "var_ready", "rstd_ready", "xbf_done", "xq_done", "xqt_raw", "xqt_done", "f_raw",
                           "x_done", "stored") as (block, sems):
                    (v_chain, var_ready, rstd_ready, xbf_done, xq_done, xqt_raw, xqt_done, f_raw, x_done, stored) = sems

                    @block.vector
                    def _(dve):
                        v = Chain(dve, v_chain)
                        for u in range(U):
                            dve_stats(dve, v, u, x, var_ready)
                        for u in range(U):
                            dve_normalize(dve, u, x, xbf, rstd_ready, xbf_done)
                        dve.wait_ge(xbf_done, NT)
                        v.do(dve.tensor_scalar(qf[0][:], xbf[:].rearrange("p n d -> p (n d)"), rscale[:, 0:1], None,
                                               ALU.mult))
                        v.sync()
                        quantise(dve, v, qf, xq[:].rearrange("p n d -> p (n d)"), NT * D, xq_done)
                        for u in range(U):
                            sl = slice(TPB * u, TPB * (u + 1))
                            dve.wait_ge(f_raw, u + 1)
                            v.do(dve.tensor_scalar(fo[:, sl, :], bank[2 + u][:].rearrange("p (j d) -> p j d", d=D),
                                                   sprod[:, 0:1], None, ALU.mult))
                            v.sync()
                            v.do(dve.tensor_tensor(fo[:, sl, :], fo[:, sl, :], fbias[:].unsqueeze(1).broadcast_to(
                                [P, TPB, D]), ALU.add))
                            v.sync()
                            dve.scalar_tensor_tensor(out=x[:, sl, :], in0=fo[:, sl, :], scalar=tg[:, 3:4],
                                                     in1=x[:, sl, :], op0=ALU.mult, op1=ALU.add).then_inc(x_done, 1)

                    @block.gpsimd
                    def _(pool):
                        for u in range(U):
                            pool_rstd(pool, u, var_ready, rstd_ready)

                    @block.tensor
                    def _(pe):
                        pe.wait_ge(xq_done, 1)
                        for u in range(U):
                            for j in range(TPB):
                                t = pe.transpose(bank[u][:].bitcast(BF16)[:, j * P:(j + 1) * P], xq[:, TPB * u + j, :],
                                                 ident_bf[:])
                            t.then_inc(xqt_raw, 1)
                        for u in range(U):
                            pe.wait_ge(xqt_done, u + 1)
                            for j in range(TPB):
                                mm = pe.matmul(bank[2 + u][:, j * P:(j + 1) * P], xqt[:, u, j * P:(j + 1) * P], kern_q[:],
                                               start=True, stop=True)
                            mm.then_inc(f_raw, 1)

                    @block.scalar
                    def _(act):
                        for u in range(U):
                            act.wait_ge(xqt_raw, u + 1)
                            act.activation(xqt[:, u, :], bank[u][:].bitcast(BF16)[:, 0:S], ACT.Copy).then_inc(xqt_done, 1)

                    @block.sync
                    def _(sp):
                        dst = out[bass.ds(pair, 1)].rearrange("o (u j p) d -> o u p j d", p=P, u=U)
                        for u in range(U):
                            sp.wait_ge(x_done, u + 1)
                            sp.dma_start(dst[:, u].rearrange("o p j d -> p (o j) d"),
                                         x[:, TPB * u:TPB * (u + 1), :]).then_inc(stored, 16)
                        sp.wait_ge(stored, 16 * U)


def constants():
    f = np.float32
    c = {"c_ident": np.eye(P, dtype=f)}
    p = np.arange(P)
    c["c_headmask_a"] = (p[:, None] // DA == np.arange(HA)).astype(f)
    c["c_headmask_c"] = (p[:, None] // DC == np.arange(HC)).astype(f)
    for name, heads, chunks in (("c_vmask_a", HA, CA), ("c_vmask_c", HC, CC)):
        m = np.zeros((P, chunks, WIN), f)
        for k in range(chunks):
            r = np.arange(chunk_rows(k, heads))
            m[r, k, (P * k + r) // SK - chunk_head(k, heads)] = 1
        c[name] = m
    half = np.arange(0, DH, 2, dtype=f)
    inv = (f(1.0) / np.power(f(10000.0), half / f(DH))).astype(f)
    t = np.arange(S, dtype=f)
    ang = (t[None, :] * inv[:, None]).astype(f)
    power = ((t - S // 2) / f(W // 2)).astype(f)
    basis = ((half + f(0.4 * DH)) / f(1.4 * DH)).astype(f)
    scale = np.power(basis[:, None], power[None, :]).astype(f)
    sign = np.where(np.arange(DH) < DH // 2, -1, 1).astype(f)
    rows = lambda m: np.concatenate([m, m]).T
    cos, sin, scale = rows(np.cos(ang)), rows(np.sin(ang)) * sign, rows(scale)
    tables = np.stack([cos * scale, sin * scale, cos / scale, sin / scale], 1).astype(f)
    c["c_rot"] = tables.reshape(TPB, P, 4, DH).transpose(1, 0, 2, 3)
    i = p[:, None] % W
    slot = p[None, :]
    even = p[:, None] < W
    key = np.where(even, np.where(slot < W, slot, slot - 2 * W), np.where(slot < W, slot - W, slot - W))
    ok = (key <= i) & (key >= i - W)
    first = ok & ~(even & (slot >= W))
    c["c_band"] = np.stack([np.where(ok, 0, NEG), np.where(first, 0, NEG)], 1).astype(f)
    sh = np.zeros((P, 2, P), f)
    sh[p[:-1], 0, p[1:]] = 1
    sh[P - 1, 1, 0] = 1
    c["c_shift"] = sh
    return c


def layout(i):
    a = constants()
    n = B // U
    a["x"] = i["x"].reshape(n, U * S, D)
    a["tmat"] = i["fside_BxSxS2_0"].reshape(n, U * S, SK)
    a["ctxt"] = i["ctx_1024"].reshape(n, U, SK, D).transpose(0, 3, 1, 2)
    m = i["mask_BxS2_bf0"].reshape(n, U, SK)
    a["mrow"] = m.reshape(n, U, SK)
    flat = m[:, :, np.arange(CA * P) % SK].reshape(n, U, CA, P)
    a["mflat"] = flat.transpose(0, 3, 1, 2)
    for k, w in (("q", "Wq"), ("k", "Wk"), ("v", "Wv"), ("o", "Wo")):
        a["wa_" + k] = i["L0_xattn_" + w]
    for k, w in (("q", "Wq"), ("k", "Wk"), ("v", "Wv"), ("p", "Wp")):
        a["wc_" + k] = i["L1_xattn_" + w].T
    a["wa1"], a["wa2"] = i["L0_xattn_W1"], i["L0_xattn_W2"]
    x0 = lambda k: i["L0_xattn_" + k]
    a["cols_a"] = np.stack([x0("bq"), x0("bk"), x0("bv"), x0("ln1_g"), x0("ln1_b")], 1)
    a["b1_a"] = x0("b1").reshape(FF // P, P).T
    a["rows"] = np.stack([x0("bo"), x0("ln1_g"), x0("ln1_b"), x0("b2"), x0("ln2_g"), x0("ln2_b"), i["L1_xattn_bp"]])
    a["gates"] = np.concatenate([i["g_xattn"], i["g_ffn"]])
    a["kern"] = i["L1_ffn_kernel"]
    a["fscale"] = np.concatenate([i["L1_ffn_input_scale"], i["L1_ffn_kernel_scale"]])
    a["fbias"] = i["L1_ffn_bias"]
    f = lambda k: i["L0_ffn_" + k]
    a["wqkv"], a["wo_b"], a["w1_b"], a["w2_b"], a["row_b"] = f("wqkv"), f("wo"), f("w1"), f("w2"), f("b2")
    ahead = lambda m: np.concatenate([m, m[:1]])
    a["wqkv"] = ahead(a["wqkv"])
    swap = (np.arange(DH) + DH // 2) % DH
    a["srow_b"] = ahead(np.stack([f("q_scale"), f("q_scale")[:, swap], f("k_scale"), f("k_scale")[:, swap]], 1))
    pad = np.zeros((DEPTH, 3 * P - HID), f("b1").dtype)
    b1 = [np.concatenate([f("b1")[:, k * HID:(k + 1) * HID], pad], 1).reshape(DEPTH, 3, P).transpose(0, 2, 1)
          for k in range(2)]
    a["cols_b"] = np.concatenate([np.stack([f("ln_g"), f("ln_b")], 2), *b1], 2)
    return {k: np.ascontiguousarray(v) for k, v in a.items()}


def kernel(**inputs):
    import concourse.bacc as bacc
    from concourse.bass_utils import run_bass_kernel_spmd

    nc = bacc.Bacc("TRN2", target_bir_lowering=False, num_devices=1)
    arrays = layout({k: np.asarray(v) for k, v in inputs.items()})
    aps = {k: nc.dram_tensor(f"in_{k}", v.shape, mybir.dt.from_np(v.dtype), kind="ExternalInput").ap()
           for k, v in arrays.items()}
    out = nc.dram_tensor("out_0", (B // U, U * S, D), F32, kind="ExternalOutput").ap()
    flamingo_kernel(nc, aps, out)
    r = run_bass_kernel_spmd(nc, [{f"in_{k}": v for k, v in arrays.items()}], core_ids=[0])
    return r.results[0]["out_0"].reshape(B, S, D)
```

```python
from contextlib import ExitStack, contextmanager

import numpy as np

import concourse.bass as bass
from concourse import mybir

F32 = mybir.dt.float32
BF16 = mybir.dt.bfloat16
U8 = mybir.dt.uint8
U32 = mybir.dt.uint32
I32 = mybir.dt.int32
ALU = mybir.AluOpType
ACT = mybir.ActivationFunctionType
AX = mybir.AxisListType

P = 128
D = 128
B, S, SK = 4, 512, 77
U = 2
LP, LT, LO = 2, 3, 4
TPB = S // P
NT = U * TPB
EPS = 1e-5
NEG = -1e30

HA, DA = 16, 8
HC, DC = 8, 16
CA = -(-HA * SK // P)
CC = -(-HC * SK // P)
WIN = 3
GA = [(0, 6), (6, 12), (12, 16)]
GC = [(0, 4), (4, 8)]
FF = 512

DEPTH, HB, DH, W = 2, 8, 64, 64
INNER = HB * DH
HID = 341
HCH = [(0, 128), (128, 128), (256, 85)]
PAD = W


CONSTS = dict(ident=P, headmask_a=HA, headmask_c=HC, vmask_a=CA * WIN, vmask_c=CC * WIN, shift=2 * P, band=2 * P)


def offsets(widths):
    at, o = {}, 0
    for k, w in widths.items():
        at[k], o = o, o + w
    return at


def chunk_rows(c, heads):
    return min(P, heads * SK - P * c)


def chunk_head(c, heads):
    return min(P * c // SK, heads - WIN)


class Chain:

    def __init__(self, eng, sem):
        self.eng, self.sem, self.n = eng, sem, 0

    def do(self, ins):
        ins.then_inc(self.sem, 1)
        self.n += 1
        return self.n

    def sync(self):
        self.eng.wait_ge(self.sem, self.n)


def quantise(dve, v, q, dst, n, ready=None):
    t, m, r = (b[:, 0:n] for b in q)
    v.do(dve.tensor_scalar(m.bitcast(U32), t.bitcast(U32), 0x7F800000, None, ALU.bitwise_and))
    v.sync()
    v.do(dve.tensor_scalar(m, m, 2.0 ** -6, 1.5 * 2.0 ** 20, ALU.max, ALU.mult))
    v.sync()
    v.do(dve.tensor_tensor(r, t, m, ALU.add))
    v.sync()
    v.do(dve.tensor_tensor(r, r, m, ALU.subtract))
    v.sync()
    v.do(dve.tensor_scalar(t.bitcast(U32), r.bitcast(U32), 0x7FFFFFFF, None, ALU.bitwise_and))
    v.sync()
    v.do(dve.tensor_scalar(t, t, 448.0, 448.0, ALU.max, ALU.subtract))
    v.sync()
    v.do(dve.tensor_scalar(t, t, 3e38, 0.0, ALU.mult, ALU.mult))
    v.sync()
    ins = dve.tensor_tensor(dst, r, t, ALU.add)
    v.do(ins) if ready is None else ins.then_inc(ready, 1)


def flamingo_kernel(nc, a, out):
    with ExitStack() as ctx:
        def sb(name, shape, dt=F32, scope=ctx):
            return scope.enter_context(nc.sbuf_tensor(name, shape, dt))

        bank = [ctx.enter_context(nc.psum_tensor(f"bank{i}", [P, 512], F32)) for i in range(8)]

        consts = sb("consts", [P, sum(CONSTS.values())])
        part = {k: consts[:, o:o + CONSTS[k]] for k, o in offsets(CONSTS).items()}
        ident, headmask_a, headmask_c = part["ident"], part["headmask_a"], part["headmask_c"]
        vmask_a = part["vmask_a"].rearrange("p (c w) -> p c w", w=WIN)
        vmask_c = part["vmask_c"].rearrange("p (c w) -> p c w", w=WIN)
        shift = part["shift"].rearrange("p (k q) -> p k q", k=2)
        band_f = part["band"].rearrange("p (k q) -> p k q", k=2)
        ident_bf = sb("ident_bf", [P, P], BF16)
        rot = sb("rot", [P, TPB, 4, DH])
        band = sb("band", [P, 2, P], BF16)
        minus_half = sb("minus_half", [P, TPB])
        ones_bf = sb("ones_bf", [1, P], BF16)

        w8 = sb("w8", [P, 8, D])
        wa = {k: w8[:, i, :] for i, k in enumerate("qkvo")}
        wc = {k: w8[:, 4 + i, :] for i, k in enumerate("qkvp")}
        wa1 = sb("wa1", [P, FF])
        wa2 = sb("wa2", [P, FF // P, D])
        cols = sb("cols", [P, 5 + FF // P])
        cols_a = cols[:, 0:5]
        b1_a = cols[:, 5:]
        vecs = sb("vecs", [P, 7 * D + 6])
        rows = vecs[:, 0:7 * D].rearrange("p (r d) -> p r d", d=D)
        gates = vecs[:, 7 * D:7 * D + 4]
        fscale = vecs[:, 7 * D + 4:]
        tg = sb("tg", [P, 4])
        gated_rows = sb("gated_rows", [P, 3, D])
        kern = sb("kern", [P, D], BF16)
        kern_q = sb("kern_q", [P, D], BF16)
        rscale = sb("rscale", [P, 2])
        sprod = sb("sprod", [P, 1])
        fbias = sb("fbias", [P, D], BF16)

        x = sb("x", [P, NT, D])
        xn = sb("xn", [P, NT, D])
        y = sb("y", [P, NT, D])
        tmat = sb("tmat", [P, NT, SK])
        ctxt = sb("ctxt", [P, U, SK])
        mflat = sb("mflat", [P, U, CA], U8)
        mrow = sb("mrow", [1, U, SK], U8)
        keep = sb("keep", [P, U, CA])
        mrow_bf = sb("mrow_bf", [1, U, SK], BF16)
        kt_a = sb("kt_a", [P, U, SK])
        kt_c = sb("kt_c", [P, U, SK])
        kbd_c = sb("kbd_c", [P, U, HC, SK])
        kmask = sb("kmask", [P, U, CA, WIN])
        vbd_a = sb("vbd_a", [P, U, CA, WIN, DA + 1])
        vbd_c = sb("vbd_c", [P, U, CC, WIN, DC])

        st = sb("st", [P, NT, 2, 6])
        mv = sb("mv", [P, NT, 2])
        rstd = sb("rstd", [P, NT])

        xt = sb("xt", [P, U, S])
        qt = sb("qt", [P, U, S])
        mx = sb("mx", [P, 2, HA])
        den = sb("den", [P, 2, HA])
        rd = sb("rd", [P, 2, HA])
        att = sb("att", [P, 2, D])
        attt = sb("attt", [P, 2, D])
        base = sb("base", [P, NT, D])

        wqkv = sb("wqkv", [P, 3 * INNER])
        wo_b = sb("wo_b", [P, INNER // P, D])
        w1_b = sb("w1_b", [P, 2 * HID])
        w2_b = sb("w2_b", [P, 3, D])
        srow = sb("srow", [P, 4, DH])
        cols_b = sb("cols_b", [P, 8])
        row_b = sb("row_b", [P, D])
        ht = sb("ht", [P, U, PAD + S + 1])
        rn = sb("rn", [P, NT, 2, HB])
        nb = sb("nb", [P, 2, HB])
        qsc = sb("qsc", [P, NT, HB])

        @contextmanager
        def stage(*names):
            with ExitStack() as c:
                sems = [c.enter_context(nc.semaphore(n)) for n in names]
                with nc.Block() as block:
                    yield block, sems
                nums = [s.num for s in sems]
                nc.all_engine_barrier(sems_to_clear=range(min(nums), max(nums) + 1))

        def dve_stats(dve, v, u, src, var_ready, src2=None):
            for j in range(TPB):
                n = TPB * u + j
                if src2 is None:
                    v.do(dve.bn_stats(st[:, n, 0, :], src[:, n, :]))
                else:
                    v.do(dve.bn_stats(st[:, n, 0, :], src[:, n, 0:64]))
                    v.do(dve.bn_stats(st[:, n, 1, :], src2(j)))
            v.sync()
            for j in range(TPB):
                n = TPB * u + j
                v.do(dve.bn_aggr(mv[:, n, :], st[:, n, 0, :] if src2 is None
                                 else st[:, n, :, :].rearrange("p a b -> p (a b)")))
            v.sync()
            dve.tensor_scalar(rstd[:, TPB * u:TPB * u + TPB], mv[:, TPB * u:TPB * u + TPB, 1], EPS, None,
                              ALU.add).then_inc(var_ready, 1)

        def pool_rstd(pool, u, var_ready, rstd_ready):
            pool.wait_ge(var_ready, u + 1)
            r = rstd[:, TPB * u:TPB * u + TPB]
            pool.tensor_tensor(r, r, minus_half[:, 0:TPB], ALU.pow).then_inc(rstd_ready, 1)

        def dve_normalize(dve, u, src, dst, rstd_ready, done=None, halves=None):
            dve.wait_ge(rstd_ready, u + 1)
            for j in range(TPB):
                n = TPB * u + j
                m, r = mv[:, n, 0:1], rstd[:, n:n + 1]
                if halves is None:
                    ins = dve.tensor_scalar(dst[:, n, :], src[:, n, :], m, r, ALU.subtract, ALU.mult)
                else:
                    dve.tensor_scalar(dst[:, n, 0:64], src[:, n, 0:64], m, r, ALU.subtract, ALU.mult)
                    ins = dve.tensor_scalar(dst[:, n, 64:128], halves(j), m, r, ALU.subtract, ALU.mult)
                if done is not None:
                    ins.then_inc(done, 1)

        def pair_loads(p):
            q = bass.ds(p, 1)
            return [(ctxt, a["ctxt"][q].rearrange("o p u k -> p (o u) k")),
                    (mflat, a["mflat"][q].rearrange("o p u k -> p (o u) k")), (mrow, a["mrow"][q]),
                    (tmat, a["tmat"][q].rearrange("o (n p) d -> p (o n) d", p=P))]

        with ExitStack() as once:
            qf = [sb(f"qf{i}k", [P, D], scope=once) for i in range(3)]
            with stage("first_loaded", "loaded", "v_chain", "tanh_done") as (block, sems):
                first_loaded, loaded, v_chain, tanh_done = sems
                first = [(vecs, a["vecs"].partition_broadcast(P)), (kern, a["kern"])]
                loads = [(consts, a["c_consts"]), (wqkv, a["wqkv"][0]), (w8, a["w8"]), (rot, a["c_rot"]), (wa1, a["wa1"]),
                         (wa2, a["wa2"].rearrange("(c p) d -> p c d", p=P)), (cols, a["cols"]),
                         (srow, a["srow_b"][0].partition_broadcast(P)), (fbias, a["fbias"].partition_broadcast(P)),
                         (x, a["x"][0].rearrange("(n p) d -> p n d", p=P)), *pair_loads(0)]
                NF, NL = 16 * len(first), 16 * len(loads)

                @block.sync
                def _(sp):
                    for dst, src in first:
                        sp.dma_start(dst[:], src).then_inc(first_loaded, 16)
                    for dst, src in loads[0::2]:
                        sp.dma_start(dst[:], src).then_inc(loaded, 16)

                @block.scalar
                def _(act):
                    for dst, src in loads[1::2]:
                        act.dma_start(dst[:], src).then_inc(loaded, 16)
                    act.wait_ge(first_loaded, NF)
                    act.activation(tg[:], gates[:], ACT.Tanh).then_inc(tanh_done, 1)
                    act.wait_ge(loaded, NL)
                    act.activation(ident_bf[:], ident[:], ACT.Copy)
                    act.activation(band[:], band_f[:], ACT.Copy)

                @block.gpsimd
                def _(pool):
                    pool.memset(minus_half[:], -0.5)
                    pool.memset(ones_bf[:], 1.0)
                    pool.memset(ht[:], 0.0)

                @block.vector
                def _(dve):
                    v = Chain(dve, v_chain)
                    dve.wait_ge(first_loaded, NF)
                    dve.wait_ge(tanh_done, 1)
                    for i, (r, g) in enumerate(((4, 0), (5, 0), (6, 1))):
                        v.do(dve.tensor_scalar(gated_rows[:, i, :], rows[:, r, :], tg[:, g:g + 1], None, ALU.mult))
                    v.do(dve.tensor_tensor(sprod[:], fscale[:, 0:1], fscale[:, 1:2], ALU.mult))
                    v.do(dve.reciprocal(rscale[:], fscale[:]))
                    v.sync()
                    v.do(dve.tensor_scalar(qf[0][:], kern[:], rscale[:, 1:2], None, ALU.mult))
                    v.sync()
                    quantise(dve, v, qf, kern_q[:], D)

        with nc.Fori(0, B // U) as pair:
            with ExitStack() as cross_a:
                kbd_a = sb("kbd_a", [P, U, HA, SK], scope=cross_a)
                rep = sb("rep", [P, U, CA * P], scope=cross_a)
                sh = sb("sh", [P, 2, HA * SK], scope=cross_a)
                pr = sb("pr", [P, 3, HA * SK], scope=cross_a)
                pt = sb("pt", [P, CA, P], scope=cross_a)
                with stage("kt_raw", "kt_done", "rep_done", "v_raw", "v_chain", "var_ready", "rstd_ready", "xn_done",
                           "xnt_raw", "xnt_done", "q_raw") as (block, sems):
                    (kt_raw, kt_done, rep_done, v_raw, v_chain, var_ready, rstd_ready, xn_done,
                     xnt_raw, xnt_done, q_raw) = sems

                    @block.tensor
                    def _(pe):
                        c = ctxt[:].rearrange("p u k -> p (u k)")
                        pe.matmul(bank[0][:, 0:U * SK], wa["k"][:], c, start=True, stop=True).then_inc(kt_raw, 1)
                        pe.matmul(bank[1][:, 0:U * SK], wc["k"][:], c, start=True, stop=True).then_inc(kt_raw, 1)
                        for u in range(U):
                            pe.wait_ge(rep_done, u + 1)
                            for k in range(CA):
                                h0 = chunk_head(k, HA)
                                w = WIN * DA
                                mm = pe.matmul(bank[2 + u][:, k * w:(k + 1) * w], rep[:, u, k * P:(k + 1) * P],
                                               wa["v"][:, h0 * DA:h0 * DA + w], start=True, stop=True)
                            for k in range(CC):
                                h0 = chunk_head(k, HC)
                                w = WIN * DC
                                mm = pe.matmul(bank[4 + u][:, k * w:(k + 1) * w], rep[:, u, k * P:(k + 1) * P],
                                               wc["v"][:, h0 * DC:h0 * DC + w], start=True, stop=True)
                            mm.then_inc(v_raw, 1)
                        for u in range(U):
                            pe.wait_ge(xn_done, TPB * (u + 1))
                            for j in range(TPB):
                                t = pe.transpose(bank[6 + u][:, j * P:(j + 1) * P], xn[:, TPB * u + j, :], ident[:])
                            t.then_inc(xnt_raw, 1)
                        pe.wait_ge(kt_done, 1)
                        for u in range(U):
                            pe.wait_ge(xnt_done, u + 1)
                            pe.matmul(bank[u][:], wa["q"][:], xt[:, u, :], start=True, stop=True).then_inc(q_raw, 1)

                    @block.scalar
                    def _(act):
                        act.wait_ge(kt_raw, 2)
                        act.activation(kt_a[:].rearrange("p u k -> p (u k)"), bank[0][:, 0:U * SK], ACT.Identity,
                                       bias=cols_a[:, 1:2])
                        act.activation(kt_c[:].rearrange("p u k -> p (u k)"), bank[1][:, 0:U * SK],
                                       ACT.Copy).then_inc(kt_done, 1)
                        for u in range(U):
                            act.wait_ge(xnt_raw, u + 1)
                            act.activation(xt[:, u, :], bank[6 + u][:], ACT.Copy).then_inc(xnt_done, 1)
                        for u in range(U):
                            act.wait_ge(q_raw, u + 1)
                            act.activation(qt[:, u, :], bank[u][:], ACT.Identity, bias=cols_a[:, 0:1])

                    @block.gpsimd
                    def _(pool):
                        for u in range(U):
                            pool_rstd(pool, u, var_ready, rstd_ready)
                        for u in range(U):
                            pool.wait_ge(xn_done, TPB * (u + 1))
                            pool.tensor_tensor(base[:, TPB * u:TPB * (u + 1), :], xn[:, TPB * u:TPB * (u + 1), :],
                                               rows[:, 0:1, :].broadcast_to([P, TPB, D]), ALU.add)

                    @block.vector
                    def _(dve):
                        v = Chain(dve, v_chain)
                        for u in range(U):
                            dve_stats(dve, v, u, x, var_ready)
                            full = CA * P // SK
                            dve.tensor_copy(rep[:, u, 0:full * SK].rearrange("p (r k) -> p r k", k=SK),
                                            ctxt[:, u, :].unsqueeze(1).broadcast_to([P, full, SK]))
                            dve.tensor_copy(rep[:, u, full * SK:CA * P],
                                            ctxt[:, u, 0:CA * P - full * SK]).then_inc(rep_done, 1)
                        for u in range(U):
                            dve_normalize(dve, u, x, xn, rstd_ready, xn_done)
                        v.do(dve.tensor_scalar(keep[:], mflat[:], -1.0, 1.0, ALU.mult, ALU.add))
                        v.do(dve.tensor_scalar(mrow_bf[:], mrow[:], NEG, None, ALU.mult))
                        v.sync()
                        for u in range(U):
                            v.do(dve.tensor_tensor(kmask[:, u], vmask_a[:],
                                                   keep[:, u, :].unsqueeze(2).broadcast_to([P, CA, WIN]), ALU.mult))
                        dve.wait_ge(kt_done, 1)
                        for u in range(U):
                            dve.tensor_tensor(kbd_a[:, u], kt_a[:, u, :].unsqueeze(1).broadcast_to([P, HA, SK]),
                                              headmask_a[:].unsqueeze(2).broadcast_to([P, HA, SK]), ALU.mult)
                            dve.tensor_tensor(kbd_c[:, u], kt_c[:, u, :].unsqueeze(1).broadcast_to([P, HC, SK]),
                                              headmask_c[:].unsqueeze(2).broadcast_to([P, HC, SK]), ALU.mult)
                        v.sync()
                        for u in range(U):
                            dve.wait_ge(v_raw, u + 1)
                            dve.tensor_tensor(vbd_a[:, u, :, :, 0:DA].rearrange("p c w d -> p (c w) d"),
                                              bank[2 + u][:, 0:CA * WIN * DA].rearrange("p (w d) -> p w d", d=DA),
                                              kmask[:, u].rearrange("p c w -> p (c w)").unsqueeze(2).broadcast_to(
                                                  [P, CA * WIN, DA]), ALU.mult)
                            dve.tensor_copy(vbd_a[:, u, :, :, DA], kmask[:, u])
                            dve.tensor_tensor(vbd_c[:, u].rearrange("p c w d -> p (c w) d"),
                                              bank[4 + u][:, 0:CC * WIN * DC].rearrange("p (w d) -> p w d", d=DC),
                                              vmask_c[:].rearrange("p c w -> p (c w)").unsqueeze(2).broadcast_to(
                                                  [P, CC * WIN, DC]), ALU.mult)

                with stage("v_chain", "s_raw", "s_used", "exp_done", "pt_raw", "pt_done", "o_raw", "att_done",
                           "attt_raw", "attt_done", "r_raw", "r_done") as (block, sems):
                    (v_chain, s_raw, s_used, exp_done, pt_raw, pt_done, o_raw, att_done,
                     attt_raw, attt_done, r_raw, r_done) = sems
                    PTG = [(0, 4), (4, 8), (8, 10)]

                    @block.vector
                    def _(dve):
                        v = Chain(dve, v_chain)
                        for n in range(NT + LO):
                            if n >= LO:
                                m = n - LO
                                dve.wait_ge(r_raw, m + 1)
                                dve.tensor_tensor(base[:, m, :], bank[7][:, P:2 * P], base[:, m, :],
                                                  ALU.add).then_inc(r_done, 1)
                            if n < NT:
                                k = n % 2
                                s3 = sh[:, k, :].rearrange("p (h k) -> p h k", k=SK)
                                for g, (h0, h1) in enumerate(GA):
                                    dve.wait_ge(s_raw, 3 * n + g + 1)
                                    src = bank[g][:, 0:(h1 - h0) * SK].rearrange("p (h k) -> p h k", k=SK)
                                    v.do(dve.tensor_reduce(mx[:, k, h0:h1], src, AX.X, ALU.max))
                                v.sync()
                                if n >= 2:
                                    dve.wait_ge(exp_done, n - 1)
                                for g, (h0, h1) in enumerate(GA):
                                    src = bank[g][:, 0:(h1 - h0) * SK].rearrange("p (h k) -> p h k", k=SK)
                                    dve.tensor_tensor(s3[:, h0:h1, :], src,
                                                      mx[:, k, h0:h1].unsqueeze(2).broadcast_to([P, h1 - h0, SK]),
                                                      ALU.subtract).then_inc(s_used, 1)
                            if LP <= n < NT + LP:
                                m = n - LP
                                k = m % 2
                                o3 = bank[6][:, 0:HA * (DA + 1)].rearrange("p (h d) -> p h d", d=DA + 1)
                                dve.wait_ge(o_raw, m + 1)
                                v.do(dve.reciprocal(rd[:, k, :], o3[:, :, DA]))
                                v.sync()
                                if m >= 2:
                                    dve.wait_ge(attt_raw, m - 1)
                                dve.tensor_tensor(att[:, k, :].rearrange("p (h d) -> p h d", d=DA), o3[:, :, 0:DA],
                                                  rd[:, k, :].unsqueeze(2).broadcast_to([P, HA, DA]),
                                                  ALU.mult).then_inc(att_done, 1)

                    @block.tensor
                    def _(pe):
                        for n in range(NT + LO):
                            if n >= LO:
                                m = n - LO
                                pe.wait_ge(attt_done, m + 1)
                                pe.matmul(bank[7][:, P:2 * P], attt[:, m % 2, :], wa["o"][:], start=True,
                                          stop=True).then_inc(r_raw, 1)
                            if n < NT:
                                u, j = divmod(n, TPB)
                                for g, (h0, h1) in enumerate(GA):
                                    if n:
                                        pe.wait_ge(s_used, 3 * (n - 1) + g + 1)
                                    w = (h1 - h0) * SK
                                    pe.matmul(bank[g][:, 0:w], ones_bf[:],
                                              mrow_bf[:, u:u + 1, :].broadcast_to([1, h1 - h0, SK]), start=True, stop=False)
                                    pe.matmul(bank[g][:, 0:w], qt[:, u, j * P:(j + 1) * P],
                                              kbd_a[:, u, h0:h1, :].rearrange("p h k -> p (h k)"),
                                              start=False, stop=True).then_inc(s_raw, 1)
                            if LP <= n < NT + LP:
                                m = n - LP
                                pe.wait_ge(exp_done, m + 1)
                                for g, (c0, c1) in enumerate(PTG):
                                    if m:
                                        pe.wait_ge(pt_done, 3 * (m - 1) + g + 1)
                                    for c in range(c0, c1):
                                        r = chunk_rows(c, HA)
                                        t = pe.transpose(bank[3 + g][0:r, (c - c0) * P:(c - c0 + 1) * P],
                                                         pr[:, m % 3, c * P:c * P + r], ident[:])
                                    t.then_inc(pt_raw, 1)
                            if LT <= n < NT + LT:
                                m = n - LT
                                pe.wait_ge(att_done, m + 1)
                                if m:
                                    pe.wait_ge(r_done, m)
                                pe.transpose(bank[7][:, 0:P], att[:, m % 2, :], ident[:]).then_inc(attt_raw, 1)
                            if LP <= n < NT + LP:
                                m = n - LP
                                u = m // TPB
                                if m:
                                    pe.wait_ge(att_done, m)
                                for c in range(CA):
                                    r, h0 = chunk_rows(c, HA), chunk_head(c, HA)
                                    pe.wait_ge(pt_done, 3 * m + min(c // 4, 2) + 1)
                                    mm = pe.matmul(bank[6][:, h0 * (DA + 1):(h0 + WIN) * (DA + 1)], pt[0:r, c, :],
                                                   vbd_a[0:r, u, c, :, :].rearrange("p w d -> p (w d)"),
                                                   start=(c == 0), stop=True, skip_group_check=True)
                                mm.then_inc(o_raw, 1)

                    @block.scalar
                    def _(act):
                        for n in range(NT + LT):
                            if LP <= n < NT + LP:
                                m = n - LP
                                if m:
                                    act.wait_ge(o_raw, m)
                                for g, (c0, c1) in enumerate(PTG):
                                    act.wait_ge(pt_raw, 3 * m + g + 1)
                                    if g < 2:
                                        act.activation(pt[:, c0:c1, :], bank[3 + g][:].rearrange("p (c q) -> p c q", q=P),
                                                       ACT.Copy).then_inc(pt_done, 1)
                                    else:
                                        r = chunk_rows(CA - 1, HA)
                                        act.activation(pt[:, 8, :], bank[5][:, 0:P], ACT.Copy)
                                        act.activation(pt[0:r, 9, :], bank[5][0:r, P:2 * P], ACT.Copy).then_inc(pt_done, 1)
                            if n >= LT:
                                m = n - LT
                                act.wait_ge(attt_raw, m + 1)
                                if m >= 2:
                                    act.wait_ge(r_raw, m - 1)
                                act.activation(attt[:, m % 2, :], bank[7][:, 0:P], ACT.Identity,
                                               bias=cols_a[:, 2:3]).then_inc(attt_done, 1)
                            if n < NT:
                                act.wait_ge(s_used, 3 * (n + 1))
                                if n >= 3:
                                    act.wait_ge(pt_raw, 3 * (n - 2))
                                act.activation(pr[:, n % 3, :], sh[:, n % 2, :], ACT.Exp,
                                               scale=DA ** -0.5).then_inc(exp_done, 1)

            with ExitStack() as ffn:
                hidt = sb("hidt", [P, U, FF // P, S], scope=ffn)
                with stage("v_chain", "p_chain", "var1", "rstd1", "var2", "rstd2", "var3", "rstd3", "xn_done", "xnt_raw",
                           "xnt_done", "h_raw", "h_done", "f_raw", "base_done", "xb_done") as (block, sems):
                    (v_chain, p_chain, var1, rstd1, var2, rstd2, var3, rstd3, xn_done, xnt_raw,
                     xnt_done, h_raw, h_done, f_raw, base_done, xb_done) = sems
                    NC = FF // P

                    @block.vector
                    def _(dve):
                        v = Chain(dve, v_chain)
                        for u in range(U):
                            dve_stats(dve, v, u, base, var1)
                        for u in range(U):
                            dve_normalize(dve, u, base, xn, rstd1, xn_done)
                        for u in range(U):
                            sl = slice(TPB * u, TPB * (u + 1))
                            dve.wait_ge(f_raw, u + 1)
                            dve.wait_ge(base_done, u + 1)
                            v.do(dve.tensor_tensor(base[:, sl, :], bank[6 + u][:].rearrange("p (j d) -> p j d", d=D),
                                                   base[:, sl, :], ALU.add))
                            v.sync()
                            dve_stats(dve, v, u, base, var2)
                            for n in range(TPB * u, TPB * (u + 1)):
                                v.do(dve.scalar_tensor_tensor(out=base[:, n, :], in0=base[:, n, :], scalar=mv[:, n, 0:1],
                                                              in1=gated_rows[:, 0, :], op0=ALU.subtract, op1=ALU.mult))
                            v.sync()
                            dve.wait_ge(rstd2, u + 1)
                            dve.wait_ge(xb_done, u + 1)
                            for n in range(TPB * u, TPB * (u + 1)):
                                v.do(dve.scalar_tensor_tensor(out=x[:, n, :], in0=base[:, n, :], scalar=rstd[:, n:n + 1],
                                                              in1=x[:, n, :], op0=ALU.mult, op1=ALU.add))
                            v.sync()
                            dve_stats(dve, v, u, x, var3)
                            dve_normalize(dve, u, x, y, rstd3)

                    @block.gpsimd
                    def _(pool):
                        p = Chain(pool, p_chain)

                        def rows_op(u, dst, src, t, r, op):
                            sl = slice(TPB * u, TPB * (u + 1))
                            return pool.tensor_tensor(dst[:, sl, :], src[:, sl, :],
                                                      t[:, r:r + 1, :].broadcast_to([P, TPB, D]), op)

                        for u in range(U):
                            pool_rstd(pool, u, var1, rstd1)
                        for u in range(U):
                            pool.wait_ge(xn_done, TPB * (u + 1))
                            p.do(rows_op(u, base, xn, rows, 1, ALU.mult))
                            p.sync()
                            p.do(rows_op(u, base, base, rows, 2, ALU.add))
                            p.sync()
                            rows_op(u, base, base, rows, 3, ALU.add).then_inc(base_done, 1)
                            rows_op(u, x, x, gated_rows, 1, ALU.add).then_inc(xb_done, 1)
                        for u in range(U):
                            pool_rstd(pool, u, var2, rstd2)
                            pool_rstd(pool, u, var3, rstd3)

                    @block.tensor
                    def _(pe):
                        for u in range(U):
                            for j in range(TPB):
                                n = TPB * u + j
                                pe.wait_ge(xn_done, n + 1)
                                t = pe.transpose(bank[u][:, j * P:(j + 1) * P], xn[:, n, :], ident[:])
                            t.then_inc(xnt_raw, 1)
                        for u in range(U):
                            pe.wait_ge(xnt_done, u + 1)
                            for c in range(NC):
                                if u:
                                    pe.wait_ge(h_done, NC * (u - 1) + c + 1)
                                pe.matmul(bank[2 + c][:], wa1[:, c * P:(c + 1) * P], xt[:, u, :], start=True,
                                          stop=True).then_inc(h_raw, 1)
                            pe.wait_ge(h_done, NC * (u + 1))
                            for j in range(TPB):
                                for c in range(NC):
                                    mm = pe.matmul(bank[6 + u][:, j * P:(j + 1) * P], hidt[:, u, c, j * P:(j + 1) * P],
                                                   wa2[:, c, :], start=(c == 0), stop=(c == NC - 1))
                            mm.then_inc(f_raw, 1)

                    @block.scalar
                    def _(act):
                        for u in range(U):
                            act.wait_ge(xnt_raw, u + 1)
                            act.activation(xt[:, u, :], bank[u][:], ACT.Identity, bias=cols_a[:, 4:5],
                                           scale=cols_a[:, 3:4]).then_inc(xnt_done, 1)
                        for u in range(U):
                            for c in range(NC):
                                act.wait_ge(h_raw, NC * u + c + 1)
                                act.activation(hidt[:, u, c, :], bank[2 + c][:], ACT.Gelu,
                                               bias=b1_a[:, c:c + 1]).then_inc(h_done, 1)

            with nc.Fori(0, DEPTH) as layer:
                with ExitStack() as local:
                    qtb = sb("qtb", [P, U, 4, S], scope=local)
                    ktb = sb("ktb", [P, U, 4, PAD + S], scope=local)
                    va = sb("va", [P, U, TPB, INNER], scope=local)
                    vm = sb("vm", [P, U, TPB + 1, INNER], scope=local)
                    rt = sb("rt", [P, TPB, 4, DH], scope=local)
                    sq = sb("sq", [P, 2, INNER], scope=local)
                    t2 = sb("t2", [P, 2, INNER], scope=local)
                    qrot = sb("qrot", [P, 2, INNER], scope=local)
                    krot = sb("krot", [P, 2, INNER], scope=local)
                    n2 = sb("n2", [P, 2, 2 * HB], scope=local)
                    nh = sb("nh", [P, 2 * HB], scope=local)
                    pb = sb("pb", [P, 2, HB, P], scope=local)
                    ptb = sb("ptb", [P, HB, P], scope=local)
                    on = xt
                    ont = qt
                    with stage("loaded", "wo_loaded", "v_chain", "y_raw", "ht_done", "pads_done", "rt_done", "q_raw", "k_raw", "v_raw", "sq_done",
                               "k_prod", "q_prod", "k_sum", "q_sum", "n2_done", "rn_done", "k_normed", "qt_raw", "kt_raw",
                               "qt_done", "kt_done", "v_done", "s_raw", "nb_done", "exp_done", "pt_raw", "pt_done", "o_raw",
                               "on_done", "ont_raw", "ont_done", "r_raw", "r_done") as (block, sems):
                        (loaded, wo_loaded, v_chain, y_raw, ht_done, pads_done, rt_done, q_raw, k_raw, v_raw, sq_done,
                         k_prod, q_prod, k_sum, q_sum, n2_done, rn_done, k_normed, qt_raw, kt_raw,
                         qt_done, kt_done, v_done, s_raw, nb_done, exp_done, pt_raw, pt_done, o_raw,
                         on_done, ont_raw, ont_done, r_raw, r_done) = sems
                        LT1, LS, LV, LW = 1, 2, 3, 4
                        b_q, b_k, b_v, b_o = bank[0], bank[1], bank[2], bank[5]

                        def b_s(m):
                            return bank[3:5] if m < NT - 1 else bank[0:2]

                        b_t = bank[6:8]

                        @block.sync
                        def _(sp):
                            l = bass.ds(layer, 1)
                            sp.dma_start(wo_b[:], a["wo_b"][l].rearrange("o (c p) d -> p (o c) d", p=P)).then_inc(wo_loaded, 16)
                            sp.dma_start(cols_b[:], a["cols_b"][l].rearrange("o p n -> (o p) n")).then_inc(loaded, 16)
                            sp.dma_start(w1_b[:], a["w1_b"][l].rearrange("o p n -> (o p) n")).then_inc(loaded, 16)
                            sp.dma_start(w2_b[:, 0:2, :], a["w2_b"][l, 0:2 * P, :].rearrange(
                                "o (c p) d -> p (o c) d", p=P)).then_inc(loaded, 16)
                            sp.dma_start(w2_b[0:HID - 2 * P, 2, :], a["w2_b"][l, 2 * P:HID, :].rearrange(
                                "o p d -> p (o d)")).then_inc(loaded, 16)
                            sp.dma_start(row_b[:], a["row_b"][l].partition_broadcast(P).rearrange(
                                "p o d -> p (o d)")).then_inc(loaded, 16)
                            sp.wait_ge(rt_done, 1)
                            sp.dma_start(srow[:], a["srow_b"][bass.ds(layer + 1, 1)].partition_broadcast(P).rearrange(
                                "p o i d -> p (o i) d")).then_inc(loaded, 16)
                            sp.wait_ge(v_raw, NT)
                            sp.dma_start(wqkv[:], a["wqkv"][bass.ds(layer + 1, 1)].rearrange(
                                "o p n -> (o p) n")).then_inc(loaded, 16)
                            sp.wait_ge(loaded, 16 * 7)

                        @block.tensor
                        def _(pe):
                            for u in range(U):
                                for j in range(TPB):
                                    t = pe.transpose(b_t[u][:, j * P:(j + 1) * P], y[:, TPB * u + j, :], ident[:])
                                t.then_inc(y_raw, 1)
                            for n in range(NT + LW):
                                if LS <= n < NT + LS:
                                    m = n - LS
                                    u, j = divmod(m, TPB)
                                    if m == NT - 1:
                                        pe.wait_ge(q_prod, NT)
                                        pe.wait_ge(sq_done, 2 * NT)
                                    elif m:
                                        pe.wait_ge(exp_done, HB * m)
                                    else:
                                        pe.wait_ge(pads_done, 2)
                                    for g in range(2):
                                        pe.matmul(b_s(m)[g][:], ident_bf[:], band[:, 0 if j else 1, :].unsqueeze(1).broadcast_to(
                                            [P, 4, P]), start=True, stop=True, skip_group_check=True)
                                    pe.wait_ge(qt_done, m + 1)
                                    pe.wait_ge(kt_done, m + 1)
                                    q0 = j * P
                                    for g in range(2):
                                        for c in range(4):
                                            r, col = slice(64 * g, 64 * g + 64), slice(c * P, (c + 1) * P)
                                            keys = ktb[r, u, c, q0:q0 + P].rearrange("p (a e) -> p a e", a=2)[:, ::-1, :]
                                            pe.matmul(b_s(m)[g][0:64, col], qtb[r, u, c, q0:q0 + 64], keys, start=False, stop=True,
                                                      skip_group_check=True)
                                            mm = pe.matmul(b_s(m)[g][64:128, col], qtb[r, u, c, q0 + 64:q0 + P],
                                                           ktb[r, u, c, PAD + q0:PAD + q0 + P], start=False, stop=True,
                                                           skip_group_check=True)
                                        mm.then_inc(s_raw, 1)
                                if n >= LW:
                                    m = n - LW
                                    pe.wait_ge(on_done, m + 1)
                                    pe.wait_ge(qt_done, min(n - 1, NT))
                                    for c in range(4):
                                        t = pe.transpose(b_t[0][:, c * P:(c + 1) * P], on[:, m % 2, c * P:(c + 1) * P], ident[:])
                                    t.then_inc(ont_raw, 1)
                                if n < NT:
                                    u, j = divmod(n, TPB)
                                    h = ht[:, u, PAD + j * P:PAD + (j + 1) * P]
                                    pe.wait_ge(ht_done, u + 1)
                                    if n:
                                        pe.wait_ge(q_prod, n)
                                        pe.wait_ge(sq_done, 2 * n - 1)
                                    pe.matmul(b_q[:], h, wqkv[:, 0:INNER], start=True, stop=True).then_inc(q_raw, 1)
                                    if n:
                                        pe.wait_ge(k_prod, n)
                                        pe.wait_ge(sq_done, 2 * n)
                                    pe.matmul(b_k[:], h, wqkv[:, INNER:2 * INNER], start=True, stop=True).then_inc(k_raw, 1)
                                if n >= LW:
                                    m = n - LW
                                    pe.wait_ge(wo_loaded, 16)
                                    pe.wait_ge(ont_done, m + 1)
                                    pe.wait_ge(kt_done, min(n - 1, NT))
                                    for c in range(4):
                                        mm = pe.matmul(b_t[1][:, 0:P], ont[:, m % 2, c * P:(c + 1) * P], wo_b[:, c, :],
                                                       start=(c == 0), stop=(c == 3))
                                    mm.then_inc(r_raw, 1)
                                for g in range(2):
                                    if g == 1 and n < NT:
                                        if n:
                                            pe.wait_ge(v_done, n)
                                        pe.matmul(b_v[:], h, wqkv[:, 2 * INNER:], start=True, stop=True).then_inc(v_raw, 1)
                                    if LV <= n < NT + LV:
                                        m = n - LV
                                        pe.wait_ge(exp_done, HB * m + 4 * g + 4)
                                        if n >= LW:
                                            pe.wait_ge((ont_done, r_done)[g], n - LW + 1)
                                        else:
                                            pe.wait_ge((qt_done, kt_done)[g], n - 1)
                                        for c in range(4):
                                            t = pe.transpose(b_t[g][:, c * P:(c + 1) * P], pb[:, m % 2, 2 * c + g, :], ident[:])
                                        t.then_inc(pt_raw, 1)
                                if LT1 <= n < NT + LT1:
                                    m = n - LT1
                                    pe.wait_ge(ht_done, U)
                                    for g, (rotated, done, src, raw) in enumerate(((q_sum, qt_done, qrot, qt_raw),
                                                                                   (k_normed, kt_done, krot, kt_raw))):
                                        pe.wait_ge(rotated, m + 1)
                                        if n >= LV:
                                            pe.wait_ge(pt_done, 2 * (n - LV) + g + 1)
                                        elif m:
                                            pe.wait_ge(done, m)
                                        for c in range(4):
                                            t = pe.transpose(b_t[g][:, c * P:(c + 1) * P], src[:, m % 2, c * P:(c + 1) * P], ident[:])
                                        t.then_inc(raw, 1)
                                if LV <= n < NT + LV:
                                    m = n - LV
                                    u, j = divmod(m, TPB)
                                    pe.wait_ge(v_done, m + 1)
                                    if m:
                                        pe.wait_ge(on_done, m)
                                    for i in range(HB):
                                        h = 2 * (i % 4) + i // 4
                                        pe.wait_ge(pt_done, 2 * m + i // 4 + 1)
                                        hs = slice(h * DH, (h + 1) * DH)
                                        pe.matmul(b_o[0:64, hs], ptb[:, i, 0:64], vm[:, u, j, hs], start=True, stop=True)
                                        mm = pe.matmul(b_o[64:128, hs], ptb[:, i, 64:128], va[:, u, j, hs], start=True, stop=True)
                                    mm.then_inc(o_raw, 1)

                        @block.scalar
                        def _(act):
                            for u in range(U):
                                act.wait_ge(y_raw, u + 1)
                                act.activation(ht[0:64, u, PAD:PAD + S], b_t[u][0:64, :], ACT.Copy)
                                act.activation(ht[64:128, u, PAD + 1:PAD + S + 1], b_t[u][64:128, :], ACT.Copy).then_inc(ht_done, 1)

                            def exps(m, g, heads=range(4)):
                                act.wait_ge(nb_done, 2 * m + g + 1)
                                for c in heads:
                                    h = 2 * c + g
                                    act.activation(pb[:, m % 2, h, :], b_s(m)[g][:, c * P:(c + 1) * P], ACT.Exp, bias=nb[:, m % 2, h:h + 1],
                                                   scale=qsc[:, m, h:h + 1], accum_out=den[:, m % 2, h:h + 1]).then_inc(exp_done, 1)

                            for n in range(NT + LW):
                                if n >= LW:
                                    m = n - LW
                                    act.wait_ge(ont_raw, m + 1)
                                    if m >= 2:
                                        act.wait_ge(r_raw, m - 1)
                                    act.activation(ont[:, m % 2, :], b_t[0][:], ACT.Copy).then_inc(ont_done, 1)
                                if LS <= n < NT + LS:
                                    m = n - LS
                                    if m >= 2:
                                        act.wait_ge(pt_raw, 2 * (m - 1))
                                        act.wait_ge(on_done, m - 1)
                                    exps(m, 0)
                                if n < NT:
                                    if n:
                                        act.wait_ge(n2_done, n)
                                    act.wait_ge(q_raw, n + 1)
                                    act.activation(sq[:, 0, :], b_q[:], ACT.Square).then_inc(sq_done, 1)
                                for g in range(2):
                                    if LV <= n < NT + LV:
                                        m = n - LV
                                        if m:
                                            act.wait_ge(o_raw, m)
                                        act.wait_ge(pt_raw, 2 * m + g + 1)
                                        act.activation(ptb[:, 4 * g:4 * g + 4, :], b_t[g][:].rearrange(
                                            "p (h q) -> p h q", q=P), ACT.Copy).then_inc(pt_done, 1)
                                    if LS <= n < NT:
                                        exps(n - LS, 1, range(2 * g, 2 * g + 2))
                                if n < NT:
                                    act.wait_ge(k_prod, n + 1)
                                    act.activation(sq[:, 1, :], b_k[:], ACT.Square).then_inc(sq_done, 1)
                                if LT1 <= n < NT + LT1:
                                    u, j = divmod(n - LT1, TPB)
                                    act.wait_ge(qt_raw, n - LT1 + 1)
                                    act.activation(qtb[:, u, :, j * P:(j + 1) * P], b_t[0][:].rearrange("p (c q) -> p c q", q=P),
                                                   ACT.Copy).then_inc(qt_done, 1)
                                    act.wait_ge(kt_raw, n - LT1 + 1)
                                    act.activation(ktb[:, u, :, PAD + j * P:PAD + (j + 1) * P], b_t[1][:].rearrange(
                                        "p (c q) -> p c q", q=P), ACT.Copy).then_inc(kt_done, 1)
                                if NT <= n < NT + LS:
                                    exps(n - LS, 1)
                                if n < NT:
                                    u, j = divmod(n, TPB)
                                    act.wait_ge(v_raw, n + 1)
                                    act.activation(va[:, u, j, :], b_v[:], ACT.Copy)
                                    act.activation(vm[0:64, u, j, :], b_v[0:64, :], ACT.Copy)
                                    act.activation(vm[64:128, u, j + 1, :], b_v[64:128, :], ACT.Copy).then_inc(v_done, 1)

                        @block.vector
                        def _(dve):
                            v = Chain(dve, v_chain)
                            dve.tensor_tensor(rt[:], rot[:], srow[:].unsqueeze(1).broadcast_to([P, TPB, 4, DH]),
                                              ALU.mult).then_inc(rt_done, 1)
                            dve.wait_ge(rt_done, 1)

                            def products(src, dst, tmp, j, i):
                                dve.tensor_tensor(dst.rearrange("p (h d) -> p h d", d=DH), src.rearrange("p (h d) -> p h d", d=DH),
                                                  rt[:, j, i:i + 1, :].broadcast_to([P, HB, DH]), ALU.mult)
                                return dve.tensor_tensor(
                                    tmp.rearrange("p (h a e) -> p h a e", a=2, e=DH // 2),
                                    src.rearrange("p (h a e) -> p h a e", a=2, e=DH // 2)[:, :, ::-1, :],
                                    rt[:, j, i + 1:i + 2, :].rearrange("p i (a e) -> p i a e", a=2).broadcast_to(
                                        [P, HB, 2, DH // 2]), ALU.mult)

                            def norm_start(m):
                                e, w = n2[:, m % 2, :], rn[:, m].rearrange("p k h -> p (k h)")
                                dve.wait_ge(n2_done, m + 1)
                                v.do(dve.tensor_scalar(e, e, 1e-24, None, ALU.max))
                                v.sync()
                                v.do(dve.tensor_scalar(w.bitcast(I32), e.bitcast(I32), -0.5, 1597463007.0, ALU.mult, ALU.add))

                            def norm_step(m, last=False):
                                e, w = n2[:, m % 2, :], rn[:, m].rearrange("p k h -> p (k h)")
                                v.sync()
                                v.do(dve.scalar_tensor_tensor(out=nh[:], in0=w, scalar=-0.5, in1=w, op0=ALU.mult, op1=ALU.mult))
                                v.sync()
                                v.do(dve.tensor_tensor(nh[:], nh[:], e, ALU.mult))
                                v.sync()
                                ins = dve.scalar_tensor_tensor(out=w, in0=nh[:], scalar=1.5, in1=w, op0=ALU.add, op1=ALU.mult)
                                ins.then_inc(rn_done, 1) if last else v.do(ins)

                            for n in range(NT + LW):
                                if LS <= n < NT + LS:
                                    m = n - LS
                                    k = m % 2
                                    for g in range(2):
                                        hs = slice(g, HB, 2)
                                        dve.wait_ge(s_raw, 2 * m + g + 1)
                                        v.do(dve.tensor_reduce(mx[:, k, hs], b_s(m)[g][:].rearrange("p (h q) -> p h q", q=P), AX.X,
                                                               ALU.max))
                                        v.sync()
                                        if m >= 2:
                                            dve.wait_ge(exp_done, HB * (m - 1))
                                        dve.scalar_tensor_tensor(out=nb[:, k, hs], in0=mx[:, k, hs], scalar=-1.0, in1=qsc[:, m, hs],
                                                                 op0=ALU.mult, op1=ALU.mult).then_inc(nb_done, 1)
                                        if g == 0 and n <= NT:
                                            norm_step(n - 1, last=True)
                                elif n == 1:
                                    norm_step(0, last=True)
                                if 1 <= n <= NT:
                                    dve.wait_ge(rn_done, n)
                                    v.do(dve.tensor_scalar(qsc[:, n - 1, :], rn[:, n - 1, 0, :], 8.0, None, ALU.mult))
                                if n < NT:
                                    j = n % TPB
                                    dve.wait_ge(k_raw, n + 1)
                                    if n:
                                        dve.wait_ge(k_sum, n)
                                    if n >= 2:
                                        dve.wait_ge(kt_raw, n - 1)
                                    products(b_k[:], krot[:, n % 2, :], t2[:, 1, :], j, 2).then_inc(k_prod, 1)
                                if n >= LW:
                                    m = n - LW
                                    dve.wait_ge(r_raw, m + 1)
                                    dve.tensor_tensor(y[:, m, :], b_t[1][:, 0:P], y[:, m, :], ALU.add).then_inc(r_done, 1)
                                if n < NT:
                                    dve.wait_ge(sq_done, 2 * n + 1)
                                    if n:
                                        dve.wait_ge(q_sum, n)
                                    if n >= 2:
                                        dve.wait_ge(qt_raw, n - 1)
                                    products(b_q[:], qrot[:, n % 2, :], t2[:, 0, :], j, 0).then_inc(q_prod, 1)
                                    dve.wait_ge(sq_done, 2 * n + 2)
                                    dve.tensor_reduce(n2[:, n % 2, :], sq[:].rearrange("p k (h d) -> p (k h) d", d=DH), AX.X,
                                                      ALU.add).then_inc(n2_done, 1)
                                    norm_start(n)
                                    norm_step(n)
                                if LV <= n < NT + LV:
                                    m = n - LV
                                    k = m % 2
                                    dve.wait_ge(exp_done, HB * (m + 1))
                                    v.do(dve.reciprocal(rd[:, k, 0:HB], den[:, k, 0:HB]))
                                    dve.wait_ge(o_raw, m + 1)
                                    v.sync()
                                    if m >= 2:
                                        dve.wait_ge(ont_raw, m - 1)
                                    dve.tensor_tensor(on[:, k, :].rearrange("p (h d) -> p h d", d=DH),
                                                      b_o[:].rearrange("p (h d) -> p h d", d=DH),
                                                      rd[:, k, 0:HB].unsqueeze(2).broadcast_to([P, HB, DH]),
                                                      ALU.mult).then_inc(on_done, 1)
                                if n < NT:
                                    norm_step(n)

                        @block.gpsimd
                        def _(pool):
                            pool.memset(ktb[:, :, :, 0:PAD], 0.0).then_inc(pads_done, 1)
                            pool.wait_ge(pads_done, 1)
                            pool.memset(vm[64:128, :, 0, :], 0.0).then_inc(pads_done, 1)
                            pool.wait_ge(pads_done, 2)
                            for n in range(NT + 1):
                                if n:
                                    m = n - 1
                                    pool.wait_ge(rn_done, m + 1)
                                    pool.wait_ge(k_sum, m + 1)
                                    k3 = krot[:, m % 2, :].rearrange("p (h d) -> p h d", d=DH)
                                    pool.tensor_tensor(k3, k3, rn[:, m, 1, :].unsqueeze(2).broadcast_to([P, HB, DH]),
                                                       ALU.mult).then_inc(k_normed, 1)
                                if n < NT:
                                    pool.wait_ge(k_prod, n + 1)
                                    pool.tensor_tensor(krot[:, n % 2, :], krot[:, n % 2, :], t2[:, 1, :], ALU.add).then_inc(k_sum, 1)
                                    pool.wait_ge(q_prod, n + 1)
                                    pool.tensor_tensor(qrot[:, n % 2, :], qrot[:, n % 2, :], t2[:, 0, :], ALU.add).then_inc(q_sum, 1)

                with ExitStack() as ffn:
                    hidt = sb("hidt_b", [P, U, len(HCH), S], scope=ffn)
                    gel = sb("gel", [P, 2, S], scope=ffn)
                    with stage("v_chain", "sh_raw", "var_ready", "rstd_ready", "xn_done", "xnt_raw", "xnt_done", "g_raw",
                               "gel_done", "hid_done", "f_raw", "base_done") as (block, sems):
                        (v_chain, sh_raw, var_ready, rstd_ready, xn_done, xnt_raw, xnt_done, g_raw,
                         gel_done, hid_done, f_raw, base_done) = sems
                        NH = len(HCH)

                        @block.tensor
                        def _(pe):
                            for u in range(U):
                                t0 = TPB * u
                                pe.matmul(bank[u][:, 0:TPB * 64], shift[:, 0, :], y[:, t0:t0 + TPB, 64:128], start=True,
                                          stop=True, skip_group_check=True)
                                pe.matmul(bank[u][:, 64:TPB * 64], shift[:, 1, :], y[:, t0:t0 + TPB - 1, 64:128],
                                          start=False, stop=True, skip_group_check=True).then_inc(sh_raw, 1)
                            for u in range(U):
                                pe.wait_ge(xn_done, TPB * (u + 1))
                                for j in range(TPB):
                                    t = pe.transpose(bank[u][:, j * P:(j + 1) * P], xn[:, TPB * u + j, :], ident[:])
                                t.then_inc(xnt_raw, 1)
                            for u in range(U):
                                pe.wait_ge(xnt_done, u + 1)
                                for c, (h0, w) in enumerate(HCH):
                                    g = NH * u + c
                                    if g >= 2:
                                        pe.wait_ge(hid_done, g - 1)
                                    b0 = 2 + 2 * (g % 2)
                                    pe.matmul(bank[b0][0:w, :], w1_b[:, h0:h0 + w], xt[:, u, :], start=True, stop=True)
                                    pe.matmul(bank[b0 + 1][0:w, :], w1_b[:, HID + h0:HID + h0 + w], xt[:, u, :], start=True,
                                              stop=True).then_inc(g_raw, 1)
                            for u in range(U):
                                pe.wait_ge(hid_done, NH * (u + 1))
                                for j in range(TPB):
                                    for c, (h0, w) in enumerate(HCH):
                                        mm = pe.matmul(bank[6 + u][:, j * P:(j + 1) * P], hidt[0:w, u, c, j * P:(j + 1) * P],
                                                       w2_b[0:w, c, :], start=(c == 0), stop=(c == NH - 1))
                                mm.then_inc(f_raw, 1)

                        @block.scalar
                        def _(act):
                            for u in range(U):
                                act.wait_ge(xnt_raw, u + 1)
                                act.activation(xt[:, u, :], bank[u][:], ACT.Identity, bias=cols_b[:, 1:2],
                                               scale=cols_b[:, 0:1]).then_inc(xnt_done, 1)
                            for u in range(U):
                                for c, (h0, w) in enumerate(HCH):
                                    g = NH * u + c
                                    act.wait_ge(g_raw, g + 1)
                                    if g >= 2:
                                        act.wait_ge(hid_done, g - 1)
                                    act.activation(gel[0:w, g % 2, :], bank[3 + 2 * (g % 2)][0:w, :], ACT.Gelu,
                                                   bias=cols_b[0:w, 5 + c:6 + c]).then_inc(gel_done, 1)

                        @block.gpsimd
                        def _(pool):
                            for u in range(U):
                                pool_rstd(pool, u, var_ready, rstd_ready)
                            for u in range(U):
                                sl = slice(TPB * u, TPB * (u + 1))
                                pool.tensor_tensor(base[:, sl, :], y[:, sl, :], row_b[:].unsqueeze(1).broadcast_to([P, TPB, D]),
                                                   ALU.add).then_inc(base_done, 1)

                        @block.vector
                        def _(dve):
                            v = Chain(dve, v_chain)
                            for u in range(U):
                                dve.wait_ge(sh_raw, u + 1)
                                dve_stats(dve, v, u, y, var_ready, lambda j: bank[u][:, 64 * j:64 * j + 64])
                            for u in range(U):
                                dve_normalize(dve, u, y, xn, rstd_ready, xn_done, lambda j: bank[u][:, 64 * j:64 * j + 64])
                            for u in range(U):
                                for c, (h0, w) in enumerate(HCH):
                                    g = NH * u + c
                                    dve.wait_ge(gel_done, g + 1)
                                    dve.scalar_tensor_tensor(out=hidt[0:w, u, c, :], in0=bank[2 + 2 * (g % 2)][0:w, :],
                                                             scalar=cols_b[0:w, 2 + c:3 + c], in1=gel[0:w, g % 2, :],
                                                             op0=ALU.add, op1=ALU.mult).then_inc(hid_done, 1)
                            for u in range(U):
                                sl = slice(TPB * u, TPB * (u + 1))
                                dve.wait_ge(f_raw, u + 1)
                                dve.wait_ge(base_done, u + 1)
                                dve.tensor_tensor(y[:, sl, :], bank[6 + u][:].rearrange("p (j d) -> p j d", d=D),
                                                  base[:, sl, :], ALU.add)

            with ExitStack() as cross_c:
                sh = sb("sh_c", [P, 2, HA * SK], scope=cross_c)
                gt = sb("gt_c", [P, 2, HC * SK], scope=cross_c)
                pr = sb("pr_c", [P, 2, HA * SK], scope=cross_c)
                pt = sb("pt_c", [P, CA, P], scope=cross_c)
                with stage("v_chain", "var_ready", "rstd_ready", "xn_done", "xnt_raw", "xnt_done", "q_raw", "q_done",
                           "s_raw", "g_done", "sh_done", "exp_done", "pm_done", "pt_raw", "pt_done", "o_raw", "att_done",
                           "attt_raw", "attt_done", "r_raw", "r_done", "base_done", "mx_done", "den_done") as (block, sems):
                    (v_chain, var_ready, rstd_ready, xn_done, xnt_raw, xnt_done, q_raw, q_done,
                     s_raw, g_done, sh_done, exp_done, pm_done, pt_raw, pt_done, o_raw, att_done,
                     attt_raw, attt_done, r_raw, r_done, base_done, mx_done, den_done) = sems
                    WC_ = HC * SK

                    @block.vector
                    def _(dve):
                        v = Chain(dve, v_chain)
                        v.do(dve.scalar_tensor_tensor(out=x[:], in0=y[:], scalar=tg[:, 2:3], in1=x[:], op0=ALU.mult,
                                                      op1=ALU.add))
                        v.sync()
                        for u in range(U):
                            dve_stats(dve, v, u, x, var_ready)
                        for u in range(U):
                            dve_normalize(dve, u, x, xn, rstd_ready, xn_done)
                        for n in range(NT + LO):
                            if n >= LO:
                                m = n - LO
                                dve.wait_ge(r_raw, m + 1)
                                dve.wait_ge(base_done, U)
                                dve.scalar_tensor_tensor(out=x[:, m, :], in0=bank[7][:, P:2 * P], scalar=tg[:, 1:2],
                                                         in1=base[:, m, :], op0=ALU.mult, op1=ALU.add).then_inc(r_done, 1)
                            if n < NT:
                                k = n % 2
                                g3 = gt[:, k, :].rearrange("p (h k) -> p h k", k=SK)
                                if n >= 2:
                                    dve.wait_ge(pm_done, n - 1)
                                for g, (h0, h1) in enumerate(GC):
                                    dve.wait_ge(s_raw, 2 * n + g + 1)
                                    src = bank[2 * k + g][:, 0:(h1 - h0) * SK].rearrange("p (h k) -> p h k", k=SK)
                                    dve.tensor_tensor(g3[:, h0:h1, :], src, tmat[:, n:n + 1, :].broadcast_to(
                                        [P, h1 - h0, SK]), ALU.mult).then_inc(g_done, 1)
                                dve.wait_ge(g_done, 2 * (n + 1))
                                if n >= 2:
                                    dve.wait_ge(sh_done, n - 1)
                                dve.tensor_reduce(mx[:, k, 0:HC], g3, AX.X, ALU.max).then_inc(mx_done, 1)
                            if 1 <= n <= NT:
                                m = n - 1
                                k = m % 2
                                dve.wait_ge(exp_done, m + 1)
                                dve.tensor_reduce(den[:, k, 0:HC], sh[:, k, 0:WC_].rearrange("p (h k) -> p h k", k=SK),
                                                  AX.X, ALU.add).then_inc(den_done, 1)
                                if m >= 2:
                                    dve.wait_ge(pt_raw, 2 * (m - 1))
                                dve.scalar_tensor_tensor(out=pr[:, k, 0:WC_], in0=gt[:, k, :], scalar=0.0,
                                                         in1=sh[:, k, 0:WC_], op0=ALU.not_equal,
                                                         op1=ALU.mult).then_inc(pm_done, 1)
                                dve.wait_ge(den_done, m + 1)
                                v.do(dve.reciprocal(rd[:, k, 0:HC], den[:, k, 0:HC]))
                            if LP <= n < NT + LP:
                                m = n - LP
                                k = m % 2
                                dve.wait_ge(o_raw, m + 1)
                                v.sync()
                                if m >= 2:
                                    dve.wait_ge(attt_raw, m - 1)
                                dve.tensor_tensor(att[:, k, :].rearrange("p (h d) -> p h d", d=DC),
                                                  bank[6][:, 0:P].rearrange("p (h d) -> p h d", d=DC),
                                                  rd[:, k, 0:HC].unsqueeze(2).broadcast_to([P, HC, DC]),
                                                  ALU.mult).then_inc(att_done, 1)

                    @block.gpsimd
                    def _(pool):
                        for u in range(U):
                            pool_rstd(pool, u, var_ready, rstd_ready)
                        for u in range(U):
                            sl = slice(TPB * u, TPB * (u + 1))
                            pool.tensor_tensor(base[:, sl, :], x[:, sl, :], gated_rows[:, 2:3, :].broadcast_to([P, TPB, D]),
                                               ALU.add).then_inc(base_done, 1)
                        for n in range(NT):
                            k = n % 2
                            pool.wait_ge(mx_done, n + 1)
                            if n >= 2:
                                pool.wait_ge(den_done, n - 1)
                                pool.wait_ge(pm_done, n - 1)
                            pool.tensor_tensor(sh[:, k, 0:WC_].rearrange("p (h k) -> p h k", k=SK),
                                               gt[:, k, :].rearrange("p (h k) -> p h k", k=SK),
                                               mx[:, k, 0:HC].unsqueeze(2).broadcast_to([P, HC, SK]),
                                               ALU.subtract).then_inc(sh_done, 1)

                    @block.tensor
                    def _(pe):
                        for u in range(U):
                            for j in range(TPB):
                                n = TPB * u + j
                                pe.wait_ge(xn_done, n + 1)
                                t = pe.transpose(bank[2 * u][:, j * P:(j + 1) * P], xn[:, n, :], ident[:])
                            t.then_inc(xnt_raw, 1)
                        for u in range(U):
                            pe.wait_ge(xnt_done, u + 1)
                            pe.matmul(bank[2 * u + 1][:], wc["q"][:], xt[:, u, :], start=True, stop=True).then_inc(q_raw, 1)
                        for n in range(NT + LO):
                            if n >= LO:
                                m = n - LO
                                pe.wait_ge(attt_done, m + 1)
                                pe.matmul(bank[7][:, P:2 * P], attt[:, m % 2, :], wc["p"][:], start=True,
                                          stop=True).then_inc(r_raw, 1)
                            if n < NT:
                                u, j = divmod(n, TPB)
                                pe.wait_ge(q_done, U)
                                for g, (h0, h1) in enumerate(GC):
                                    if n >= 2:
                                        pe.wait_ge(g_done, 2 * (n - 2) + g + 1)
                                    pe.matmul(bank[2 * (n % 2) + g][:, 0:(h1 - h0) * SK], qt[:, u, j * P:(j + 1) * P],
                                              kbd_c[:, u, h0:h1, :].rearrange("p h k -> p (h k)"),
                                              start=True, stop=True).then_inc(s_raw, 1)
                            if LP <= n < NT + LP:
                                m = n - LP
                                pe.wait_ge(pm_done, m + 1)
                                for g in range(2):
                                    if m:
                                        pe.wait_ge(pt_done, 2 * (m - 1) + g + 1)
                                    for c in range(4 * g, min(4 * g + 4, CC)):
                                        r = chunk_rows(c, HC)
                                        t = pe.transpose(bank[4 + g][0:r, (c % 4) * P:(c % 4 + 1) * P],
                                                         pr[:, m % 2, c * P:c * P + r], ident[:])
                                    t.then_inc(pt_raw, 1)
                            if LT <= n < NT + LT:
                                m = n - LT
                                pe.wait_ge(att_done, m + 1)
                                if m:
                                    pe.wait_ge(r_done, m)
                                pe.transpose(bank[7][:, 0:P], att[:, m % 2, :], ident[:]).then_inc(attt_raw, 1)
                            if LP <= n < NT + LP:
                                m = n - LP
                                u = m // TPB
                                if m:
                                    pe.wait_ge(att_done, m)
                                for c in range(CC):
                                    r, h0 = chunk_rows(c, HC), chunk_head(c, HC)
                                    pe.wait_ge(pt_done, 2 * m + c // 4 + 1)
                                    mm = pe.matmul(bank[6][:, h0 * DC:(h0 + WIN) * DC], pt[0:r, c, :],
                                                   vbd_c[0:r, u, c, :, :].rearrange("p w d -> p (w d)"),
                                                   start=(c == 0), stop=True, skip_group_check=True)
                                mm.then_inc(o_raw, 1)

                    @block.scalar
                    def _(act):
                        for u in range(U):
                            act.wait_ge(xnt_raw, u + 1)
                            act.activation(xt[:, u, :], bank[2 * u][:], ACT.Copy).then_inc(xnt_done, 1)
                        for u in range(U):
                            act.wait_ge(q_raw, u + 1)
                            act.activation(qt[:, u, :], bank[2 * u + 1][:], ACT.Copy).then_inc(q_done, 1)
                        for n in range(NT + LT):
                            if LP <= n < NT + LP:
                                m = n - LP
                                if m:
                                    act.wait_ge(o_raw, m)
                                act.wait_ge(pt_raw, 2 * m + 1)
                                act.activation(pt[:, 0:4, :], bank[4][:].rearrange("p (c q) -> p c q", q=P),
                                               ACT.Copy).then_inc(pt_done, 1)
                                act.wait_ge(pt_raw, 2 * m + 2)
                                r = chunk_rows(CC - 1, HC)
                                act.activation(pt[0:r, 4, :], bank[5][0:r, 0:P], ACT.Copy).then_inc(pt_done, 1)
                            if n >= LT:
                                m = n - LT
                                act.wait_ge(attt_raw, m + 1)
                                if m >= 2:
                                    act.wait_ge(r_raw, m - 1)
                                act.activation(attt[:, m % 2, :], bank[7][:, 0:P], ACT.Copy).then_inc(attt_done, 1)
                            if n < NT:
                                act.wait_ge(sh_done, n + 1)
                                act.activation(sh[:, n % 2, 0:WC_], sh[:, n % 2, 0:WC_], ACT.Exp,
                                               scale=DC ** -0.5).then_inc(exp_done, 1)

            with ExitStack() as quant:
                xbf = sb("xbf", [P, NT, D], BF16, scope=quant)
                xq = sb("xq", [P, NT, D], BF16, scope=quant)
                xqt = sb("xqt", [P, U, S], BF16, scope=quant)
                fo = sb("fo", [P, NT, D], BF16, scope=quant)
                qf = [sb(f"qf{i}", [P, TPB * D], scope=quant) for i in range(3)]
                with stage("v_chain", "var_ready", "rstd_ready", "xbf_done", "xq_done", "xqt_raw", "xqt_done", "f_raw",
                           "fo_done", "x_done", "stored", "loaded", "x_loaded") as (block, sems):
                    (v_chain, var_ready, rstd_ready, xbf_done, xq_done, xqt_raw, xqt_done, f_raw, fo_done, x_done, stored, loaded, x_loaded) = sems

                    @block.vector
                    def _(dve):
                        v = Chain(dve, v_chain)
                        for u in range(U):
                            dve_stats(dve, v, u, x, var_ready)
                        for u in range(U):
                            dve_normalize(dve, u, x, xbf, rstd_ready, xbf_done)
                            dve.wait_ge(xbf_done, TPB * (u + 1))
                            sl = slice(TPB * u, TPB * (u + 1))
                            v.do(dve.tensor_scalar(qf[0][:], xbf[:, sl, :].rearrange("p n d -> p (n d)"),
                                                   rscale[:, 0:1], None, ALU.mult))
                            v.sync()
                            quantise(dve, v, qf, xq[:, sl, :].rearrange("p n d -> p (n d)"), TPB * D, xq_done)
                        for u in range(U):
                            sl = slice(TPB * u, TPB * (u + 1))
                            dve.wait_ge(fo_done, u + 1)
                            v.do(dve.tensor_tensor(fo[:, sl, :], fo[:, sl, :], fbias[:].unsqueeze(1).broadcast_to(
                                [P, TPB, D]), ALU.add))
                            v.sync()
                            dve.scalar_tensor_tensor(out=y[:, sl, :], in0=fo[:, sl, :], scalar=tg[:, 3:4],
                                                     in1=x[:, sl, :], op0=ALU.mult, op1=ALU.add).then_inc(x_done, 1)

                    @block.gpsimd
                    def _(pool):
                        for u in range(U):
                            pool_rstd(pool, u, var_ready, rstd_ready)

                    @block.tensor
                    def _(pe):
                        for u in range(U):
                            pe.wait_ge(xq_done, u + 1)
                            for j in range(TPB):
                                t = pe.transpose(bank[u][:].bitcast(BF16)[:, j * P:(j + 1) * P], xq[:, TPB * u + j, :],
                                                 ident_bf[:])
                            t.then_inc(xqt_raw, 1)
                            pe.wait_ge(xqt_done, u + 1)
                            for j in range(TPB):
                                mm = pe.matmul(bank[2 + u][:, j * P:(j + 1) * P], xqt[:, u, j * P:(j + 1) * P], kern_q[:],
                                               start=True, stop=True)
                            mm.then_inc(f_raw, 1)

                    @block.scalar
                    def _(act):
                        for u in range(U):
                            act.wait_ge(xqt_raw, u + 1)
                            act.activation(xqt[:, u, :], bank[u][:].bitcast(BF16)[:, 0:S], ACT.Copy).then_inc(xqt_done, 1)
                            act.wait_ge(f_raw, u + 1)
                            act.activation(fo[:, TPB * u:TPB * (u + 1), :], bank[2 + u][:].rearrange(
                                "p (j d) -> p j d", d=D), ACT.Identity, scale=sprod[:, 0:1]).then_inc(fo_done, 1)
                        xp = a["x"][bass.ds(pair + 1, 1)].rearrange("o (u j p) d -> o u p j d", p=P, u=U)
                        for u in range(U):
                            act.wait_ge(x_done, u + 1)
                            act.dma_start(x[:, TPB * u:TPB * (u + 1), :], xp[:, u].rearrange(
                                "o p j d -> p (o j) d")).then_inc(x_loaded, 16)
                        act.wait_ge(x_loaded, 16 * U)

                    @block.sync
                    def _(sp):
                        for buf, src in pair_loads(pair + 1):
                            sp.dma_start(buf[:], src).then_inc(loaded, 16)
                        dst = out[bass.ds(pair, 1)].rearrange("o (u j p) d -> o u p j d", p=P, u=U)
                        for u in range(U):
                            sp.wait_ge(x_done, u + 1)
                            sp.dma_start(dst[:, u].rearrange("o p j d -> p (o j) d"),
                                         y[:, TPB * u:TPB * (u + 1), :]).then_inc(stored, 16)
                        sp.wait_ge(stored, 16 * U)
                        sp.wait_ge(loaded, 16 * 4)


def constants():
    f = np.float32
    c = {"c_ident": np.eye(P, dtype=f)}
    p = np.arange(P)
    c["c_headmask_a"] = (p[:, None] // DA == np.arange(HA)).astype(f)
    c["c_headmask_c"] = (p[:, None] // DC == np.arange(HC)).astype(f)
    for name, heads, chunks in (("c_vmask_a", HA, CA), ("c_vmask_c", HC, CC)):
        m = np.zeros((P, chunks, WIN), f)
        for k in range(chunks):
            r = np.arange(chunk_rows(k, heads))
            m[r, k, (P * k + r) // SK - chunk_head(k, heads)] = 1
        c[name] = m
    half = np.arange(0, DH, 2, dtype=f)
    inv = (f(1.0) / np.power(f(10000.0), half / f(DH))).astype(f)
    t = np.arange(S, dtype=f)
    ang = (t[None, :] * inv[:, None]).astype(f)
    power = ((t - S // 2) / f(W // 2)).astype(f)
    basis = ((half + f(0.4 * DH)) / f(1.4 * DH)).astype(f)
    scale = np.power(basis[:, None], power[None, :]).astype(f)
    sign = np.where(np.arange(DH) < DH // 2, -1, 1).astype(f)
    rows = lambda m: np.concatenate([m, m]).T
    cos, sin, scale = rows(np.cos(ang)), rows(np.sin(ang)) * sign, rows(scale)
    tables = np.stack([cos * scale, sin * scale, cos / scale, sin / scale], 1).astype(f)
    c["c_rot"] = tables.reshape(TPB, P, 4, DH).transpose(1, 0, 2, 3)
    i = p[:, None] % W
    slot = p[None, :]
    even = p[:, None] < W
    key = np.where(even, np.where(slot < W, slot, slot - 2 * W), np.where(slot < W, slot - W, slot - W))
    ok = (key <= i) & (key >= i - W)
    first = ok & ~(even & (slot >= W))
    c["c_band"] = np.stack([np.where(ok, 0, NEG), np.where(first, 0, NEG)], 1).astype(f)
    sh = np.zeros((P, 2, P), f)
    sh[p[:-1], 0, p[1:]] = 1
    sh[P - 1, 1, 0] = 1
    c["c_shift"] = sh
    return {"c_rot": c["c_rot"], "c_consts": np.concatenate([c["c_" + k].reshape(P, w) for k, w in CONSTS.items()], 1)}


def layout(i):
    a = constants()
    n = B // U
    a["x"] = i["x"].reshape(n, U * S, D)
    a["tmat"] = i["fside_BxSxS2_0"].reshape(n, U * S, SK)
    a["ctxt"] = i["ctx_1024"].reshape(n, U, SK, D).transpose(0, 3, 1, 2)
    m = i["mask_BxS2_bf0"].reshape(n, U, SK)
    a["mrow"] = m.reshape(n, U, SK)
    flat = m[:, :, np.arange(CA * P) % SK].reshape(n, U, CA, P)
    a["mflat"] = flat.transpose(0, 3, 1, 2)
    a["w8"] = np.stack([i["L0_xattn_" + w] for w in ("Wq", "Wk", "Wv", "Wo")] +
                       [i["L1_xattn_" + w].T for w in ("Wq", "Wk", "Wv", "Wp")], 1)
    for k in ("x", "tmat", "ctxt", "mrow", "mflat"):
        a[k] = np.concatenate([a[k], a[k][:1]])
    a["wa1"], a["wa2"] = i["L0_xattn_W1"], i["L0_xattn_W2"]
    x0 = lambda k: i["L0_xattn_" + k]
    a["cols"] = np.concatenate([np.stack([x0("bq"), x0("bk"), x0("bv"), x0("ln1_g"), x0("ln1_b")], 1),
                                x0("b1").reshape(FF // P, P).T], 1)
    a["vecs"] = np.concatenate([x0("bo"), x0("ln1_g"), x0("ln1_b"), x0("b2"), x0("ln2_g"), x0("ln2_b"), i["L1_xattn_bp"],
                                i["g_xattn"], i["g_ffn"], i["L1_ffn_input_scale"], i["L1_ffn_kernel_scale"]])
    a["kern"] = i["L1_ffn_kernel"]
    a["fbias"] = i["L1_ffn_bias"]
    f = lambda k: i["L0_ffn_" + k]
    a["wqkv"], a["wo_b"], a["w1_b"], a["w2_b"], a["row_b"] = f("wqkv"), f("wo"), f("w1"), f("w2"), f("b2")
    ahead = lambda m: np.concatenate([m, m[:1]])
    a["wqkv"] = ahead(a["wqkv"])
    swap = (np.arange(DH) + DH // 2) % DH
    a["srow_b"] = ahead(np.stack([f("q_scale"), f("q_scale")[:, swap], f("k_scale"), f("k_scale")[:, swap]], 1))
    pad = np.zeros((DEPTH, 3 * P - HID), f("b1").dtype)
    b1 = [np.concatenate([f("b1")[:, k * HID:(k + 1) * HID], pad], 1).reshape(DEPTH, 3, P).transpose(0, 2, 1)
          for k in range(2)]
    a["cols_b"] = np.concatenate([np.stack([f("ln_g"), f("ln_b")], 2), *b1], 2)
    return {k: np.ascontiguousarray(v) for k, v in a.items()}


def kernel(**inputs):
    import concourse.bacc as bacc
    from concourse.bass_utils import run_bass_kernel_spmd

    nc = bacc.Bacc("TRN2", target_bir_lowering=False, num_devices=1)
    arrays = layout({k: np.asarray(v) for k, v in inputs.items()})
    aps = {k: nc.dram_tensor(f"in_{k}", v.shape, mybir.dt.from_np(v.dtype), kind="ExternalInput").ap()
           for k, v in arrays.items()}
    out = nc.dram_tensor("out_0", (B // U, U * S, D), F32, kind="ExternalOutput").ap()
    flamingo_kernel(nc, aps, out)
    r = run_bass_kernel_spmd(nc, [{f"in_{k}": v for k, v in arrays.items()}], core_ids=[0])
    return r.results[0]["out_0"].reshape(B, S, D)
```
